# Optimizing a Trainium2 kernel written in Bass

```python
import numpy as np
import jax
import jax.numpy as jnp

def _softmax(x, axis=-1):
    return jax.nn.softmax(x, axis=axis)

def _gelu(x):
    return jax.nn.gelu(x, approximate=True)

def _silu(x):
    return jax.nn.silu(x)

def _sigmoid(x):
    return jax.nn.sigmoid(x)

def _layernorm(x, axis=-1, eps=1e-05):
    m = jnp.mean(x, axis=axis, keepdims=True)
    v = jnp.var(x, axis=axis, keepdims=True)
    return (x - m) / jnp.sqrt(v + eps)

def _scatter_add(tgt, idx, src, axis=0):
    return tgt.at[idx].add(src)

def _segment_sum(src, seg, n):
    return jax.ops.segment_sum(src, seg, n)
kernel_name = 'mk_macaron_d1_jaxref_r4_876934'

def setup_inputs(seed: int=0):
    np.random.seed(seed)
    _w = jnp.asarray

    def _L0_attn_setup():
        import jax, jax.numpy as jnp
        import numpy as np
        _PAIRS = [(0, 1), (0, 2), (0, 3), (1, 2), (1, 3), (2, 3)]
        _J6 = jnp.array([[0, 0, 0, 0, 0, 1], [0, 0, 0, 0, -1, 0], [0, 0, 0, 1, 0, 0], [0, 0, 1, 0, 0, 0], [0, -1, 0, 0, 0, 0], [1, 0, 0, 0, 0, 0]], dtype=jnp.float32)

        def exterior(p1, p2):
            parts = [p1[..., i] * p2[..., j] - p1[..., j] * p2[..., i] for i, j in _PAIRS]
            L = jnp.stack(parts, axis=-1)
            n = jnp.maximum(jnp.linalg.norm(L, axis=-1, keepdims=True), 1e-12)
            return L / n
        key = jax.random.key(seed)
        B, T, D, H = (4, 512, 256, 16)
        ks = jax.random.split(key, 10)
        s = 0.02
        return {'x': jax.random.normal(ks[0], (B, T, D), dtype=jnp.float32), 'W1_q': jax.random.normal(ks[1], (2 * D, 4 * H), dtype=jnp.float32) * s, 'W2_q': jax.random.normal(ks[2], (2 * D, 4 * H), dtype=jnp.float32) * s, 'W1_k': jax.random.normal(ks[3], (D, 4 * H), dtype=jnp.float32) * s, 'W2_k': jax.random.normal(ks[4], (D, 4 * H), dtype=jnp.float32) * s, 'W_v': jax.random.normal(ks[5], (D, D), dtype=jnp.float32) * s, 'b_v': jnp.zeros((D,), dtype=jnp.float32), 'W_o': jax.random.normal(ks[6], (D, D), dtype=jnp.float32) * s, 'b_o': jnp.zeros((D,), dtype=jnp.float32)}
    _L0_attn_in = _L0_attn_setup()

    def _L0_ffn_setup():
        import jax, jax.numpy as jnp
        import numpy as np
        DIM = 256
        E = 16
        TOPK = 2
        G = 4
        TOPK_G = 2
        INTER = 128
        N_SHARED = 2
        ROUTE_SCALE = 1.0

        def _gate(xf, gate_w, gate_b):
            scores = xf @ gate_w.T
            scores = jax.nn.softmax(scores.astype(jnp.float32), axis=-1)
            orig = scores
            scores = scores + gate_b
            T = xf.shape[0]
            sg = scores.reshape(T, G, E // G)
            group_scores = jax.lax.top_k(sg, 2)[0].sum(-1)
            _, gidx = jax.lax.top_k(group_scores, TOPK_G)
            keep = jax.nn.one_hot(gidx, G).sum(axis=1) > 0
            sg = jnp.where(keep[:, :, None], sg, -jnp.inf)
            scores = sg.reshape(T, E)
            _, idx = jax.lax.top_k(scores, TOPK)
            weights = jnp.take_along_axis(orig, idx, axis=1)
            weights = (weights * ROUTE_SCALE).astype(xf.dtype)
            return (weights, idx)
        key = jax.random.key(seed)
        ks = jax.random.split(key, 16)
        s = lambda fan_in: 1.0 / np.sqrt(fan_in)
        inp = {'x': jax.random.normal(ks[0], (4, 256, DIM), dtype=jnp.float32), 'gate_w': jax.random.normal(ks[1], (E, DIM), dtype=jnp.float32) * s(DIM), 'gate_b': jnp.zeros((E,), dtype=jnp.float32), 'We1': jax.random.normal(ks[2], (E, DIM, INTER), dtype=jnp.float32) * s(DIM), 'be1': jnp.zeros((E, INTER), dtype=jnp.float32), 'We2': jax.random.normal(ks[3], (E, INTER, DIM), dtype=jnp.float32) * s(INTER), 'be2': jnp.zeros((E, DIM), dtype=jnp.float32), 'We3': jax.random.normal(ks[4], (E, DIM, INTER), dtype=jnp.float32) * s(DIM), 'be3': jnp.zeros((E, INTER), dtype=jnp.float32), 'ws1': jax.random.normal(ks[5], (DIM, N_SHARED * INTER), dtype=jnp.float32) * s(DIM), 'bs1': jnp.zeros((N_SHARED * INTER,), dtype=jnp.float32), 'ws2': jax.random.normal(ks[6], (N_SHARED * INTER, DIM), dtype=jnp.float32) * s(N_SHARED * INTER), 'bs2': jnp.zeros((DIM,), dtype=jnp.float32), 'ws3': jax.random.normal(ks[7], (DIM, N_SHARED * INTER), dtype=jnp.float32) * s(DIM), 'bs3': jnp.zeros((N_SHARED * INTER,), dtype=jnp.float32)}
        return inp
    _L0_ffn_in = _L0_ffn_setup()
    _d = {'L0_attn_x': _L0_attn_in['x'], 'L0_attn_W1_q': _L0_attn_in['W1_q'], 'L0_attn_W2_q': _L0_attn_in['W2_q'], 'L0_attn_W1_k': _L0_attn_in['W1_k'], 'L0_attn_W2_k': _L0_attn_in['W2_k'], 'L0_attn_W_v': _L0_attn_in['W_v'], 'L0_attn_b_v': _L0_attn_in['b_v'], 'L0_attn_W_o': _L0_attn_in['W_o'], 'L0_attn_b_o': _L0_attn_in['b_o'], 'L0_ffn_gate_w': _L0_ffn_in['gate_w'], 'L0_ffn_gate_b': _L0_ffn_in['gate_b'], 'L0_ffn_We1': _L0_ffn_in['We1'], 'L0_ffn_be1': _L0_ffn_in['be1'], 'L0_ffn_We2': _L0_ffn_in['We2'], 'L0_ffn_be2': _L0_ffn_in['be2'], 'L0_ffn_We3': _L0_ffn_in['We3'], 'L0_ffn_be3': _L0_ffn_in['be3'], 'L0_ffn_ws1': _L0_ffn_in['ws1'], 'L0_ffn_bs1': _L0_ffn_in['bs1'], 'L0_ffn_ws2': _L0_ffn_in['ws2'], 'L0_ffn_bs2': _L0_ffn_in['bs2'], 'L0_ffn_ws3': _L0_ffn_in['ws3'], 'L0_ffn_bs3': _L0_ffn_in['bs3']}
    _x0 = _d['L0_attn_x']
    _d['L0_attn_x'] = jax.random.normal(jax.random.fold_in(jax.random.key(seed), 1), (2, 2048, 256), dtype=_x0.dtype)
    del _x0
    return _d

def reference(L0_attn_x, L0_attn_W1_q, L0_attn_W2_q, L0_attn_W1_k, L0_attn_W2_k, L0_attn_W_v, L0_attn_b_v, L0_attn_W_o, L0_attn_b_o, L0_ffn_gate_w, L0_ffn_gate_b, L0_ffn_We1, L0_ffn_be1, L0_ffn_We2, L0_ffn_be2, L0_ffn_We3, L0_ffn_be3, L0_ffn_ws1, L0_ffn_bs1, L0_ffn_ws2, L0_ffn_bs2, L0_ffn_ws3, L0_ffn_bs3):

    def _L0_attn_ref(x, W1_q, W2_q, W1_k, W2_k, W_v, b_v, W_o, b_o):
        import jax, jax.numpy as jnp
        import numpy as np
        _PAIRS = [(0, 1), (0, 2), (0, 3), (1, 2), (1, 3), (2, 3)]
        _J6 = jnp.array([[0, 0, 0, 0, 0, 1], [0, 0, 0, 0, -1, 0], [0, 0, 0, 1, 0, 0], [0, 0, 1, 0, 0, 0], [0, -1, 0, 0, 0, 0], [1, 0, 0, 0, 0, 0]], dtype=jnp.float32)

        def exterior(p1, p2):
            parts = [p1[..., i] * p2[..., j] - p1[..., j] * p2[..., i] for i, j in _PAIRS]
            L = jnp.stack(parts, axis=-1)
            n = jnp.maximum(jnp.linalg.norm(L, axis=-1, keepdims=True), 1e-12)
            return L / n
        B, T, D = x.shape
        H = W1_k.shape[1] // 4
        d_head = D // H
        scale = 6.0 ** (-0.5)
        x_prev = jnp.concatenate([jnp.zeros((B, 1, D), dtype=x.dtype), x[:, :-1]], axis=1)
        x_bigram = jnp.concatenate([x, x_prev], axis=-1)
        q1 = (x_bigram @ W1_q).reshape(B, T, H, 4)
        q2 = (x_bigram @ W2_q).reshape(B, T, H, 4)
        L_q = exterior(q1, q2)
        k1 = (x @ W1_k).reshape(B, T, H, 4)
        k2 = (x @ W2_k).reshape(B, T, H, 4)
        L_k = exterior(k1, k2)
        JL_k = L_k @ _J6.T
        attn = jnp.einsum('bqhc,bkhc->bhqk', L_q, JL_k) * scale
        causal = jnp.tril(jnp.ones((T, T), dtype=bool))
        attn = jnp.where(causal, attn, -jnp.inf)
        attn = jax.nn.softmax(attn, axis=-1)
        v = (x @ W_v + b_v).reshape(B, T, H, d_head)
        out = jnp.einsum('bhqk,bkhd->bqhd', attn, v).reshape(B, T, D)
        return out @ W_o + b_o

    def _L0_ffn_ref(x, gate_w, gate_b, We1, be1, We2, be2, We3, be3, ws1, bs1, ws2, bs2, ws3, bs3):
        import jax, jax.numpy as jnp
        import numpy as np
        DIM = 256
        E = 16
        TOPK = 2
        G = 4
        TOPK_G = 2
        INTER = 128
        N_SHARED = 2
        ROUTE_SCALE = 1.0

        def _gate(xf, gate_w, gate_b):
            scores = xf @ gate_w.T
            scores = jax.nn.softmax(scores.astype(jnp.float32), axis=-1)
            orig = scores
            scores = scores + gate_b
            T = xf.shape[0]
            sg = scores.reshape(T, G, E // G)
            group_scores = jax.lax.top_k(sg, 2)[0].sum(-1)
            _, gidx = jax.lax.top_k(group_scores, TOPK_G)
            keep = jax.nn.one_hot(gidx, G).sum(axis=1) > 0
            sg = jnp.where(keep[:, :, None], sg, -jnp.inf)
            scores = sg.reshape(T, E)
            _, idx = jax.lax.top_k(scores, TOPK)
            weights = jnp.take_along_axis(orig, idx, axis=1)
            weights = (weights * ROUTE_SCALE).astype(xf.dtype)
            return (weights, idx)
        shape = x.shape
        xf = x.reshape(-1, DIM)
        weights, idx = _gate(xf, gate_w, gate_b)
        combine = (jax.nn.one_hot(idx, E, dtype=xf.dtype) * weights[..., None]).sum(1)
        h1 = jnp.einsum('td,edi->tei', xf, We1) + be1
        h3 = jnp.einsum('td,edi->tei', xf, We3) + be3
        h = jax.nn.silu(h1) * h3
        yo = jnp.einsum('tei,eid->ted', h, We2) + be2
        y = jnp.einsum('te,ted->td', combine, yo)
        z = jax.nn.silu(xf @ ws1 + bs1) * (xf @ ws3 + bs3) @ ws2 + bs2
        return (y + z).reshape(shape)
    x = L0_attn_x
    x = x + 0.5 * _L0_ffn_ref(_layernorm(x, axis=-1), L0_ffn_gate_w, L0_ffn_gate_b, L0_ffn_We1, L0_ffn_be1, L0_ffn_We2, L0_ffn_be2, L0_ffn_We3, L0_ffn_be3, L0_ffn_ws1, L0_ffn_bs1, L0_ffn_ws2, L0_ffn_bs2, L0_ffn_ws3, L0_ffn_bs3)
    x = x + _L0_attn_ref(_layernorm(x, axis=-1), L0_attn_W1_q, L0_attn_W2_q, L0_attn_W1_k, L0_attn_W2_k, L0_attn_W_v, L0_attn_b_v, L0_attn_W_o, L0_attn_b_o)
    x = x + 0.5 * _L0_ffn_ref(_layernorm(x, axis=-1), L0_ffn_gate_w, L0_ffn_gate_b, L0_ffn_We1, L0_ffn_be1, L0_ffn_We2, L0_ffn_be2, L0_ffn_We3, L0_ffn_be3, L0_ffn_ws1, L0_ffn_bs1, L0_ffn_ws2, L0_ffn_bs2, L0_ffn_ws3, L0_ffn_bs3)
    return x

_drawn_inputs = setup_inputs


def setup_inputs(seed=0):
    import zlib

    import numpy as np

    out = dict(_drawn_inputs(seed))
    spreads = {'L0_attn_b_v': (0.0, 0.1),
     'L0_attn_b_o': (0.0, 0.1),
     'L0_ffn_gate_b': (0.0, 0.1),
     'L0_ffn_be1': (0.0, 0.542),
     'L0_ffn_be2': (0.0, 0.337),
     'L0_ffn_be3': (0.0, 0.556),
     'L0_ffn_bs1': (0.0, 0.1),
     'L0_ffn_bs2': (0.0, 0.1),
     'L0_ffn_bs3': (0.0, 0.1)}
    factors = {'L0_attn_W1_q': 8.0,
     'L0_attn_W2_q': 8.0,
     'L0_attn_W1_k': 8.0,
     'L0_attn_W2_k': 8.0,
     'L0_attn_W_v': 6.517}
    for name, (base, spread) in spreads.items():
        noise = np.random.default_rng([zlib.crc32(name.encode()), seed]).standard_normal(out[name].shape)
        drawn = base * np.exp(spread * noise) if base else spread * noise
        out[name] = jnp.asarray(drawn.astype(out[name].dtype))
    for name, factor in factors.items():
        out[name] = (out[name] * factor).astype(out[name].dtype)
    return out
```

```python
from collections import namedtuple
from contextlib import ExitStack

import concourse.bass as bass
from concourse import mybir

FP32 = mybir.dt.float32
FP16 = mybir.dt.float16
BF16 = mybir.dt.bfloat16
I32 = mybir.dt.int32
ALU = mybir.AluOpType
ACT = mybir.ActivationFunctionType
AX = mybir.AxisListType.X

P = 128
BATCH, T, D = 2, 2048, 256
DC = D // P
TILES = BATCH * T // P
BT = 4
BLOCKS = TILES // BT
BW = BT * P
EPS = 1e-5

E, G, TOPK, INTER = 16, 4, 2, 128
SHARED = 2 * INTER
ROUND = 4
SLOT_TILES = -(-((TOPK * TILES * P + E * (P - 1)) // P) // ROUND) * ROUND
LOWEST = -3.0e38

H, PL = 16, 6
DH = D // H
HG = 4
GROUPS = H // HG
HR = P // HG
QW = 512
QC = T // QW
KT = T // P
SCALE = 6.0 ** -0.5


def dma_rows(ap):
    return ap.rearrange("(n p) d -> p n d", p=P)


def over_partitions(ap, n, *shape):
    flat = ap.rearrange("(o n) -> o n", o=1) if len(ap.shape) == 1 else ap.rearrange("(o e) i -> o e i", o=1)
    return flat.to_broadcast([n, *shape])


class Core:
    pass


def setup(nc, core, x_dram, ctx):
    sb = lambda name, shape, dt=FP32: ctx.enter_context(nc.sbuf_tensor(name, shape, dt))
    core.x = sb("x_res", [P, TILES, D])
    core.ident = sb("ident", [P, P])
    core.ident16 = sb("ident16", [P, P], FP16)
    core.before = sb("before", [P, P], BF16)
    core.ones = sb("ones", [P, P], BF16)
    core.falling = sb("falling", [P, E])
    core.lower4 = sb("lower4", [P, G, G])
    core.full_tiles = sb("full_tiles", [P, TILES])
    core.tile_id = sb("tile_id", [1, SLOT_TILES])
    core.banks = ctx.enter_context(nc.psum_tensor("banks", [P, 8, 512], FP32))
    core.bank = [core.banks[:, i, :] for i in range(8)]
    with ExitStack() as own, nc.Block() as block:
        x_loaded = own.enter_context(nc.semaphore("x_loaded"))
        filled = own.enter_context(nc.semaphore("filled"))

        @block.sync
        def _(sp):
            rows = dma_rows(x_dram.rearrange("b t d -> (b t) d"))
            for b in range(BLOCKS):
                sp.dma_start(core.x[:, b * BT:(b + 1) * BT, :], rows[:, b * BT:(b + 1) * BT, :]).then_inc(x_loaded, 16)
            sp.wait_ge(x_loaded, 16 * BLOCKS)

        @block.gpsimd
        def _(pool):
            pool.memset(core.ident[:], 0.0)
            pool.memset(core.ident16[:], 0.0)
            pool.memset(core.before[:], 1.0)
            pool.memset(core.ones[:], 1.0)
            pool.memset(core.lower4[:], 1.0).then_inc(filled, 1)
            pool.iota(core.falling[:], [[-1, E]], base=E, channel_multiplier=0, allow_small_or_imprecise_dtypes=True)
            pool.iota(core.full_tiles[:], [[P, TILES]], base=0, channel_multiplier=0, allow_small_or_imprecise_dtypes=True)
            pool.iota(core.tile_id[:], [[1, SLOT_TILES]], base=0, channel_multiplier=0, allow_small_or_imprecise_dtypes=True)
            pool.wait_ge(filled, 1)
            for eye in (core.ident, core.ident16):
                pool.affine_select(out=eye[:], in_=eye[:], compare_op=ALU.not_equal, fill=1.0, base=0,
                                   pattern=[[-1, P]], channel_multiplier=1)
            pool.affine_select(out=core.before[:], in_=core.before[:], compare_op=ALU.is_gt, fill=0.0, base=0,
                               pattern=[[1, P]], channel_multiplier=-1)
            pool.affine_select(out=core.lower4[:], in_=core.lower4[:], compare_op=ALU.is_gt, fill=0.0, base=0,
                               pattern=[[1, G], [-1, G]], channel_multiplier=0)


def norm_statistics(nc, dve, act, core, s, sem):
    if dve is not None:
        n = [0]

        def step(ins):
            n[0] += 1
            ins.then_inc(sem.stat_step, 1)
            dve.wait_ge(sem.stat_step, n[0])

        with dve.Fori(0, BLOCKS) as i:
            for j in range(BT):
                dve.bn_stats(s.parts[:, bass.ds(i * BT + j, 1), :], core.x[:, bass.ds(i * BT + j, 1), :]
                             .rearrange("p o d -> p (o d)")).then_inc(sem.stats, 1)
        dve.wait_ge(sem.stats, TILES)
        mean_even, m2_even = s.parts[:, :, 1], s.parts[:, :, 2]
        mean_odd, m2_odd = s.parts[:, :, 4], s.parts[:, :, 5]
        step(dve.tensor_tensor(s.mean[:], mean_even, mean_odd, ALU.add))
        step(dve.tensor_scalar(s.mean[:], s.mean[:], 0.5, None, ALU.mult))
        step(dve.tensor_tensor(s.gap[:], mean_even, mean_odd, ALU.subtract))
        step(dve.tensor_tensor(s.gap[:], s.gap[:], s.gap[:], ALU.mult))
        step(dve.tensor_tensor(s.var[:], m2_even, m2_odd, ALU.add))
        step(dve.tensor_scalar(s.var[:], s.var[:], 1.0 / D, EPS, ALU.mult, ALU.add))
        dve.scalar_tensor_tensor(s.var[:], s.gap[:], 0.25, s.var[:], ALU.mult, ALU.add).then_inc(sem.var_ready, 1)
        dve.wait_ge(sem.root_ready, 1)
        step(dve.reciprocal(s.rstd[:], s.root[:]))
    if act is not None:
        act.wait_ge(sem.var_ready, 1)
        act.activation(s.root[:], s.var[:], ACT.Sqrt).then_inc(sem.root_ready, 1)


def semaphores(nc, tag, names):
    names = names.split()
    return namedtuple("Semaphores", names)(*[nc.alloc_semaphore(name=f"{tag}_{name}") for name in names])


def ring_semaphores(nc, name, n):
    return [nc.alloc_semaphore(name=f"{name}{k}") for k in range(n)]


def give_back(nc, *kinds):
    nc.clear_and_free_semaphores([one for kind in kinds for one in kind])
    nc.all_engine_barrier()


def ffn(nc, core, w, x_slots, y_slots, tag, out=None):
    ctx = ExitStack()
    with ctx:
        sb = lambda name, shape, dt=FP32: ctx.enter_context(nc.sbuf_tensor(f"{tag}_{name}", shape, dt))
        x, bank = core.x, core.bank
        s = Core()
        s.parts, s.mean, s.gap = sb("parts", [P, TILES, 6]), sb("mean", [P, TILES]), sb("gap", [P, TILES])
        s.var, s.root, s.rstd = sb("var", [P, TILES]), sb("root", [P, TILES]), sb("rstd", [P, TILES])
        xn = sb("xn", [P, TILES, D])
        stage = sb("stage", [P, BT, D])
        w13 = sb("w13", [P, E, DC, 2 * INTER])
        w2 = sb("w2", [P, E, D])
        ws13 = sb("ws13", [P, DC, 2 * SHARED])
        ws2 = sb("ws2", [P, SHARED // P, D])
        bs = sb("bs", [P, 2 * SHARED // P])
        bs2 = sb("bs2", [P, D])
        gate_t = sb("gate_t", [P, DC, E])
        gate_b = sb("gate_b", [P, E])
        region = sb("region", [P, E, 2 * INTER + D])
        table = [region[:, e, :] for e in range(E)]
        zero_rows, gate_rows, bs_rows = table[14][:, 0:D], table[15][0:E, 0:D], table[15][0:2 * SHARED // P, D:D + P]
        xnt = sb("xnt", [P, DC, TILES * P])
        rings = xnt[:, :, :].rearrange("p c n -> p (c n)")
        taken = [0]

        def ring(n, width):
            at = taken[0]
            taken[0] += n * width
            return rings[:, at:at + n * width].rearrange("p (n w) -> p n w", n=n)

        rows_in, rows_t = ring(ROUND, D), ring(2, D)
        hidden, gated, prod, prod_t = ring(2, 2 * INTER), ring(2, INTER), ring(2, INTER), ring(2, INTER)
        y_rows, back = ring(ROUND, D), ring(16, D)
        s_silu, s_lin = sb("s_silu", [P, 2, BW]), sb("s_lin", [P, 2, BW])
        s_prod = stage[:].rearrange("p t d -> p (t d)").rearrange("p (c n) -> p c n", c=2)
        logits_t = s_silu[0:E, 0, :]
        z_half = sb("z_half", [P, 2, 2 * D])
        slots = sb("slots", [P, TILES, TOPK], I32)
        slots_f = sb("slots_f", [P, TILES, TOPK])
        weight = sb("weight", [P, TOPK, TILES])
        small = sb("small", [P, 8, E])
        col = sb("col", [P, 4, TILES])
        expert_of = sb("expert_of", [1, SLOT_TILES], I32)
        expert_f = sb("expert_f", [1, SLOT_TILES])
        assigned = sb("assigned", [P, TILES * E], BF16)
        expert_hit = region[0:1, 6:9, :].rearrange("p a b -> p (a b)")[:, 0:SLOT_TILES * E].rearrange("p (n e) -> p n e", e=E)

        sem = semaphores(nc, tag, "zeroed half_ready gate_loaded shared_loaded experts_loaded biases_loaded cleared "
                    "stat_step stats var_ready root_ready gate_turned gate_ready bias_turned bias_ready staged normed turned "
                    "xnt0_ready xnt1_ready logits_ready logits_kept logits_turned logits_stored "
                    "route_step shifted exp_ready pairs_ready counted slots_ready "
                    "up_ready silu_ready lin_ready prod_ready down_ready z_ready z_added bs2_added "
                    "sent rows_turned rows_kept up_done hidden_ready gated_ready prod_done prod_turned prod_kept "
                    "y_done y_ready combined out_stored")
        row_loaded = ring_semaphores(nc, f"{tag}_row_loaded", ROUND)
        row_stored = ring_semaphores(nc, f"{tag}_row_stored", ROUND)
        fetched = ring_semaphores(nc, f"{tag}_fetched", 8)

        def tile(buf, t):
            return buf[:, bass.ds(t, 1), :].rearrange("p o d -> p (o d)")

        block = ctx.enter_context(nc.Block())

        def expert_steps(eng, emit, lag):
            for n in range(ROUND):
                emit(n, n, n // ROUND)
            with eng.Fori(1, SLOT_TILES // ROUND) as i:
                for j in range(ROUND):
                    emit(i * ROUND + j, j, i)
            for n in range(SLOT_TILES, SLOT_TILES + lag):
                emit(n, n, n // ROUND)

        def runs(n, lag):
            return not isinstance(n, int) or 0 <= n - lag < SLOT_TILES

        @block.sync
        def _(sp):
            sp.dma_start(gate_rows, w["gate_w"]).then_inc(sem.gate_loaded, 16)
            sp.dma_start(bs_rows[0:2, :], w["bs1"].rearrange("(c p) -> c p", p=P)).then_inc(sem.gate_loaded, 16)
            sp.dma_start(bs_rows[2:4, :], w["bs3"].rearrange("(c p) -> c p", p=P)).then_inc(sem.gate_loaded, 16)
            sp.dma_start(gate_b[:], over_partitions(w["gate_b"], P, E)).then_inc(sem.gate_loaded, 16)
            sp.dma_start(bs2[:], over_partitions(w["bs2"], P, D)).then_inc(sem.gate_loaded, 16)
            sp.dma_start(ws13[:, :, 0:SHARED], w["ws1"].rearrange("(c p) f -> p c f", p=P)).then_inc(sem.shared_loaded, 16)
            sp.dma_start(ws13[:, :, SHARED:], w["ws3"].rearrange("(c p) f -> p c f", p=P)).then_inc(sem.shared_loaded, 16)
            sp.dma_start(ws2[:], w["ws2"].rearrange("(c p) d -> p c d", p=P)).then_inc(sem.shared_loaded, 16)
            if x_slots is not None and core.clear_slots:
                sp.wait_ge(sem.zeroed, 1)
                sp.dma_start(dma_rows(x_slots), zero_rows.rearrange("p (o d) -> p o d", o=1)
                             .to_broadcast([P, SLOT_TILES, D])).then_inc(sem.cleared, 16)
            for c in range(DC):
                sp.dma_start(w13[:, :, c, 0:INTER], w["We1"][:, c * P:(c + 1) * P, :].rearrange("e p i -> p e i")
                             ).then_inc(sem.experts_loaded, 16)
                sp.dma_start(w13[:, :, c, INTER:], w["We3"][:, c * P:(c + 1) * P, :].rearrange("e p i -> p e i")
                             ).then_inc(sem.experts_loaded, 16)
            sp.dma_start(w2[:], w["We2"].rearrange("e i d -> i e d")).then_inc(sem.experts_loaded, 16)
            sp.wait_ge(sem.slots_ready, 1)
            if core.clear_slots:
                sp.wait_ge(sem.cleared, 16)
            sp.dma_start(region[:, :, 0:INTER], over_partitions(w["be1"], P, E, INTER)).then_inc(sem.biases_loaded, 16)
            sp.dma_start(region[:, :, INTER:2 * INTER], over_partitions(w["be3"], P, E, INTER)).then_inc(sem.biases_loaded, 16)
            sp.dma_start(region[:, :, 2 * INTER:], over_partitions(w["be2"], P, E, D)).then_inc(sem.biases_loaded, 16)
            sp.wait_ge(sem.sent, 16 * TOPK * TILES)
            sp.wait_ge(sem.up_ready, 4 * BLOCKS)

            def load(n, j):
                if not isinstance(n, int) or n >= ROUND:
                    sp.wait_ge(sem.rows_turned, n - ROUND + 1)
                sp.dma_start(rows_in[:, j % ROUND, :], x_slots[bass.ds(n * P, P), :]).then_inc(row_loaded[j % ROUND], 16)

            def emit(n, j):
                if runs(n, -2):
                    load(n + 2, j + 2)
                if runs(n, ROUND):
                    sp.wait_ge(sem.y_ready, n - ROUND + 1)
                    sp.dma_start(y_slots[bass.ds((n - ROUND) * P, P), :], y_rows[:, j % ROUND, :]).then_inc(row_stored[j % ROUND], 16)

            load(0, 0)
            load(1, 1)
            for n in range(ROUND):
                emit(n, n)
            with sp.Fori(1, SLOT_TILES // ROUND - 1) as i:
                for j in range(ROUND):
                    emit(i * ROUND + j, j)
            for n in range(SLOT_TILES - ROUND, SLOT_TILES + ROUND):
                emit(n, n)
            for stored in row_stored:
                sp.wait_ge(stored, 16 * (SLOT_TILES // ROUND))
            if out is not None:
                rows = dma_rows(out.rearrange("b t d -> (b t) d"))
                for g in range(TILES // 8):
                    sp.wait_ge(sem.combined, 8 * (g + 1))
                    sp.dma_start(rows[:, g * 8:(g + 1) * 8, :], x[:, g * 8:(g + 1) * 8, :]).then_inc(sem.out_stored, 16)
                sp.wait_ge(sem.out_stored, 16 * (TILES // 8))

        def shared_up_wait(eng, i):
            eng.wait_ge(sem.xnt0_ready, i + 1)
            eng.wait_ge(sem.xnt1_ready, i + 1)

        FIRST_SHARED = 4

        @block.tensor
        def _(pe):
            pe.wait_ge(sem.gate_loaded, 80)
            for c in range(DC):
                pe.transpose(bank[2][:, c * E:(c + 1) * E], gate_rows[:, c * P:(c + 1) * P], core.ident[0:E, 0:E])
            pe.transpose(bank[2][:, 2 * E:2 * E + 4], bs_rows, core.ident[0:4, 0:4]).then_inc(sem.gate_turned, 1)
            pe.wait_ge(sem.gate_ready, 1)

            def gate_block(i):
                pe.wait_ge(sem.staged, i + 1)
                for c in range(DC):
                    for j in range(BT):
                        last = pe.transpose(bank[c][:, j * P:(j + 1) * P], stage[:, j, c * P:(c + 1) * P], core.ident[:])
                last.then_inc(sem.turned, 1)
                shared_up_wait(pe, i)
                for c in range(DC):
                    last = pe.matmul(bank[2][0:E, :], gate_t[:, c, :], xnt[:, c, bass.ds(i * BW, BW)],
                                     start=(c == 0), stop=(c == DC - 1))
                last.then_inc(sem.logits_ready, 1)
                pe.wait_ge(sem.logits_kept, i + 1)
                if not isinstance(i, int) or i > 0:
                    pe.wait_ge(sem.logits_stored, i)
                for j in range(BT):
                    last = pe.matmul(bank[3][:, j * E:(j + 1) * E], logits_t[:, j * P:(j + 1) * P], core.ident[0:E, 0:E], start=True, stop=True)
                last.then_inc(sem.logits_turned, 1)

            gate_block(0)
            with pe.Fori(1, BLOCKS) as i:
                gate_block(i)

            def shared_down(i):
                pe.wait_ge(sem.prod_ready, i + 1)
                for j in range(BT):
                    if j % 2 == 0 and (not isinstance(i, int) or i > 0):
                        pe.wait_ge(sem.z_ready, 2 * (i - 1) + j // 2 + 1)
                    for c in range(SHARED // P):
                        last = pe.matmul(bank[4 + j // 2][:, j % 2 * D:(j % 2 + 1) * D], s_prod[:, c, j * P:(j + 1) * P],
                                         ws2[:, c, :], start=(c == 0), stop=(c == SHARED // P - 1))
                    if j % 2:
                        last.then_inc(sem.down_ready, 1)

            def shared_up(i):
                for f in range(4):
                    if not isinstance(i, int) or i > 0:
                        if f < 2:
                            pe.wait_ge(sem.silu_ready, 2 * (i - 1) + f + 1)
                        else:
                            pe.wait_ge(sem.lin_ready, 2 * (i - 1) + f - 1)
                    for c in range(DC):
                        last = pe.matmul(bank[f][:, :], ws13[:, c, f * P:(f + 1) * P], xnt[:, c, bass.ds(i * BW, BW)],
                                         start=(c == 0), stop=(c == DC - 1))
                    last.then_inc(sem.up_ready, 1)

            pe.wait_ge(sem.shared_loaded, 48)
            pe.wait_ge(sem.logits_stored, BLOCKS)
            shared_up(0)
            shared_up(1)
            shared_down(0)
            with pe.Fori(1, FIRST_SHARED // 2) as k:
                for q in range(2):
                    shared_up(k * 2 + q)
                    shared_down(k * 2 + q - 1)
            pe.wait_ge(sem.pairs_ready, 1)
            pe.matmul(bank[6][:, :], core.before[:], assigned[:], start=True, stop=True)
            pe.matmul(bank[7][:, :], core.ones[:], assigned[:], start=True, stop=True).then_inc(sem.counted, 1)
            with pe.Fori(FIRST_SHARED // 2, BLOCKS // 2) as k:
                for q in range(2):
                    shared_up(k * 2 + q)
                    shared_down(k * 2 + q - 1)
            shared_down(BLOCKS - 1)

            pe.wait_ge(sem.experts_loaded, 80)
            pe.wait_ge(sem.lin_ready, 2 * BLOCKS)
            pe.wait_ge(sem.z_ready, 2 * BLOCKS)

            def emit(n, j, r):
                if runs(n, 0):
                    pe.wait_ge(row_loaded[j % ROUND], 16 * r + 16)
                    if not isinstance(n, int) or n >= 2:
                        pe.wait_ge(sem.rows_kept, n - 1)
                    for c in range(DC):
                        last = pe.transpose(bank[j % 2][:, c * P:(c + 1) * P], rows_in[:, j % ROUND, c * P:(c + 1) * P], core.ident[:])
                    last.then_inc(sem.rows_turned, 1)
                if runs(n, 1):
                    m = (j - 1) % 2
                    expert = pe.value_load(expert_of[0:1, bass.ds(n - 1, 1)], min_val=0, max_val=E - 1)
                    pe.wait_ge(sem.rows_kept, n)
                    if not isinstance(n, int) or n >= 3:
                        pe.wait_ge(sem.hidden_ready, n - 2)
                    for c in range(DC):
                        last = pe.matmul(bank[2 + m][:, 0:2 * INTER], rows_t[:, m, c * P:(c + 1) * P],
                                         w13[:, bass.ds(expert, 1), c, :].rearrange("p o f -> p (o f)"),
                                         start=(c == 0), stop=(c == DC - 1))
                    last.then_inc(sem.up_done, 1)
                if runs(n, 2):
                    m = (j - 2) % 2
                    pe.wait_ge(sem.prod_done, n - 1)
                    if not isinstance(n, int) or n >= 4:
                        pe.wait_ge(sem.prod_kept, n - 3)
                    pe.transpose(bank[4 + m][:, 0:INTER], prod[:, m, :], core.ident[:]).then_inc(sem.prod_turned, 1)
                if runs(n, 3):
                    m = (j - 3) % 2
                    expert = pe.value_load(expert_of[0:1, bass.ds(n - 3, 1)], min_val=0, max_val=E - 1)
                    pe.wait_ge(sem.prod_kept, n - 2)
                    if not isinstance(n, int) or n >= 5:
                        pe.wait_ge(sem.y_ready, n - 4)
                    pe.matmul(bank[6 + m][:, 0:D], prod_t[:, m, :],
                              w2[:, bass.ds(expert, 1), :].rearrange("p o d -> p (o d)"),
                              start=True, stop=True).then_inc(sem.y_done, 1)

            pe.wait_ge(sem.slots_ready, 1)
            expert_steps(pe, emit, 3)

        @block.scalar
        def _(act):
            norm_statistics(nc, None, act, core, s, sem)
            act.wait_ge(sem.gate_turned, 1)
            act.activation(gate_t[:].rearrange("p c e -> p (c e)"), bank[2][:, 0:DC * E], ACT.Copy)
            act.activation(bs[:], bank[2][:, 2 * E:2 * E + 4], ACT.Copy).then_inc(sem.gate_ready, 1)

            def gate_block(i):
                act.wait_ge(sem.turned, i + 1)
                act.activation(xnt[:, 0, bass.ds(i * BW, BW)], bank[0][:, :], ACT.Copy).then_inc(sem.xnt0_ready, 1)
                act.wait_ge(sem.logits_ready, i + 1)
                if not isinstance(i, int) or i > 0:
                    act.wait_ge(sem.logits_turned, i)
                act.activation(logits_t, bank[2][0:E, :], ACT.Copy).then_inc(sem.logits_kept, 1)

            gate_block(0)
            with act.Fori(1, BLOCKS) as i:
                gate_block(i)
            act.wait_ge(sem.shifted, 1)
            act.activation(table[1], table[1], ACT.Exp).then_inc(sem.exp_ready, 1)

            def shared_block(i):
                for f in range(2):
                    act.wait_ge(sem.up_ready, 4 * i + f + 1)
                    if f == 0 and (not isinstance(i, int) or i > 0):
                        act.wait_ge(sem.prod_ready, i)
                    act.activation(s_silu[:, f, :], bank[f][:, :], ACT.Silu, bias=bs[:, f:f + 1]).then_inc(sem.silu_ready, 1)
                for f in range(2):
                    act.wait_ge(sem.up_ready, 4 * i + f + 3)
                    act.activation(s_lin[:, f, :], bank[2 + f][:, :], ACT.Identity, bias=bs[:, 2 + f:3 + f]).then_inc(sem.lin_ready, 1)

            def shared_out(i):
                for j in range(2):
                    act.wait_ge(sem.down_ready, 2 * i + j + 1)
                    if not isinstance(i, int) or i > 0:
                        act.wait_ge(sem.z_added, 2 * (i - 1) + j + 1)
                    act.activation(z_half[:, j, :], bank[4 + j][:, :], ACT.Copy, scale=0.5).then_inc(sem.z_ready, 1)

            shared_block(0)
            shared_block(1)
            shared_out(0)
            with act.Fori(2, BLOCKS) as i:
                shared_block(i)
                shared_out(i - 1)
            shared_out(BLOCKS - 1)

            def emit(n, j, r):
                if runs(n, 0):
                    act.wait_ge(sem.rows_turned, n + 1)
                    if not isinstance(n, int) or n >= 2:
                        act.wait_ge(sem.up_done, n - 1)
                    act.activation(rows_t[:, j % 2, :], bank[j % 2][:, 0:D], ACT.Copy).then_inc(sem.rows_kept, 1)
                if runs(n, 1):
                    m = (j - 1) % 2
                    act.wait_ge(sem.hidden_ready, n)
                    if not isinstance(n, int) or n >= 3:
                        act.wait_ge(sem.prod_done, n - 2)
                    act.activation(gated[:, m, :], hidden[:, m, 0:INTER], ACT.Silu).then_inc(sem.gated_ready, 1)
                if runs(n, 2):
                    m = (j - 2) % 2
                    act.wait_ge(sem.prod_turned, n - 1)
                    if not isinstance(n, int) or n >= 4:
                        act.wait_ge(sem.y_done, n - 3)
                    act.activation(prod_t[:, m, :], bank[4 + m][:, 0:INTER], ACT.Copy).then_inc(sem.prod_kept, 1)

            expert_steps(act, emit, 2)

        @block.gpsimd
        def _(pool):
            if core.clear_slots:
                pool.memset(zero_rows, 0.0).then_inc(sem.zeroed, 1)
            pool.wait_ge(sem.gate_loaded, 80)
            pool.tensor_scalar(bs2[:], bs2[:], 0.5, 0.0, ALU.mult, ALU.add).then_inc(sem.half_ready, 1)
            pool.wait_ge(sem.half_ready, 1)
            with pool.Fori(0, BLOCKS) as i:
                pool.wait_ge(sem.normed, i + 1)
                part = x[:, bass.ds(i * BT, BT), :]
                pool.tensor_tensor(part, part, bs2[:].rearrange("p (o d) -> p o d", o=1).to_broadcast([P, BT, D]), ALU.add
                                   ).then_inc(sem.bs2_added, 1)

            def shared_block(i):
                pool.wait_ge(sem.silu_ready, 2 * i + 2)
                pool.wait_ge(sem.lin_ready, 2 * i + 2)
                if not isinstance(i, int) or i > 0:
                    pool.wait_ge(sem.down_ready, 2 * i)
                pool.tensor_tensor(s_prod.rearrange("p c n -> p (c n)"), s_silu[:].rearrange("p c n -> p (c n)"),
                                   s_lin[:].rearrange("p c n -> p (c n)"), ALU.mult).then_inc(sem.prod_ready, 1)

            def shared_out(i):
                for j in range(2):
                    pool.wait_ge(sem.z_ready, 2 * i + j + 1)
                    pair = x[:, bass.ds(i * BT + 2 * j, 2), :].rearrange("p n d -> p (n d)")
                    pool.tensor_tensor(pair, pair, z_half[:, j, :], ALU.add).then_inc(sem.z_added, 1)

            def send(t):
                for k in range(TOPK):
                    pool.indirect_dma_start(out=x_slots, out_offset=bass.IndirectOffsetOnAxis(ap=slots[:, t, k:k + 1], axis=0),
                                            in_=xn[:, t, :], in_offset=None).then_inc(sem.sent, 16)

            pool.wait_ge(sem.bs2_added, BLOCKS)
            shared_block(0)
            shared_block(1)
            shared_out(0)
            with pool.Fori(1, FIRST_SHARED // 2) as k:
                for q in range(2):
                    shared_block(k * 2 + q)
                    shared_out(k * 2 + q - 1)
            pool.wait_ge(sem.slots_ready, 1)
            if core.clear_slots:
                pool.wait_ge(sem.cleared, 16)
            per = -(-TILES // (BLOCKS - FIRST_SHARED))
            for i in range(FIRST_SHARED, BLOCKS):
                shared_block(i)
                shared_out(i - 1)
                for t in range((i - FIRST_SHARED) * per, min(TILES, (i - FIRST_SHARED + 1) * per)):
                    send(t)
            shared_out(BLOCKS - 1)
            for stored in row_stored:
                pool.wait_ge(stored, 16 * (SLOT_TILES // ROUND))
            for t in range(TILES):
                if t >= 8:
                    pool.wait_ge(sem.combined, t - 7)
                for k in range(TOPK):
                    pool.indirect_dma_start(out=back[:, 2 * (t % 8) + k, :], out_offset=None, in_=y_slots,
                                            in_offset=bass.IndirectOffsetOnAxis(ap=slots[:, t, k:k + 1], axis=0)
                                            ).then_inc(fetched[t % 8], 16)

        @block.vector
        def _(dve):
            norm_statistics(nc, dve, None, core, s, sem)

            def normalize(i):
                if not isinstance(i, int) or i > 0:
                    dve.wait_ge(sem.turned, i)
                for buf, signal in ((stage, sem.staged), (xn, sem.normed)):
                    for j in range(BT):
                        t = i * BT + j
                        dst = stage[:, j, :] if buf is stage else tile(xn, t)
                        last = dve.tensor_scalar(dst, tile(x, t), s.mean[:, bass.ds(t, 1)], s.rstd[:, bass.ds(t, 1)],
                                                 ALU.subtract, ALU.mult)
                    last.then_inc(signal, 1)

            logits = table[0].rearrange("p (t e) -> p t e", e=E)

            def gate_block(i):
                dve.wait_ge(sem.turned, i + 1)
                dve.tensor_copy(xnt[:, 1, bass.ds(i * BW, BW)], bank[1][:, :]).then_inc(sem.xnt1_ready, 1)

            def store_logits(i):
                dve.wait_ge(sem.logits_turned, i + 1)
                dve.tensor_copy(logits[:, bass.ds(i * BT, BT), :].rearrange("p t e -> p (t e)"), bank[3][:, 0:BT * E]
                                ).then_inc(sem.logits_stored, 1)

            normalize(0)
            gate_block(0)
            with dve.Fori(1, BLOCKS) as i:
                normalize(i)
                store_logits(i - 1)
                gate_block(i)
            store_logits(BLOCKS - 1)

            n = [0]

            def step(ins):
                n[0] += 1
                ins.then_inc(sem.route_step, 1)
                dve.wait_ge(sem.route_step, n[0])

            def by_expert(tab):
                return tab.rearrange("p (t e) -> p t e", e=E)

            def by_group(tab):
                return tab.rearrange("p (q m) -> p q m", m=E // G)

            def spread(ap, m):
                return ap.rearrange("p (n o) -> p n o", o=1).to_broadcast([P, ap.shape[1], m])

            def rows(ap, r):
                return ap.rearrange("p (o m) -> p o m", o=1).to_broadcast([P, r, ap.shape[1]])

            top, total = col[:, 0, :], col[:, 1, :]
            probs, score, work, first, second = table[1], table[2], table[3], table[4], table[5]
            equal, above = table[6], table[7]
            gsum, keep = table[8][:, 0:TILES * G], table[8][:, 256:256 + TILES * G]
            pairs = region[:, 9:11, :].rearrange("p a b -> p (a b)")[:, 0:TILES * G * 6].rearrange("p (q m) -> p q m", m=6)
            dve.wait_ge(sem.logits_stored, BLOCKS)
            step(dve.tensor_reduce(top, logits, AX, ALU.max))
            dve.tensor_tensor(by_expert(probs), logits, spread(top, E), ALU.subtract).then_inc(sem.shifted, 1)
            dve.wait_ge(sem.exp_ready, 1)
            step(dve.tensor_reduce(total, by_expert(probs), AX, ALU.add))
            step(dve.reciprocal(total, total))
            step(dve.tensor_tensor(by_expert(probs), by_expert(probs), spread(total, E), ALU.mult))
            step(dve.tensor_tensor(by_expert(score), by_expert(probs), rows(gate_b[:], TILES), ALU.add))
            quad = by_group(score)
            dve.tensor_tensor(pairs[:, :, 0:3], quad[:, :, 0:3], quad[:, :, 1:4], ALU.add)
            dve.tensor_tensor(pairs[:, :, 3:5], quad[:, :, 0:2], quad[:, :, 2:4], ALU.add)
            step(dve.tensor_tensor(pairs[:, :, 5:6], quad[:, :, 0:1], quad[:, :, 3:4], ALU.add))
            step(dve.tensor_reduce(gsum, pairs, AX, ALU.max))
            others = gsum.rearrange("p (t o g) -> p t o g", o=1, g=G).to_broadcast([P, TILES, G, G])
            own = gsum.rearrange("p (t g o) -> p t g o", o=1, g=G).to_broadcast([P, TILES, G, G])
            square = lambda tab: tab.rearrange("p (t g h) -> p t g h", g=G, h=G)
            dve.tensor_tensor(square(above), others, own, ALU.is_gt)
            step(dve.tensor_tensor(square(equal), others, own, ALU.is_equal))
            step(dve.tensor_tensor(by_expert(equal), by_expert(equal), rows(core.lower4[:].rearrange("p g h -> p (g h)"), TILES), ALU.mult))
            step(dve.tensor_tensor(above, above, equal, ALU.add))
            step(dve.tensor_reduce(keep, above.rearrange("p (q m) -> p q m", m=G), AX, ALU.add))
            step(dve.tensor_scalar(keep, keep, float(2), None, ALU.is_lt))
            step(dve.tensor_tensor(quad, quad, spread(keep, E // G), ALU.mult))
            step(dve.tensor_scalar(keep, keep, 1.0, -LOWEST, ALU.subtract, ALU.mult))
            step(dve.tensor_tensor(quad, quad, spread(keep, E // G), ALU.add))
            for k, pick in ((0, first), (1, second)):
                step(dve.tensor_reduce(top, by_expert(score), AX, ALU.max))
                step(dve.tensor_tensor(by_expert(work), by_expert(score), spread(top, E), ALU.is_equal))
                step(dve.tensor_tensor(by_expert(work), by_expert(work), rows(core.falling[:], TILES), ALU.mult))
                step(dve.tensor_reduce(top, by_expert(work), AX, ALU.max))
                step(dve.tensor_tensor(by_expert(pick), by_expert(work), spread(top, E), ALU.is_equal))
                if k == 0:
                    step(dve.scalar_tensor_tensor(score, first, LOWEST, score, ALU.mult, ALU.add))
            dve.tensor_tensor(assigned[:], first, second, ALU.add).then_inc(sem.pairs_ready, 1)
            for k, pick in ((0, first), (1, second)):
                step(dve.tensor_tensor(work, pick, probs, ALU.mult))
                step(dve.tensor_reduce(weight[:, k, :], by_expert(work), AX, ALU.add))
            step(dve.tensor_scalar(weight[:].rearrange("p k t -> p (k t)"), weight[:].rearrange("p k t -> p (k t)"), 0.5, None, ALU.mult))
            per_tile, ahead, offset = table[11], table[12], table[13]
            expert_major = lambda tab: tab.rearrange("p (e t) -> p e t", t=TILES)
            count, tiles_of, tiles_end, shift = small[:, 0, :], small[:, 1, :], small[:, 2, :], small[:, 3, :]
            dve.wait_ge(sem.counted, 1)
            step(dve.tensor_copy(expert_major(per_tile), bank[7][:, :].rearrange("p (t e) -> p e t", e=E)))
            step(dve.tensor_reduce(count, expert_major(per_tile), AX, ALU.add))
            step(dve.tensor_tensor_scan(ahead, core.ones[:, 0:1].to_broadcast([P, TILES * E]), per_tile, 0.0, ALU.mult, ALU.add))
            step(dve.tensor_tensor(ahead, ahead, per_tile, ALU.subtract))
            step(dve.tensor_tensor(expert_major(work), spread(count, TILES), rows(core.full_tiles[:], E), ALU.is_gt))
            step(dve.tensor_reduce(tiles_of, expert_major(work), AX, ALU.add))
            step(dve.tensor_tensor_scan(tiles_end, core.ones[:, 0:1].to_broadcast([P, E]), tiles_of, 0.0, ALU.mult, ALU.add))
            step(dve.tensor_tensor(shift, tiles_end, tiles_of, ALU.subtract))
            step(dve.scalar_tensor_tensor(shift, shift, float(P), expert_major(ahead)[:, :, 0], ALU.mult, ALU.subtract))
            step(dve.tensor_tensor(offset.rearrange("p (t e) -> p e t", e=E), expert_major(ahead), spread(shift, TILES), ALU.add))
            step(dve.tensor_tensor(offset, bank[6][:, :], offset, ALU.add))
            for k, pick in ((0, first), (1, second)):
                step(dve.tensor_tensor(work, pick, offset, ALU.mult))
                step(dve.tensor_reduce(slots_f[:, :, k], by_expert(work), AX, ALU.add))
            step(dve.tensor_tensor(expert_hit, tiles_end[0:1, :].rearrange("p (o e) -> p o e", o=1).to_broadcast([1, SLOT_TILES, E]),
                                   core.tile_id[:].rearrange("p (n o) -> p n o", o=1).to_broadcast([1, SLOT_TILES, E]), ALU.is_le))
            step(dve.tensor_reduce(expert_f[:], expert_hit, AX, ALU.add))
            dve.tensor_scalar(expert_of[:], expert_f[:], float(E - 1), None, ALU.min)
            dve.tensor_copy(slots[:].rearrange("p t k -> p (t k)"), slots_f[:].rearrange("p t k -> p (t k)")).then_inc(sem.slots_ready, 1)

            dve.wait_ge(sem.biases_loaded, 48)
            dve.wait_ge(sem.slots_ready, 1)

            def emit(n, j, r):
                if runs(n, 1):
                    m = (j - 1) % 2
                    expert = dve.value_load(expert_of[0:1, bass.ds(n - 1, 1)], min_val=0, max_val=E - 1)
                    dve.wait_ge(sem.up_done, n)
                    if not isinstance(n, int) or n >= 3:
                        dve.wait_ge(sem.prod_done, n - 2)
                    dve.tensor_tensor(hidden[:, m, :], bank[2 + m][:, 0:2 * INTER],
                                      region[:, bass.ds(expert, 1), 0:2 * INTER].rearrange("p o f -> p (o f)"), ALU.add
                                      ).then_inc(sem.hidden_ready, 1)
                if runs(n, 4):
                    m = (j - 4) % 2
                    expert = dve.value_load(expert_of[0:1, bass.ds(n - 4, 1)], min_val=0, max_val=E - 1)
                    dve.wait_ge(sem.y_done, n - 3)
                    if not isinstance(n, int) or n >= 2 * ROUND:
                        dve.wait_ge(row_stored[j % ROUND], 16 * r - 16)
                    dve.tensor_tensor(y_rows[:, (j - 4) % ROUND, :], bank[6 + m][:, 0:D],
                                      region[:, bass.ds(expert, 1), 2 * INTER:].rearrange("p o f -> p (o f)"), ALU.add
                                      ).then_inc(sem.y_ready, 1)
                if runs(n, 1):
                    m = (j - 1) % 2
                    dve.wait_ge(sem.gated_ready, n)
                    if not isinstance(n, int) or n >= 3:
                        dve.wait_ge(sem.prod_turned, n - 2)
                    dve.tensor_tensor(prod[:, m, :], gated[:, m, :], hidden[:, m, INTER:], ALU.mult).then_inc(sem.prod_done, 1)

            for n in range(2 * ROUND):
                emit(n, n, n // ROUND)
            with dve.Fori(2, SLOT_TILES // ROUND) as i:
                for j in range(ROUND):
                    emit(i * ROUND + j, j, i)
            for n in range(SLOT_TILES, SLOT_TILES + 4):
                emit(n, n, n // ROUND)

            dve.wait_ge(sem.z_added, 2 * BLOCKS)
            added = [0]

            def combine(t, i):
                xt = tile(x, t)
                dve.wait_ge(fetched[added[0] % 8], 32 * (i + 1))
                dve.scalar_tensor_tensor(xt, back[:, 2 * (added[0] % 8), :], weight[:, 0, bass.ds(t, 1)], xt, ALU.mult, ALU.add
                                         ).then_inc(sem.stats, 1)
                dve.wait_ge(sem.stats, t + TILES + 1)
                dve.scalar_tensor_tensor(xt, back[:, 2 * (added[0] % 8) + 1, :], weight[:, 1, bass.ds(t, 1)], xt, ALU.mult, ALU.add
                                         ).then_inc(sem.combined, 1)
                added[0] += 1

            with dve.Fori(0, TILES // 8) as i:
                for j in range(8):
                    combine(i * 8 + j, i)
    give_back(nc, sem, row_loaded, row_stored, fetched)


def attention(nc, core, w, tag):
    q_dram = nc.dram_tensor(f"{tag}_q", (BLOCKS, GROUPS, P, BW), FP16, kind="Internal").ap()
    k_dram = nc.dram_tensor(f"{tag}_k", (BLOCKS, GROUPS, P, BW), FP16, kind="Internal").ap()
    v_dram = nc.dram_tensor(f"{tag}_v", (BLOCKS, GROUPS, BT, P, P), FP32, kind="Internal").ap()
    lines(nc, core, w, f"{tag}_lines", q_dram, k_dram, v_dram)
    attend(nc, core, w, f"{tag}_attend", q_dram, k_dram, v_dram)


def lines(nc, core, w, tag, q_dram, k_dram, v_dram):
    ctx = ExitStack()
    with ctx:
        sb = lambda name, shape, dt=FP32: ctx.enter_context(nc.sbuf_tensor(f"{tag}_{name}", shape, dt))
        x, bank = core.x, core.bank
        s = Core()
        s.parts, s.mean, s.gap = sb("parts", [P, TILES, 6]), sb("mean", [P, TILES]), sb("gap", [P, TILES])
        s.var, s.root, s.rstd = sb("var", [P, TILES]), sb("root", [P, TILES]), sb("rstd", [P, TILES])
        w_now = sb("w_now", [P, DC, 2 * D])
        w_prev = sb("w_prev", [P, DC, P])
        b_v, b_o = sb("b_v", [P, D]), sb("b_o", [P, D])
        goes_on = sb("goes_on", [P, BLOCKS])
        stage = sb("stage", [P, BT, D])
        xt = sb("xt", [P, DC, 1 + BW])
        points = sb("points", [P, 2 * BT, 2, H, 4])
        line, other = sb("line", [P, 2 * BT * H, PL]), sb("other", [P, 2 * BT * H, PL])
        size, inverse = sb("size", [P, 2 * BT * H]), sb("inverse", [P, 2 * BT * H])
        feats = sb("feats", [P, 2, BT * H, HR], FP16)
        q_out, k_out = sb("q_out", [P, GROUPS, BW], FP16), sb("k_out", [P, GROUPS, BW], FP16)
        v_out = sb("v_out", [P, BT, H, HR])
        sem = semaphores(nc, tag, "weights_loaded stat_step stats var_ready root_ready filled staged turned xt0_ready xt1_ready "
                    "projected points_ready value_ready other_ready line_step squared size_ready feats_ready "
                    "store_turn q_turned k_turned q_ready k_ready q_stored k_stored v_stored bo_added")
        block = ctx.enter_context(nc.Block())
        WEIGHTS = 16 * 9

        @block.sync
        def _(sp):
            heads = [(w["W1_q"], 0), (w["W2_q"], 64), (w["W1_k"], 128), (w["W2_k"], 192), (w["W_v"], 256)]
            for weight, at in heads:
                n = weight.shape[1]
                sp.dma_start(w_now[:, :, at:at + n], weight[0:D, :].rearrange("(c p) n -> p c n", p=P)).then_inc(sem.weights_loaded, 16)
            for weight, at in heads[0:2]:
                sp.dma_start(w_prev[:, :, at:at + 64], weight[D:2 * D, :].rearrange("(c p) n -> p c n", p=P)).then_inc(sem.weights_loaded, 16)
            sp.dma_start(b_v[:], over_partitions(w["b_v"], P, D)).then_inc(sem.weights_loaded, 16)
            sp.dma_start(b_o[:], over_partitions(w["b_o"], P, D)).then_inc(sem.weights_loaded, 16)
            with sp.Fori(0, BLOCKS) as i:
                sp.wait_ge(sem.value_ready, BT * i + BT)
                for j in range(BT):
                    sp.dma_start(v_dram[bass.ds(i, 1), :, j, :, :].rearrange("o g p n -> p (o g) n"),
                                 v_out[:, j, :, :].rearrange("p (g h) r -> p g (h r)", g=GROUPS)).then_inc(sem.v_stored, 16)
                sp.wait_ge(sem.q_ready, 2 * i + 2)
                sp.sem_inc(sem.store_turn, 1)
                sp.dma_start(q_dram[bass.ds(i, 1), :, :, :].rearrange("o g p n -> p (o g) n"), q_out[:]).then_inc(sem.q_stored, 16)
                sp.wait_ge(sem.k_ready, 2 * i + 2)
                sp.sem_inc(sem.store_turn, 1)
                sp.dma_start(k_dram[bass.ds(i, 1), :, :, :].rearrange("o g p n -> p (o g) n"), k_out[:]).then_inc(sem.k_stored, 16)
            sp.wait_ge(sem.v_stored, 16 * BT * BLOCKS)
            sp.wait_ge(sem.q_stored, 16 * BLOCKS)
            sp.wait_ge(sem.k_stored, 16 * BLOCKS)

        @block.gpsimd
        def _(pool):
            pool.memset(feats[:], 0.0)
            pool.memset(xt[:], 0.0)
            pool.memset(v_out[:], 1.0)
            pool.memset(goes_on[:], 1.0).then_inc(sem.filled, 1)
            pool.wait_ge(sem.filled, 1)
            pool.memset(goes_on[:, 0:BLOCKS:BLOCKS // BATCH], 0.0).then_inc(sem.filled, 1)
            pool.wait_ge(sem.weights_loaded, WEIGHTS)
            with pool.Fori(0, BLOCKS) as i:
                pool.wait_ge(sem.staged, i + 1)
                part = x[:, bass.ds(i * BT, BT), :]
                pool.tensor_tensor(part, part, b_o[:].rearrange("p (o d) -> p o d", o=1).to_broadcast([P, BT, D]), ALU.add
                                   ).then_inc(sem.bo_added, 1)
                pool.wait_ge(sem.points_ready, BT * i + BT)
                p1, p2 = points[:, :, 0, :, :], points[:, :, 1, :, :]
                o = other[:].rearrange("p (a h) c -> p a h c", h=H)
                spread = lambda ap, m: ap.to_broadcast([P, 2 * BT, H, m])
                pool.wait_ge(sem.squared, i + 1)
                pool.tensor_tensor(o[:, :, :, 0:3], p1[:, :, :, 1:4], spread(p2[:, :, :, 0:1], 3), ALU.mult)
                pool.tensor_tensor(o[:, :, :, 3:5], p1[:, :, :, 2:4], spread(p2[:, :, :, 1:2], 2), ALU.mult)
                pool.tensor_tensor(o[:, :, :, 5:6], p1[:, :, :, 3:4], p2[:, :, :, 2:3], ALU.mult).then_inc(sem.other_ready, 1)

        @block.tensor
        def _(pe):
            pe.wait_ge(sem.weights_loaded, WEIGHTS)
            pe.wait_ge(sem.filled, 2)

            def block_step(i):
                pe.wait_ge(sem.staged, i + 1)
                if not isinstance(i, int) or i > 0:
                    pe.wait_ge(sem.k_ready, 2 * i)
                for c in range(DC):
                    for j in range(BT):
                        last = pe.transpose(bank[c][:, j * P:(j + 1) * P], stage[:, j, c * P:(c + 1) * P], core.ident[:])
                last.then_inc(sem.turned, 1)
                pe.wait_ge(sem.xt0_ready, 2 * i + 2)
                pe.wait_ge(sem.xt1_ready, i + 1)
                for j in range(BT):
                    if not isinstance(i, int) or i > 0:
                        pe.wait_ge(sem.points_ready, BT * (i - 1) + j + 1)
                        pe.wait_ge(sem.value_ready, BT * (i - 1) + j + 1)
                    now = lambda c: xt[:, c, 1 + j * P:1 + (j + 1) * P]
                    pe.matmul(bank[2 + j], now(0), w_now[:, 0, :], start=True, stop=False)
                    for c in range(DC):
                        pe.matmul(bank[2 + j][:, 0:P], xt[:, c, j * P:(j + 1) * P], w_prev[:, c, :], start=False, stop=False)
                    pe.matmul(bank[2 + j], now(1), w_now[:, 1, :], start=False, stop=True).then_inc(sem.projected, 1)
                pe.wait_ge(sem.feats_ready, i + 1)
                for side, first, signal in ((0, 6, sem.q_turned), (1, 0, sem.k_turned)):
                    if side == 0 and (not isinstance(i, int) or i > 0):
                        pe.wait_ge(sem.q_ready, 2 * i)
                    for g in range(GROUPS):
                        turned = bank[first + g // 2].bitcast(FP16)
                        for j in range(BT):
                            at = (g % 2) * BW + j * P
                            last = pe.transpose(turned[:, at:at + P],
                                                feats[:, side, j * H + g * HG:j * H + (g + 1) * HG, :].rearrange("p h r -> p (h r)"),
                                                core.ident16[:])
                        if g % 2:
                            last.then_inc(signal, 1)

            block_step(0)
            with pe.Fori(1, BLOCKS) as i:
                block_step(i)

        @block.scalar
        def _(act):
            norm_statistics(nc, None, act, core, s, sem)
            act.wait_ge(sem.filled, 2)

            def block_step(i):
                act.wait_ge(sem.turned, i + 1)
                if not isinstance(i, int) or i > 0:
                    act.wait_ge(sem.projected, BT * i)
                act.activation(xt[:, 0, 0:1], xt[:, 0, BW:BW + 1], ACT.Copy, scale=goes_on[:, bass.ds(i, 1)]).then_inc(sem.xt0_ready, 1)
                act.wait_ge(sem.xt0_ready, 2 * i + 1)
                act.activation(xt[:, 0, 1:], bank[0], ACT.Copy).then_inc(sem.xt0_ready, 1)
                for j in range(BT):
                    act.wait_ge(sem.value_ready, BT * i + j + 1)
                    if j == 0 and (not isinstance(i, int) or i > 0):
                        act.wait_ge(sem.other_ready, i)
                        act.wait_ge(sem.squared, i + 1)
                    act.activation(points[:, j:2 * BT:BT, :, :, :].rearrange("p a b h c -> p a (b h c)"),
                                   bank[2 + j][:, 0:2 * P].rearrange("p (a n) -> p a n", a=2), ACT.Copy).then_inc(sem.points_ready, 1)
                act.wait_ge(sem.squared, i + 2)
                act.activation(size[:], size[:], ACT.Sqrt).then_inc(sem.size_ready, 1)
                for g in range(2):
                    act.wait_ge(sem.q_turned, 2 * i + g + 1)
                    if g == 0 and (not isinstance(i, int) or i > 0):
                        act.wait_ge(sem.q_stored, 16 * i)
                    act.activation(q_out[:, 2 * g:2 * g + 2, :].rearrange("p g n -> p (g n)"), bank[6 + g].bitcast(FP16), ACT.Copy
                                   ).then_inc(sem.q_ready, 1)

            block_step(0)
            with act.Fori(1, BLOCKS) as i:
                block_step(i)

        STEPS = 10

        @block.vector
        def _(dve):
            norm_statistics(nc, dve, None, core, s, sem)
            dve.wait_ge(sem.filled, 2)
            dve.wait_ge(sem.weights_loaded, WEIGHTS)
            dve.sem_inc(sem.squared, 1)

            def block_step(i):
                n = [0]

                def step(ins):
                    n[0] += 1
                    ins.then_inc(sem.line_step, 1)
                    dve.wait_ge(sem.line_step, i * STEPS + n[0])

                for j in range(BT):
                    t = i * BT + j
                    if j == 0 and (not isinstance(i, int) or i > 0):
                        dve.wait_ge(sem.turned, i)
                    last = dve.tensor_scalar(stage[:, j, :], x[:, bass.ds(t, 1), :].rearrange("p o d -> p (o d)"),
                                             s.mean[:, bass.ds(t, 1)], s.rstd[:, bass.ds(t, 1)], ALU.subtract, ALU.mult)
                last.then_inc(sem.staged, 1)
                dve.wait_ge(sem.turned, i + 1)
                if not isinstance(i, int) or i > 0:
                    dve.wait_ge(sem.projected, BT * i)
                step(dve.tensor_scalar(xt[:, 1, 0:1], xt[:, 1, BW:BW + 1], goes_on[:, bass.ds(i, 1)], None, ALU.mult))
                dve.tensor_copy(xt[:, 1, 1:], bank[1]).then_inc(sem.xt1_ready, 1)
                for j in range(BT):
                    dve.wait_ge(sem.projected, BT * i + j + 1)
                    if j == 0 and (not isinstance(i, int) or i > 0):
                        dve.wait_ge(sem.v_stored, 16 * BT * i)
                    dve.tensor_tensor(v_out[:, j, :, 0:DH], bank[2 + j][:, 2 * P:].rearrange("p (h d) -> p h d", h=H),
                                      b_v[:].rearrange("p (h d) -> p h d", h=H), ALU.add).then_inc(sem.value_ready, 1)
                dve.wait_ge(sem.points_ready, BT * i + BT)
                p1, p2 = points[:, :, 0, :, :], points[:, :, 1, :, :]
                o = line[:].rearrange("p (a h) c -> p a h c", h=H)
                spread = lambda ap, m: ap.to_broadcast([P, 2 * BT, H, m])
                dve.tensor_tensor(o[:, :, :, 0:3], spread(p1[:, :, :, 0:1], 3), p2[:, :, :, 1:4], ALU.mult)
                dve.tensor_tensor(o[:, :, :, 3:5], spread(p1[:, :, :, 1:2], 2), p2[:, :, :, 2:4], ALU.mult)
                step(dve.tensor_tensor(o[:, :, :, 5:6], p1[:, :, :, 2:3], p2[:, :, :, 3:4], ALU.mult))
                dve.wait_ge(sem.other_ready, i + 1)
                step(dve.tensor_tensor(line[:], line[:], other[:], ALU.subtract))
                step(dve.tensor_tensor(other[:], line[:], line[:], ALU.mult))
                dve.tensor_reduce(size[:], other[:], AX, ALU.add).then_inc(sem.squared, 1)
                dve.wait_ge(sem.size_ready, i + 1)
                step(dve.tensor_scalar(size[:], size[:], 1e-12, None, ALU.max))
                step(dve.reciprocal(inverse[:], size[:]))
                step(dve.tensor_tensor(line[:], line[:], inverse[:].rearrange("p (n o) -> p n o", o=1)
                                       .to_broadcast([P, 2 * BT * H, PL]), ALU.mult))
                lq, lk = line[:, 0:BT * H, :], line[:, BT * H:, :]
                step(dve.tensor_scalar(lk[:, :, 1:5:3], lk[:, :, 1:5:3], -1.0, None, ALU.mult))
                if not isinstance(i, int) or i > 0:
                    dve.wait_ge(sem.k_turned, 2 * i)
                twice = lambda ap: ap.rearrange("p n (o c) -> p n o c", o=1).to_broadcast([P, BT * H, 2, PL])
                lk = lk[:, :, ::-1]
                q_high = feats[:, 0, :, 0:2 * PL].rearrange("p n (a c) -> p n a c", a=2)
                q_low = feats[:, 0, :, 2 * PL:4 * PL].rearrange("p n (a c) -> p n a c", a=2)
                k_both = feats[:, 1, :, 0:4 * PL].rearrange("p n (a c) -> p n a c", a=2)
                k_high, k_low = k_both[:, :, :, 0:PL], k_both[:, :, :, PL:]
                step(dve.tensor_copy(q_high, twice(lq)))
                step(dve.tensor_copy(k_high, twice(lk)))
                dve.tensor_tensor(q_low, twice(lq), q_high, ALU.subtract)
                dve.tensor_tensor(k_low, twice(lk), k_high, ALU.subtract).then_inc(sem.feats_ready, 1)
                for g in range(2):
                    dve.wait_ge(sem.k_turned, 2 * i + g + 1)
                    if g == 0 and (not isinstance(i, int) or i > 0):
                        dve.wait_ge(sem.k_stored, 16 * i)
                    dve.tensor_copy(k_out[:, 2 * g:2 * g + 2, :].rearrange("p g n -> p (g n)"), bank[g].bitcast(FP16)
                                    ).then_inc(sem.k_ready, 1)
                assert n[0] == STEPS

            block_step(0)
            with dve.Fori(1, BLOCKS) as i:
                block_step(i)
    give_back(nc, sem)


def attend(nc, core, w, tag, q_dram, k_dram, v_dram):
    ctx = ExitStack()
    with ctx:
        sb = lambda name, shape, dt=FP32: ctx.enter_context(nc.sbuf_tensor(f"{tag}_{name}", shape, dt))
        x, banks = core.x, core.banks
        SLOTS, RING, LAG = 3, 4, 2
        ALL = BATCH * GROUPS
        q_now = sb("q_now", [P, HG, T], FP16)
        k_now = sb("k_now", [P, T], FP16)
        v_now = sb("v_now", [P, KT, P])
        probs = sb("probs", [P, RING, HG, QW])
        w_o = sb("w_o", [P, GROUPS, D])
        sums, below = sb("sums", [P, QW]), sb("below", [P, QW])
        heads = sb("heads", [P, 2, QW])
        score = [banks[:, 2 * n:2 * n + 2, :] for n in range(SLOTS)]
        out_bank, proj_bank = banks[:, 6, :], banks[:, 7, :]
        sem = semaphores(nc, tag, "zeroed w_loaded mask_turn shuffle_turn load_turn scores_ready exp_done masked pv_done sums_kept chain_step heads_ready "
                    "proj_done proj_added")
        q_loaded, kv_loaded = ring_semaphores(nc, f"{tag}_q_loaded", QC), ring_semaphores(nc, f"{tag}_kv_loaded", QC)
        block = ctx.enter_context(nc.Block())

        per_chunk = QW // P
        units = [(qc, kt, max(0, kt - per_chunk * qc) * P) for qc in range(QC) for kt in range(per_chunk * (qc + 1))]
        U = len(units)
        last_of = [max(u for u, v in enumerate(units) if v[0] == qc) for qc in range(QC)]
        diagonal = [u for u, (qc, kt, _) in enumerate(units) if kt >= per_chunk * qc]
        project_at = {10: (3, 0), 11: (3, 1), 12: (0, 0), 13: (0, 1), 21: (1, 0), 22: (1, 1), 33: (2, 0), 34: (2, 1)}
        turn = {3: 0, 0: 1, 1: 2, 2: 3}

        def projected_before(g, qc, half):
            return 2 * (QC * g - 1 + turn[qc]) + half

        def batch_of(g):
            return g // GROUPS

        def groups(eng, emit, end=None):
            emit(0)
            with eng.Fori(1, end or ALL) as g:
                emit(g)

        def later(g):
            return not isinstance(g, int) or g > 0

        @block.sync
        def _(sp):
            sp.wait_ge(sem.zeroed, 1)
            for j in range(HG):
                sp.dma_start(w_o[j * HR:j * HR + DH, :, :], w["W_o"].rearrange("(g j d) n -> j d g n", j=HG, d=DH)[j]
                             ).then_inc(sem.w_loaded, 16)

            def load_q(g, m):
                i, gr = batch_of(g) * QC + m, g % GROUPS
                for j in range(HG):
                    rows = slice(j * HR, (j + 1) * HR)
                    sp.dma_start(q_now[rows, j, m * QW:(m + 1) * QW],
                                 q_dram[bass.ds(i, 1), bass.ds(gr, 1), rows, :].rearrange("o g p n -> p (o g n)")).then_inc(q_loaded[m], 16)

            def load_kv(g, m):
                i, gr = batch_of(g) * QC + m, g % GROUPS
                sp.dma_start(k_now[:, m * QW:(m + 1) * QW],
                             k_dram[bass.ds(i, 1), bass.ds(gr, 1), :, :].rearrange("o g p n -> p (o g n)")).then_inc(kv_loaded[m], 16)
                sp.dma_start(v_now[:, m * BT:(m + 1) * BT, :],
                             v_dram[bass.ds(i, 1), bass.ds(gr, 1), :, :, :].rearrange("o g t p n -> p (o g t) n")).then_inc(kv_loaded[m], 16)

            for m in range(QC):
                load_q(0, m)
                load_kv(0, m)
            with sp.Fori(0, ALL - 1) as g:
                for m in range(QC - 1):
                    sp.wait_ge(sem.scores_ready, 2 * (U * g + last_of[m] + 1))
                    sp.sem_inc(sem.load_turn, 1)
                    load_q(g + 1, m)
                for m in range(QC):
                    sp.wait_ge(sem.pv_done, U * g + last_of[QC - 2] + 1 + (m + 1) * BT)
                    sp.sem_inc(sem.load_turn, 1)
                    load_kv(g + 1, m)
                load_q(g + 1, QC - 1)

        @block.tensor
        def _(pe):
            def half_scores(g, u, half):
                qc, kt, c0 = units[u]
                hu = 2 * u + half
                if u == 0 or units[u - 1][0] != qc:
                    if half == 0:
                        pe.wait_ge(q_loaded[qc], 16 * HG * (g + 1))
                        pe.wait_ge(kv_loaded[qc], 32 * (g + 1))
                older = hu - SLOTS if hu >= SLOTS else max(h for h in range(-SLOTS, 0) if (h + 2 * U) % SLOTS == hu % SLOTS)
                if later(g) or older >= 0:
                    pe.wait_ge(sem.exp_done, 2 * U * g + older + 1)
                for j in range(2):
                    h = 2 * half + j
                    last = pe.matmul(score[hu % SLOTS][:, j, c0:QW], k_now[:, kt * P:(kt + 1) * P],
                                     q_now[:, h, qc * QW + c0:(qc + 1) * QW], start=True, stop=True)
                last.then_inc(sem.scores_ready, 1)

            def weigh(g, u):
                qc, kt, c0 = units[u]
                pe.wait_ge(sem.exp_done, 2 * (U * g + u + 1))
                if u in diagonal:
                    pe.wait_ge(sem.masked, len(diagonal) * g + diagonal.index(u) + 1)
                if kt == 0 and (later(g) or qc > 0):
                    pe.wait_ge(sem.sums_kept, QC * g + qc)
                for h in range(HG):
                    rows = slice(h * HR, (h + 1) * HR)
                    last = pe.matmul(out_bank[rows, c0:QW], v_now[:, kt, rows], probs[:, u % RING, h, c0:QW],
                                     start=(kt == 0), stop=(u == last_of[qc]))
                last.then_inc(sem.pv_done, 1)

            def project(g, qc, half):
                mine = g - 1 if qc == QC - 1 else g
                pe.wait_ge(sem.heads_ready, QC * mine + qc + 1)
                before = projected_before(g, qc, half)
                if later(before):
                    pe.wait_ge(sem.proj_added, before)
                for j in range(2):
                    at = (2 * half + j) * P
                    last = pe.matmul(proj_bank[:, j * D:(j + 1) * D], heads[:, qc % 2, at:at + P],
                                     w_o[:, bass.ds(mine % GROUPS, 1), :].rearrange("p o d -> p (o d)"), start=True, stop=True)
                last.then_inc(sem.proj_done, 1)

            def step(g, u):
                half_scores(g, u, 0)
                half_scores(g, u, 1)
                if u >= LAG:
                    weigh(g, u - LAG)
                elif later(g):
                    weigh(g - 1, U + u - LAG)
                if u in project_at:
                    qc, half = project_at[u]
                    if qc < QC - 1 or later(g):
                        project(g, qc, half)

            def group(g):
                for u in range(U):
                    step(g, u)

            pe.wait_ge(sem.w_loaded, 16 * HG)
            groups(pe, group)
            for u in range(U - LAG, U):
                weigh(ALL - 1, u)
            for half in range(2):
                project(ALL, QC - 1, half)

        @block.scalar
        def _(act):
            def group(g):
                for u, (qc, kt, c0) in enumerate(units):
                    for half in range(2):
                        hu = 2 * u + half
                        act.wait_ge(sem.scores_ready, 2 * U * g + hu + 1)
                        if half == 0 and (later(g) or u >= RING):
                            act.wait_ge(sem.pv_done, U * g + u - RING + 1)
                        act.activation(probs[:, u % RING, 2 * half:2 * half + 2, c0:QW], score[hu % SLOTS][:, :, c0:QW], ACT.Exp,
                                       scale=SCALE).then_inc(sem.exp_done, 1)

            groups(act, group)

        @block.gpsimd
        def _(pool):
            pool.memset(q_now[:], 0.0)
            pool.memset(w_o[:], 0.0).then_inc(sem.zeroed, 1)

            def group(g):
                for u in diagonal:
                    c0 = units[u][2]
                    pool.wait_ge(sem.exp_done, 2 * (U * g + u + 1))
                    pool.sem_inc(sem.mask_turn, 1)
                    part = probs[:, u % RING, :, c0:c0 + P]
                    pool.affine_select(out=part, in_=part, compare_op=ALU.is_ge, fill=0.0, base=0,
                                       pattern=[[0, HG], [1, P]], channel_multiplier=-1).then_inc(sem.masked, 1)

            groups(pool, group)

        @block.vector
        def _(dve):
            def chunk(g, qc):
                dve.wait_ge(sem.pv_done, U * g + last_of[qc] + 1)
                if later(g) or qc > 0:
                    dve.wait_ge(sem.heads_ready, QC * g + qc)
                dve.tensor_copy(sums[:], out_bank).then_inc(sem.sums_kept, 1)
                dve.wait_ge(sem.sums_kept, QC * g + qc + 1)
                dve.sem_inc(sem.shuffle_turn, 1)
                dve.stream_shuffle(below[:], sums[:], [DH] * HR).then_inc(sem.chain_step, 1)
                dve.wait_ge(sem.chain_step, 2 * (QC * g + qc) + 1)
                dve.reciprocal(below[:], below[:]).then_inc(sem.chain_step, 1)
                dve.wait_ge(sem.chain_step, 2 * (QC * g + qc) + 2)
                dve.tensor_tensor(heads[:, qc % 2, :], sums[:], below[:], ALU.mult).then_inc(sem.heads_ready, 1)

            def add(g, qc):
                mine = g - 1 if qc == QC - 1 else g
                for half in range(2):
                    dve.wait_ge(sem.proj_done, projected_before(g, qc, half) + 1)
                    t = batch_of(mine) * KT + qc * BT + 2 * half
                    pair = x[:, bass.ds(t, 2), :].rearrange("p n d -> p (n d)")
                    dve.tensor_tensor(pair, proj_bank, pair, ALU.add).then_inc(sem.proj_added, 1)

            def group(g):
                chunk(g, 0)
                if later(g):
                    add(g, QC - 1)
                add(g, 0)
                for qc in range(1, QC - 1):
                    chunk(g, qc)
                    add(g, qc)
                chunk(g, QC - 1)

            groups(dve, group)
            add(ALL, QC - 1)
    give_back(nc, sem, q_loaded, kv_loaded)


FFN_NAMES = "gate_w gate_b We1 be1 We2 be2 We3 be3 ws1 bs1 ws2 bs2 ws3 bs3"
ATTN_NAMES = "W1_q W2_q W1_k W2_k W_v b_v W_o b_o"


def macaron(nc, d, out):
    w = {n: d[f"L0_ffn_{n}"] for n in FFN_NAMES.split()}
    a = {n: d[f"L0_attn_{n}"] for n in ATTN_NAMES.split()}
    x_slots = nc.dram_tensor("x_slots", (SLOT_TILES * P, D), FP32, kind="Internal").ap()
    y_slots = nc.dram_tensor("y_slots", (SLOT_TILES * P, D), FP32, kind="Internal").ap()
    core = Core()
    with ExitStack() as ctx:
        setup(nc, core, d["L0_attn_x"], ctx)
        core.clear_slots = True
        ffn(nc, core, w, x_slots, y_slots, "f1")
        core.clear_slots = False
        attention(nc, core, a, "attn")
        ffn(nc, core, w, x_slots, y_slots, "f2", out=out)


def kernel(**inputs):
    import numpy as np
    import concourse.bacc as bacc
    from concourse.bass_utils import run_bass_kernel_spmd

    nc = bacc.Bacc("TRN2", target_bir_lowering=False, num_devices=1)
    arrays, d = {}, {}
    for name, value in inputs.items():
        a = np.ascontiguousarray(value)
        arrays[name] = a
        d[name] = nc.dram_tensor(name, a.shape, mybir.dt.from_np(a.dtype), kind="ExternalInput").ap()
    out = nc.dram_tensor("out", (BATCH, T, D), FP32, kind="ExternalOutput").ap()
    macaron(nc, d, out)
    return run_bass_kernel_spmd(nc, [arrays], core_ids=[0]).results[0]["out"]
```

```python
from collections import namedtuple
from contextlib import ExitStack

import concourse.bass as bass
from concourse import mybir

FP32 = mybir.dt.float32
FP16 = mybir.dt.float16
BF16 = mybir.dt.bfloat16
I32 = mybir.dt.int32
ALU = mybir.AluOpType
ACT = mybir.ActivationFunctionType
AX = mybir.AxisListType.X

P = 128
BATCH, T, D = 2, 2048, 256
DC = D // P
TILES = BATCH * T // P
BT = 4
BLOCKS = TILES // BT
BW = BT * P
EPS = 1e-5

E, G, TOPK, INTER = 16, 4, 2, 128
SHARED = 2 * INTER
ROUND = 4
SLOT_TILES = -(-((TOPK * TILES * P + E * (P - 1)) // P) // ROUND) * ROUND
TO_WHOLE = 1.5 * 2.0 ** 23
LOWEST = -3.0e38

H, PL = 16, 6
DH = D // H
HG = 4
GROUPS = H // HG
HR = P // HG
QW = 512
QC = T // QW
KT = T // P
SCALE = 6.0 ** -0.5


def dma_rows(ap):
    return ap.rearrange("(n p) d -> p n d", p=P)


def over_partitions(ap, n, *shape):
    flat = ap.rearrange("(o n) -> o n", o=1) if len(ap.shape) == 1 else ap.rearrange("(o e) i -> o e i", o=1)
    return flat.to_broadcast([n, *shape])


class Core:
    pass


def setup(nc, core, x_dram, ctx):
    sb = lambda name, shape, dt=FP32: ctx.enter_context(nc.sbuf_tensor(name, shape, dt))
    core.x = sb("x_res", [P, TILES, D])
    core.ident = sb("ident", [P, P])
    core.ident16 = sb("ident16", [P, P], FP16)
    core.before = sb("before", [P, P], BF16)
    core.ones = sb("ones", [P, P], BF16)
    core.falling = sb("falling", [P, E])
    core.lower4 = sb("lower4", [P, G, G])
    core.full_tiles = sb("full_tiles", [P, TILES])
    core.tile_id = sb("tile_id", [P, SLOT_TILES])
    core.row_id = sb("row_id", [P, P])
    core.part_id = sb("part_id", [P, 1])
    core.tile_of_pair = sb("tile_of_pair", [P, TILES * TOPK])
    core.banks = ctx.enter_context(nc.psum_tensor("banks", [P, 8, 512], FP32))
    core.bank = [core.banks[:, i, :] for i in range(8)]
    x_loaded = ring_semaphores(nc, "x_loaded", BLOCKS)
    with nc.Block() as block:
        filled = nc.alloc_semaphore(name="filled")

        @block.sync
        def _(sp):
            rows = dma_rows(x_dram.rearrange("b t d -> (b t) d"))
            for b in range(BLOCKS):
                sp.dma_start(core.x[:, b * BT:(b + 1) * BT, :], rows[:, b * BT:(b + 1) * BT, :]).then_inc(x_loaded[b], 16)

        @block.gpsimd
        def _(pool):
            pool.memset(core.ident[:], 0.0)
            pool.memset(core.ident16[:], 0.0)
            pool.memset(core.before[:], 1.0)
            pool.memset(core.ones[:], 1.0)
            pool.memset(core.lower4[:], 1.0).then_inc(filled, 1)
            pool.iota(core.falling[:], [[-1, E]], base=E, channel_multiplier=0, allow_small_or_imprecise_dtypes=True)
            pool.iota(core.full_tiles[:], [[P, TILES]], base=0, channel_multiplier=0, allow_small_or_imprecise_dtypes=True)
            pool.iota(core.row_id[:], [[1, P]], base=0, channel_multiplier=0, allow_small_or_imprecise_dtypes=True)
            pool.iota(core.part_id[:], [[0, 1]], base=0, channel_multiplier=1, allow_small_or_imprecise_dtypes=True)
            pool.iota(core.tile_of_pair[:], [[1, TILES], [0, TOPK]], base=0, channel_multiplier=0, allow_small_or_imprecise_dtypes=True)
            pool.iota(core.tile_id[:], [[1, SLOT_TILES]], base=0, channel_multiplier=0, allow_small_or_imprecise_dtypes=True)
            pool.wait_ge(filled, 1)
            for eye in (core.ident, core.ident16):
                pool.affine_select(out=eye[:], in_=eye[:], compare_op=ALU.not_equal, fill=1.0, base=0,
                                   pattern=[[-1, P]], channel_multiplier=1)
            pool.affine_select(out=core.before[:], in_=core.before[:], compare_op=ALU.is_gt, fill=0.0, base=0,
                               pattern=[[1, P]], channel_multiplier=-1)
            pool.affine_select(out=core.lower4[:], in_=core.lower4[:], compare_op=ALU.is_gt, fill=0.0, base=0,
                               pattern=[[1, G], [-1, G]], channel_multiplier=0)
    return x_loaded


def norm_statistics(nc, dve, act, core, s, sem, x_loaded=None):
    if dve is not None:
        n = [0]

        def step(ins):
            n[0] += 1
            ins.then_inc(sem.stat_step, 1)
            dve.wait_ge(sem.stat_step, n[0])

        def block_statistics(i):
            for j in range(BT):
                dve.bn_stats(s.parts[:, bass.ds(i * BT + j, 1), :], core.x[:, bass.ds(i * BT + j, 1), :]
                             .rearrange("p o d -> p (o d)")).then_inc(sem.stats, 1)

        if x_loaded is None:
            with dve.Fori(0, BLOCKS) as i:
                block_statistics(i)
        else:
            for i in range(BLOCKS):
                dve.wait_ge(x_loaded[i], 16)
                block_statistics(i)
        dve.wait_ge(sem.stats, TILES)
        mean_even, m2_even = s.parts[:, :, 1], s.parts[:, :, 2]
        mean_odd, m2_odd = s.parts[:, :, 4], s.parts[:, :, 5]
        step(dve.tensor_tensor(s.mean[:], mean_even, mean_odd, ALU.add))
        step(dve.tensor_scalar(s.mean[:], s.mean[:], 0.5, None, ALU.mult))
        step(dve.tensor_tensor(s.gap[:], mean_even, mean_odd, ALU.subtract))
        step(dve.tensor_tensor(s.gap[:], s.gap[:], s.gap[:], ALU.mult))
        step(dve.tensor_tensor(s.var[:], m2_even, m2_odd, ALU.add))
        step(dve.tensor_scalar(s.var[:], s.var[:], 1.0 / D, EPS, ALU.mult, ALU.add))
        dve.scalar_tensor_tensor(s.var[:], s.gap[:], 0.25, s.var[:], ALU.mult, ALU.add).then_inc(sem.var_ready, 1)
        dve.wait_ge(sem.root_ready, 1)
        step(dve.reciprocal(s.rstd[:], s.root[:]))
    if act is not None:
        act.wait_ge(sem.var_ready, 1)
        act.activation(s.root[:], s.var[:], ACT.Sqrt).then_inc(sem.root_ready, 1)


def semaphores(nc, tag, names):
    names = names.split()
    return namedtuple("Semaphores", names)(*[nc.alloc_semaphore(name=f"{tag}_{name}") for name in names])


def ring_semaphores(nc, name, n):
    return [nc.alloc_semaphore(name=f"{name}{k}") for k in range(n)]


def give_back(nc, *kinds):
    nc.clear_and_free_semaphores([one for kind in kinds for one in kind])
    nc.all_engine_barrier()


def ffn(nc, core, w, xn_rows, y_slots, tag, x_loaded=None, out=None):
    ctx = ExitStack()
    with ctx:
        sb = lambda name, shape, dt=FP32: ctx.enter_context(nc.sbuf_tensor(f"{tag}_{name}", shape, dt))
        x, bank = core.x, core.bank
        s = Core()
        s.parts, s.mean, s.gap = sb("parts", [P, TILES, 6]), sb("mean", [P, TILES]), sb("gap", [P, TILES])
        s.var, s.root, s.rstd = sb("var", [P, TILES]), sb("root", [P, TILES]), sb("rstd", [P, TILES])
        stage = sb("stage", [P, 2, BT, D])
        UP = DC * 2 * INTER + 2
        w_all = sb("w_all", [P, E, UP + 2 * D])
        ws13 = sb("ws13", [P, DC, 2 * SHARED])
        ws2 = sb("ws2", [P, SHARED // P, D])
        bs = sb("bs", [P, 2 * SHARED // P])
        bs2 = sb("bs2", [P, D])
        gate_t = sb("gate_t", [P, DC, E])
        gate_b = sb("gate_b", [P, E])
        PAIRS = TILES * TOPK
        region = sb("region", [P, PAIRS * (P + 2 * SLOT_TILES) // 2])
        table = [region[:, n * TILES * E:(n + 1) * TILES * E] for n in range(16)]
        gate_rows, bs_rows, be_rows = table[15][0:E, 0:D], table[15][0:2 * SHARED // P, D:D + P], table[15][0:2 * E, D + P:D + 2 * P]
        row_hot = region[:, 0:PAIRS * P // 2].bitcast(BF16).rearrange("p (q s) -> p q s", q=PAIRS)
        tile_hot = region[:, PAIRS * P // 2:].bitcast(BF16).rearrange("p (q a s) -> p q a s", q=PAIRS, a=2)
        back = region[:, 0:16 * D].rearrange("p (n d) -> p n d", d=D)
        rows_in = region[:, 16 * D:(16 + ROUND) * D].rearrange("p (n d) -> p n d", d=D)
        xnt = sb("xnt", [P, DC, TILES * P])
        rings = xnt[:, :, :].rearrange("p c n -> p (c n)")
        taken = [0]

        def ring(n, width):
            at = taken[0]
            taken[0] += n * width
            return rings[:, at:at + n * width].rearrange("p (n w) -> p n w", n=n)

        w_up, w_down = ring(ROUND, UP), ring(ROUND, 2 * D)
        rows_t, gated, prod_t, y_rows = ring(2, D), ring(2, P), ring(2, P), ring(ROUND, D)
        s_silu, s_lin = sb("s_silu", [P, 2, BW]), sb("s_lin", [P, 2, BW])
        s_prod = stage[:, 0, :, :].rearrange("p t d -> p (t d)").rearrange("p (c n) -> p c n", c=2)
        logits_t = s_silu[0:E, 0, :]
        z_half = sb("z_half", [P, 2, 2 * D])
        slots = sb("slots", [P, TILES, TOPK], I32)
        slots_f = sb("slots_f", [P, PAIRS])
        slot_row, slot_tile = sb("slot_row", [P, PAIRS]), sb("slot_tile", [P, PAIRS])
        token_of = sb("token_of", [P, SLOT_TILES], I32)
        token_f = sb("token_f", [P, SLOT_TILES])
        weight = sb("weight", [P, TOPK, TILES])
        small = sb("small", [P, 4, E])
        col = sb("col", [P, 2, TILES])
        expert_of = sb("expert_of", [1, SLOT_TILES], I32)
        expert_f = sb("expert_f", [1, SLOT_TILES])
        assigned = sb("assigned", [P, TILES * E], BF16)
        expert_hit = region[0:1, 6 * TILES * E:6 * TILES * E + SLOT_TILES * E].rearrange("p (n e) -> p n e", e=E)

        sem = semaphores(nc, tag, "half_ready gate_loaded shared_loaded experts_loaded "
                         "stat_step stats var_ready root_ready gate_turned gate_ready staged turned "
                         "xnt0_ready xnt1_ready logits_ready logits_kept logits_turned logits_stored "
                         "route_step shifted exp_ready pairs_ready counted slots_ready hot_ready inverted tokens_ready "
                         "up_ready silu_ready lin_ready prod_ready down_ready z_ready z_added bs2_added "
                         "rows_turned rows_kept up_kept down_kept up_done gated_ready prod_done "
                         "y_done y_ready first_added combined out_stored")
        stage_stored = ring_semaphores(nc, f"{tag}_stage_stored", 2)
        row_loaded = ring_semaphores(nc, f"{tag}_row_loaded", ROUND)
        row_stored = ring_semaphores(nc, f"{tag}_row_stored", ROUND)
        fetched = ring_semaphores(nc, f"{tag}_fetched", 8)

        def tile(buf, t):
            return buf[:, bass.ds(t, 1), :].rearrange("p o d -> p (o d)")

        block = ctx.enter_context(nc.Block())

        def gate_steps(eng, emit, lag):
            for n in range(4):
                emit(n, n % 2, n // 2)
            with eng.Fori(2, BLOCKS // 2) as i:
                for q in range(2):
                    emit(i * 2 + q, q, i)
            for n in range(BLOCKS, BLOCKS + lag):
                emit(n, n % 2, n // 2)

        def gates(n, lag):
            return not isinstance(n, int) or 0 <= n - lag < BLOCKS

        def expert_steps(eng, emit, lag):
            for n in range(2 * ROUND):
                emit(n, n % ROUND, n // ROUND)
            with eng.Fori(2, SLOT_TILES // ROUND) as i:
                for j in range(ROUND):
                    emit(i * ROUND + j, j, i)
            for n in range(SLOT_TILES, SLOT_TILES + lag):
                emit(n, n % ROUND, n // ROUND)

        def runs(n, lag):
            return not isinstance(n, int) or 0 <= n - lag < SLOT_TILES

        def after(n, first):
            return not isinstance(n, int) or n >= first

        @block.sync
        def _(sp):
            sp.dma_start(gate_rows, w["gate_w"]).then_inc(sem.gate_loaded, 16)
            for n, name in enumerate(("bs1", "bs3")):
                sp.dma_start(bs_rows[2 * n:2 * n + 2, :], w[name].rearrange("(c p) -> c p", p=P)).then_inc(sem.gate_loaded, 16)
            for n, name in enumerate(("be1", "be3")):
                sp.dma_start(be_rows[n * E:(n + 1) * E, :], w[name]).then_inc(sem.gate_loaded, 16)
            sp.dma_start(gate_b[:], over_partitions(w["gate_b"], P, E)).then_inc(sem.gate_loaded, 16)
            sp.dma_start(bs2[:], over_partitions(w["bs2"], P, D)).then_inc(sem.gate_loaded, 16)
            sp.dma_start(ws13[:, :, 0:SHARED], w["ws1"].rearrange("(c p) f -> p c f", p=P)).then_inc(sem.shared_loaded, 16)
            sp.dma_start(ws13[:, :, SHARED:], w["ws3"].rearrange("(c p) f -> p c f", p=P)).then_inc(sem.shared_loaded, 16)
            sp.dma_start(ws2[:], w["ws2"].rearrange("(c p) d -> p c d", p=P)).then_inc(sem.shared_loaded, 16)

            def store_block(n, q, r):
                sp.wait_ge(sem.staged, n + 1)
                sp.dma_start(dma_rows(xn_rows)[:, bass.ds(n * BT, BT), :], stage[:, q, :, :]).then_inc(stage_stored[q], 16)

            gate_steps(sp, store_block, 0)
            for c in range(DC):
                sp.dma_start(w_all[:, :, 2 * c * INTER:(2 * c + 1) * INTER], w["We1"][:, c * P:(c + 1) * P, :].rearrange("e p i -> p e i")
                             ).then_inc(sem.experts_loaded, 16)
                sp.dma_start(w_all[:, :, (2 * c + 1) * INTER:(2 * c + 2) * INTER], w["We3"][:, c * P:(c + 1) * P, :].rearrange("e p i -> p e i")
                             ).then_inc(sem.experts_loaded, 16)
            sp.dma_start(w_all[:, :, UP:UP + D], w["We2"].rearrange("e i d -> i e d")).then_inc(sem.experts_loaded, 16)
            sp.dma_start(w_all[:, :, UP + D:], over_partitions(w["be2"], P, E, D)).then_inc(sem.experts_loaded, 16)

            def store_rows(n, j, r):
                sp.wait_ge(sem.y_ready, n + 1)
                sp.dma_start(y_slots[bass.ds(n * P, P), :], y_rows[:, j, :]).then_inc(row_stored[j], 16)

            expert_steps(sp, store_rows, 0)
            for stored in row_stored:
                sp.wait_ge(stored, 16 * (SLOT_TILES // ROUND))
            if out is not None:
                rows = dma_rows(out.rearrange("b t d -> (b t) d"))
                for g in range(TILES // 8):
                    sp.wait_ge(sem.combined, 8 * (g + 1))
                    sp.dma_start(rows[:, g * 8:(g + 1) * 8, :], x[:, g * 8:(g + 1) * 8, :]).then_inc(sem.out_stored, 16)
                sp.wait_ge(sem.out_stored, 16 * (TILES // 8))

        TO_COUNTS, TO_TOKENS = 2, 3

        @block.tensor
        def _(pe):
            pe.wait_ge(sem.gate_loaded, 16 * 7)
            for c in range(DC):
                pe.transpose(bank[2][:, c * E:(c + 1) * E], gate_rows[:, c * P:(c + 1) * P], core.ident[0:E, 0:E])
            pe.transpose(bank[2][:, 2 * E:2 * E + 4], bs_rows, core.ident[0:4, 0:4])
            pe.transpose(bank[2][:, 2 * E + 4:4 * E + 4], be_rows, core.ident[0:2 * E, 0:2 * E]).then_inc(sem.gate_turned, 1)
            pe.wait_ge(sem.gate_ready, 1)

            def gate_step(n, q, r):
                if gates(n, 0):
                    pe.wait_ge(sem.staged, n + 1)
                    if after(n, 1):
                        pe.wait_ge(sem.xnt0_ready, n)
                        pe.wait_ge(sem.xnt1_ready, n)
                    for c in range(DC):
                        for j in range(BT):
                            last = pe.transpose(bank[c][:, j * P:(j + 1) * P], stage[:, q, j, c * P:(c + 1) * P], core.ident[:])
                    last.then_inc(sem.turned, 1)
                if gates(n, 1):
                    pe.wait_ge(sem.xnt0_ready, n)
                    pe.wait_ge(sem.xnt1_ready, n)
                    if after(n, 2):
                        pe.wait_ge(sem.logits_kept, n - 1)
                    for c in range(DC):
                        last = pe.matmul(bank[2][0:E, :], gate_t[:, c, :], xnt[:, c, bass.ds((n - 1) * BW, BW)],
                                         start=(c == 0), stop=(c == DC - 1))
                    last.then_inc(sem.logits_ready, 1)
                if gates(n, 2):
                    pe.wait_ge(sem.logits_kept, n - 1)
                    if after(n, 3):
                        pe.wait_ge(sem.logits_stored, n - 2)
                    for j in range(BT):
                        last = pe.matmul(bank[3][:, j * E:(j + 1) * E], logits_t[:, j * P:(j + 1) * P], core.ident[0:E, 0:E], start=True, stop=True)
                    last.then_inc(sem.logits_turned, 1)

            gate_steps(pe, gate_step, 2)

            def shared_down(i):
                pe.wait_ge(sem.prod_ready, i + 1)
                for j in range(BT):
                    if j % 2 == 0 and after(i, 1):
                        pe.wait_ge(sem.z_ready, 2 * (i - 1) + j // 2 + 1)
                    for c in range(SHARED // P):
                        last = pe.matmul(bank[4 + j // 2][:, j % 2 * D:(j % 2 + 1) * D], s_prod[:, c, j * P:(j + 1) * P],
                                         ws2[:, c, :], start=(c == 0), stop=(c == SHARED // P - 1))
                    if j % 2:
                        last.then_inc(sem.down_ready, 1)

            def shared_up(i):
                for f in range(4):
                    if after(i, 1):
                        if f < 2:
                            pe.wait_ge(sem.silu_ready, 2 * (i - 1) + f + 1)
                        else:
                            pe.wait_ge(sem.lin_ready, 2 * (i - 1) + f - 1)
                    for c in range(DC):
                        last = pe.matmul(bank[f][:, :], ws13[:, c, f * P:(f + 1) * P], xnt[:, c, bass.ds(i * BW, BW)],
                                         start=(c == 0), stop=(c == DC - 1))
                    last.then_inc(sem.up_ready, 1)

            def shared_pairs(first, end):
                with pe.Fori(first, end) as k:
                    for q in range(2):
                        shared_up(k * 2 + q)
                        shared_down(k * 2 + q - 1)

            pe.wait_ge(sem.shared_loaded, 48)
            pe.wait_ge(sem.logits_stored, BLOCKS)
            shared_up(0)
            shared_up(1)
            shared_down(0)
            shared_pairs(1, TO_COUNTS)
            pe.wait_ge(sem.pairs_ready, 1)
            pe.matmul(bank[6][:, :], core.before[:], assigned[:], start=True, stop=True)
            pe.matmul(bank[7][:, :], core.ones[:], assigned[:], start=True, stop=True).then_inc(sem.counted, 1)
            shared_pairs(TO_COUNTS, TO_TOKENS)
            pe.wait_ge(sem.hot_ready, 1)
            for q in range(PAIRS):
                last = pe.matmul(bank[7][:, 0:2 * SLOT_TILES], row_hot[:, q, :], tile_hot[:, q, :, :].rearrange("p a s -> p (a s)"),
                                 start=(q == 0), stop=(q == PAIRS - 1))
            last.then_inc(sem.inverted, 1)
            shared_pairs(TO_TOKENS, BLOCKS // 2)
            shared_down(BLOCKS - 1)

            pe.wait_ge(sem.lin_ready, 2 * BLOCKS)
            pe.wait_ge(sem.z_ready, 2 * BLOCKS)

            def emit(n, j, r):
                if runs(n, 0):
                    pe.wait_ge(row_loaded[j], 16 * r + 16)
                    if after(n, 2):
                        pe.wait_ge(sem.rows_kept, n - 1)
                    for c in range(DC):
                        last = pe.transpose(bank[j % 2][:, c * P:(c + 1) * P], rows_in[:, j, c * P:(c + 1) * P], core.ident[:])
                    last.then_inc(sem.rows_turned, 1)
                if runs(n, 1):
                    at, m = (j - 1) % ROUND, (j - 1) % 2
                    pe.wait_ge(sem.up_kept, n)
                    pe.wait_ge(sem.rows_kept, n)
                    if after(n, 3):
                        pe.wait_ge(sem.prod_done, n - 2)
                    for f in range(2):
                        for c in range(DC):
                            col_at = (2 * c + f) * INTER
                            last = pe.matmul(bank[2 + m][:, f * P:(f + 1) * P], w_up[:, at, col_at:col_at + INTER],
                                             rows_t[:, m, c * P:(c + 1) * P], start=(c == 0), stop=(c == DC - 1))
                    last.then_inc(sem.up_done, 1)
                if runs(n, 2):
                    at, m = (j - 2) % ROUND, (j - 2) % 2
                    pe.wait_ge(sem.down_kept, n - 1)
                    pe.wait_ge(sem.prod_done, n - 1)
                    if after(n, 4):
                        pe.wait_ge(sem.y_ready, n - 3)
                    pe.matmul(bank[4 + m][:, 0:D], prod_t[:, m, :], w_down[:, at, 0:D], start=True, stop=True).then_inc(sem.y_done, 1)

            expert_steps(pe, emit, 2)

        @block.scalar
        def _(act):
            norm_statistics(nc, None, act, core, s, sem)
            act.wait_ge(sem.gate_turned, 1)
            act.activation(gate_t[:].rearrange("p c e -> p (c e)"), bank[2][:, 0:DC * E], ACT.Copy)
            act.activation(w_all[:, :, UP - 2:UP], bank[2][:, 2 * E + 4:4 * E + 4].rearrange("p (a e) -> p e a", a=2), ACT.Copy)
            act.activation(bs[:], bank[2][:, 2 * E:2 * E + 4], ACT.Copy).then_inc(sem.gate_ready, 1)

            def gate_step(n, q, r):
                if gates(n, 0):
                    act.wait_ge(sem.turned, n + 1)
                    act.activation(xnt[:, 0, bass.ds(n * BW, BW)], bank[0][:, :], ACT.Copy).then_inc(sem.xnt0_ready, 1)
                if gates(n, 1):
                    act.wait_ge(sem.logits_ready, n)
                    if after(n, 2):
                        act.wait_ge(sem.logits_turned, n - 1)
                    act.activation(logits_t, bank[2][0:E, :], ACT.Copy).then_inc(sem.logits_kept, 1)

            gate_steps(act, gate_step, 1)
            act.wait_ge(sem.shifted, 1)
            act.activation(table[1], table[1], ACT.Exp).then_inc(sem.exp_ready, 1)

            def shared_block(i):
                for f in range(2):
                    act.wait_ge(sem.up_ready, 4 * i + f + 1)
                    if f == 0 and after(i, 1):
                        act.wait_ge(sem.prod_ready, i)
                    act.activation(s_silu[:, f, :], bank[f][:, :], ACT.Silu, bias=bs[:, f:f + 1]).then_inc(sem.silu_ready, 1)
                for f in range(2):
                    act.wait_ge(sem.up_ready, 4 * i + f + 3)
                    act.activation(s_lin[:, f, :], bank[2 + f][:, :], ACT.Identity, bias=bs[:, 2 + f:3 + f]).then_inc(sem.lin_ready, 1)

            def shared_out(i):
                for j in range(2):
                    act.wait_ge(sem.down_ready, 2 * i + j + 1)
                    if after(i, 1):
                        act.wait_ge(sem.z_added, 2 * (i - 1) + j + 1)
                    act.activation(z_half[:, j, :], bank[4 + j][:, :], ACT.Copy, scale=0.5).then_inc(sem.z_ready, 1)

            shared_block(0)
            shared_block(1)
            shared_out(0)
            with act.Fori(2, BLOCKS) as i:
                shared_block(i)
                shared_out(i - 1)
            shared_out(BLOCKS - 1)

            act.wait_ge(sem.experts_loaded, 16 * 6)
            act.wait_ge(sem.slots_ready, 1)
            act.wait_ge(sem.up_ready, 4 * BLOCKS)

            def emit(n, j, r):
                if runs(n, 0):
                    expert = act.value_load(expert_of[0:1, bass.ds(n, 1)], min_val=0, max_val=E - 1)
                    if after(n, ROUND):
                        act.wait_ge(sem.prod_done, n - ROUND + 1)
                    act.activation(w_up[:, j, :], w_all[:, bass.ds(expert, 1), 0:UP].rearrange("p o f -> p (o f)"), ACT.Copy
                                   ).then_inc(sem.up_kept, 1)
                    act.wait_ge(sem.rows_turned, n + 1)
                    if after(n, 2):
                        act.wait_ge(sem.up_done, n - 1)
                    act.activation(rows_t[:, j % 2, :], bank[j % 2][:, 0:D], ACT.Copy).then_inc(sem.rows_kept, 1)
                if runs(n, 1):
                    at, m = (j - 1) % ROUND, (j - 1) % 2
                    act.wait_ge(sem.up_done, n)
                    act.wait_ge(sem.up_kept, n)
                    if after(n, 3):
                        act.wait_ge(sem.prod_done, n - 2)
                    act.activation(gated[:, m, :], bank[2 + m][:, 0:P], ACT.Silu, bias=w_up[:, at, UP - 2:UP - 1]).then_inc(sem.gated_ready, 1)

            expert_steps(act, emit, 1)

        @block.gpsimd
        def _(pool):
            pool.wait_ge(sem.gate_loaded, 16 * 7)
            pool.tensor_scalar(bs2[:], bs2[:], 0.5, 0.0, ALU.mult, ALU.add).then_inc(sem.half_ready, 1)
            pool.wait_ge(sem.half_ready, 1)
            with pool.Fori(0, BLOCKS) as i:
                pool.wait_ge(sem.staged, i + 1)
                part = x[:, bass.ds(i * BT, BT), :]
                pool.tensor_tensor(part, part, bs2[:].rearrange("p (o d) -> p o d", o=1).to_broadcast([P, BT, D]), ALU.add
                                   ).then_inc(sem.bs2_added, 1)

            def shared_block(i):
                pool.wait_ge(sem.silu_ready, 2 * i + 2)
                pool.wait_ge(sem.lin_ready, 2 * i + 2)
                if after(i, 1):
                    pool.wait_ge(sem.down_ready, 2 * i)
                pool.tensor_tensor(s_prod.rearrange("p c n -> p (c n)"), s_silu[:].rearrange("p c n -> p (c n)"),
                                   s_lin[:].rearrange("p c n -> p (c n)"), ALU.mult).then_inc(sem.prod_ready, 1)

            def shared_out(i):
                for j in range(2):
                    pool.wait_ge(sem.z_ready, 2 * i + j + 1)
                    pair = x[:, bass.ds(i * BT + 2 * j, 2), :].rearrange("p n d -> p (n d)")
                    pool.tensor_tensor(pair, pair, z_half[:, j, :], ALU.add).then_inc(sem.z_added, 1)

            pool.wait_ge(sem.bs2_added, BLOCKS)
            for stored in stage_stored:
                pool.wait_ge(stored, 16 * (BLOCKS // 2))
            shared_block(0)
            shared_block(1)
            shared_out(0)
            with pool.Fori(2, BLOCKS) as i:
                shared_block(i)
                shared_out(i - 1)
            shared_out(BLOCKS - 1)
            pool.wait_ge(sem.tokens_ready, 1)
            for n in range(SLOT_TILES):
                if n >= ROUND:
                    pool.wait_ge(sem.rows_turned, n - ROUND + 1)
                pool.indirect_dma_start(out=rows_in[:, n % ROUND, :], out_offset=None, in_=xn_rows,
                                        in_offset=bass.IndirectOffsetOnAxis(ap=token_of[:, n:n + 1], axis=0)
                                        ).then_inc(row_loaded[n % ROUND], 16)
            for stored in row_stored:
                pool.wait_ge(stored, 16 * (SLOT_TILES // ROUND))
            for t in range(TILES):
                if t >= 8:
                    pool.wait_ge(sem.combined, t - 7)
                for k in range(TOPK):
                    pool.indirect_dma_start(out=back[:, 2 * (t % 8) + k, :], out_offset=None, in_=y_slots,
                                            in_offset=bass.IndirectOffsetOnAxis(ap=slots[:, t, k:k + 1], axis=0)
                                            ).then_inc(fetched[t % 8], 16)

        @block.vector
        def _(dve):
            norm_statistics(nc, dve, None, core, s, sem, x_loaded)
            logits = table[0].rearrange("p (t e) -> p t e", e=E)

            def gate_step(n, q, r):
                if gates(n, 0):
                    if after(n, 2):
                        dve.wait_ge(sem.turned, n - 1)
                        dve.wait_ge(stage_stored[q], 16 * r)
                    for j in range(BT):
                        t = n * BT + j
                        last = dve.tensor_scalar(stage[:, q, j, :], tile(x, t), s.mean[:, bass.ds(t, 1)], s.rstd[:, bass.ds(t, 1)],
                                                 ALU.subtract, ALU.mult)
                    last.then_inc(sem.staged, 1)
                if gates(n, 1):
                    dve.wait_ge(sem.turned, n)
                    dve.tensor_copy(xnt[:, 1, bass.ds((n - 1) * BW, BW)], bank[1][:, :]).then_inc(sem.xnt1_ready, 1)
                if gates(n, 3):
                    dve.wait_ge(sem.logits_turned, n - 2)
                    if isinstance(n, int) and n == 3:
                        dve.wait_ge(sem.gate_ready, 1)
                    dve.tensor_copy(logits[:, bass.ds((n - 3) * BT, BT), :].rearrange("p t e -> p (t e)"), bank[3][:, 0:BT * E]
                                    ).then_inc(sem.logits_stored, 1)

            gate_steps(dve, gate_step, 3)

            n = [0]

            def step(ins):
                n[0] += 1
                ins.then_inc(sem.route_step, 1)
                dve.wait_ge(sem.route_step, n[0])

            def by_expert(tab):
                return tab.rearrange("p (t e) -> p t e", e=E)

            def by_group(tab):
                return tab.rearrange("p (q m) -> p q m", m=E // G)

            def spread(ap, m):
                return ap.rearrange("p (n o) -> p n o", o=1).to_broadcast([P, ap.shape[1], m])

            def rows(ap, r):
                return ap.rearrange("p (o m) -> p o m", o=1).to_broadcast([P, r, ap.shape[1]])

            top, total = col[:, 0, :], col[:, 1, :]
            probs, score, work, first, second = table[1], table[2], table[3], table[4], table[5]
            equal, above = table[6], table[7]
            gsum, keep = table[8][:, 0:TILES * G], table[8][:, 256:256 + TILES * G]
            pairs = region[:, 9 * TILES * E:9 * TILES * E + TILES * G * 6].rearrange("p (q m) -> p q m", m=6)
            dve.wait_ge(sem.logits_stored, BLOCKS)
            step(dve.tensor_reduce(top, logits, AX, ALU.max))
            dve.tensor_tensor(by_expert(probs), logits, spread(top, E), ALU.subtract).then_inc(sem.shifted, 1)
            dve.wait_ge(sem.exp_ready, 1)
            step(dve.tensor_reduce(total, by_expert(probs), AX, ALU.add))
            step(dve.reciprocal(total, total))
            step(dve.tensor_tensor(by_expert(probs), by_expert(probs), spread(total, E), ALU.mult))
            step(dve.tensor_tensor(by_expert(score), by_expert(probs), rows(gate_b[:], TILES), ALU.add))
            quad = by_group(score)
            dve.tensor_tensor(pairs[:, :, 0:3], quad[:, :, 0:3], quad[:, :, 1:4], ALU.add)
            dve.tensor_tensor(pairs[:, :, 3:5], quad[:, :, 0:2], quad[:, :, 2:4], ALU.add)
            step(dve.tensor_tensor(pairs[:, :, 5:6], quad[:, :, 0:1], quad[:, :, 3:4], ALU.add))
            step(dve.tensor_reduce(gsum, pairs, AX, ALU.max))
            others = gsum.rearrange("p (t o g) -> p t o g", o=1, g=G).to_broadcast([P, TILES, G, G])
            own = gsum.rearrange("p (t g o) -> p t g o", o=1, g=G).to_broadcast([P, TILES, G, G])
            square = lambda tab: tab.rearrange("p (t g h) -> p t g h", g=G, h=G)
            dve.tensor_tensor(square(above), others, own, ALU.is_gt)
            step(dve.tensor_tensor(square(equal), others, own, ALU.is_equal))
            step(dve.tensor_tensor(by_expert(equal), by_expert(equal), rows(core.lower4[:].rearrange("p g h -> p (g h)"), TILES), ALU.mult))
            step(dve.tensor_tensor(above, above, equal, ALU.add))
            step(dve.tensor_reduce(keep, above.rearrange("p (q m) -> p q m", m=G), AX, ALU.add))
            step(dve.tensor_scalar(keep, keep, float(2), None, ALU.is_lt))
            step(dve.tensor_tensor(quad, quad, spread(keep, E // G), ALU.mult))
            step(dve.tensor_scalar(keep, keep, 1.0, -LOWEST, ALU.subtract, ALU.mult))
            step(dve.tensor_tensor(quad, quad, spread(keep, E // G), ALU.add))
            for k, pick in ((0, first), (1, second)):
                step(dve.tensor_reduce(top, by_expert(score), AX, ALU.max))
                step(dve.tensor_tensor(by_expert(work), by_expert(score), spread(top, E), ALU.is_equal))
                step(dve.tensor_tensor(by_expert(work), by_expert(work), rows(core.falling[:], TILES), ALU.mult))
                step(dve.tensor_reduce(top, by_expert(work), AX, ALU.max))
                step(dve.tensor_tensor(by_expert(pick), by_expert(work), spread(top, E), ALU.is_equal))
                if k == 0:
                    step(dve.scalar_tensor_tensor(score, first, LOWEST, score, ALU.mult, ALU.add))
            dve.tensor_tensor(assigned[:], first, second, ALU.add).then_inc(sem.pairs_ready, 1)
            for k, pick in ((0, first), (1, second)):
                step(dve.tensor_tensor(work, pick, probs, ALU.mult))
                step(dve.tensor_reduce(weight[:, k, :], by_expert(work), AX, ALU.add))
            step(dve.tensor_scalar(weight[:].rearrange("p k t -> p (k t)"), weight[:].rearrange("p k t -> p (k t)"), 0.5, None, ALU.mult))
            per_tile, ahead, offset = table[11], table[12], table[13]
            expert_major = lambda tab: tab.rearrange("p (e t) -> p e t", t=TILES)
            count, tiles_of, tiles_end, shift = small[:, 0, :], small[:, 1, :], small[:, 2, :], small[:, 3, :]
            dve.wait_ge(sem.counted, 1)
            step(dve.tensor_copy(expert_major(per_tile), bank[7][:, :].rearrange("p (t e) -> p e t", e=E)))
            step(dve.tensor_reduce(count, expert_major(per_tile), AX, ALU.add))
            step(dve.tensor_tensor_scan(ahead, core.ones[:, 0:1].to_broadcast([P, TILES * E]), per_tile, 0.0, ALU.mult, ALU.add))
            step(dve.tensor_tensor(ahead, ahead, per_tile, ALU.subtract))
            step(dve.tensor_tensor(expert_major(work), spread(count, TILES), rows(core.full_tiles[:], E), ALU.is_gt))
            step(dve.tensor_reduce(tiles_of, expert_major(work), AX, ALU.add))
            step(dve.tensor_tensor_scan(tiles_end, core.ones[:, 0:1].to_broadcast([P, E]), tiles_of, 0.0, ALU.mult, ALU.add))
            step(dve.tensor_tensor(shift, tiles_end, tiles_of, ALU.subtract))
            step(dve.scalar_tensor_tensor(shift, shift, float(P), expert_major(ahead)[:, :, 0], ALU.mult, ALU.subtract))
            step(dve.tensor_tensor(offset.rearrange("p (t e) -> p e t", e=E), expert_major(ahead), spread(shift, TILES), ALU.add))
            step(dve.tensor_tensor(offset, bank[6][:, :], offset, ALU.add))
            for k, pick in ((0, first), (1, second)):
                step(dve.tensor_tensor(work, pick, offset, ALU.mult))
                step(dve.tensor_reduce(slots_f[:, k::TOPK], by_expert(work), AX, ALU.add))
            step(dve.tensor_tensor(expert_hit, tiles_end[0:1, :].rearrange("p (o e) -> p o e", o=1).to_broadcast([1, SLOT_TILES, E]),
                                   core.tile_id[0:1, :].rearrange("p (n o) -> p n o", o=1).to_broadcast([1, SLOT_TILES, E]), ALU.is_le))
            step(dve.tensor_reduce(expert_f[:], expert_hit, AX, ALU.add))
            step(dve.tensor_scalar(expert_of[:], expert_f[:], float(E - 1), None, ALU.min))
            dve.tensor_copy(slots[:].rearrange("p t k -> p (t k)"), slots_f[:]).then_inc(sem.slots_ready, 1)
            step(dve.tensor_scalar(slot_tile[:], slots_f[:], (P - 1) / 2, 1.0 / P, ALU.subtract, ALU.mult))
            step(dve.tensor_scalar(slot_tile[:], slot_tile[:], TO_WHOLE, None, ALU.add))
            step(dve.tensor_scalar(slot_tile[:], slot_tile[:], TO_WHOLE, None, ALU.subtract))
            step(dve.scalar_tensor_tensor(slot_row[:], slot_tile[:], -float(P), slots_f[:], ALU.mult, ALU.add))
            by_pair = lambda ap, m: ap.rearrange("p (q o) -> p q o", o=1).to_broadcast([P, PAIRS, m])
            per_pair = lambda ap: ap.rearrange("p (o m) -> p o m", o=1).to_broadcast([P, PAIRS, ap.shape[1]])
            dve.tensor_tensor(row_hot, per_pair(core.row_id[:]), by_pair(slot_row[:], P), ALU.is_equal)
            step(dve.tensor_tensor(tile_hot[:, :, 0, :], per_pair(core.tile_id[:]), by_pair(slot_tile[:], SLOT_TILES), ALU.is_equal))
            step(dve.tensor_tensor(tile_hot[:, :, 1, :], tile_hot[:, :, 0, :], by_pair(core.tile_of_pair[:], SLOT_TILES), ALU.mult))
            dve.tensor_scalar(tile_hot[:, :, 0, :], tile_hot[:, :, 0, :], core.part_id[:], None, ALU.mult).then_inc(sem.hot_ready, 1)
            dve.wait_ge(sem.inverted, 1)
            step(dve.tensor_scalar(token_f[:], bank[7][:, SLOT_TILES:2 * SLOT_TILES], float(P), None, ALU.mult))
            step(dve.tensor_tensor(token_f[:], token_f[:], bank[7][:, 0:SLOT_TILES], ALU.add))
            dve.tensor_copy(token_of[:], token_f[:]).then_inc(sem.tokens_ready, 1)

            dve.wait_ge(sem.experts_loaded, 16 * 6)
            dve.wait_ge(sem.slots_ready, 1)
            dve.wait_ge(sem.up_ready, 4 * BLOCKS)

            def emit(n, j, r):
                if runs(n, 0):
                    expert = dve.value_load(expert_of[0:1, bass.ds(n, 1)], min_val=0, max_val=E - 1)
                    if after(n, ROUND):
                        dve.wait_ge(sem.y_ready, n - ROUND + 1)
                    dve.tensor_copy(w_down[:, j, :], w_all[:, bass.ds(expert, 1), UP:].rearrange("p o f -> p (o f)")).then_inc(sem.down_kept, 1)
                if runs(n, 2):
                    at, m = (j - 2) % ROUND, (j - 2) % 2
                    dve.wait_ge(sem.y_done, n - 1)
                    dve.wait_ge(sem.down_kept, n - 1)
                    if after(n, ROUND + 2):
                        dve.wait_ge(row_stored[at], 16 * (r if j >= 2 else r - 1))
                    dve.tensor_tensor(y_rows[:, at, :], bank[4 + m][:, 0:D], w_down[:, at, D:], ALU.add).then_inc(sem.y_ready, 1)
                if runs(n, 1):
                    at, m = (j - 1) % ROUND, (j - 1) % 2
                    dve.wait_ge(sem.gated_ready, n)
                    if after(n, 3):
                        dve.wait_ge(sem.y_done, n - 2)
                    dve.scalar_tensor_tensor(prod_t[:, m, :], bank[2 + m][:, P:2 * P], w_up[:, at, UP - 1:UP], gated[:, m, :], ALU.add, ALU.mult
                                             ).then_inc(sem.prod_done, 1)

            expert_steps(dve, emit, 2)

            dve.wait_ge(sem.z_added, 2 * BLOCKS)
            added = [0]

            def combine(t, i):
                xt = tile(x, t)
                dve.wait_ge(fetched[added[0] % 8], 32 * (i + 1))
                dve.scalar_tensor_tensor(xt, back[:, 2 * (added[0] % 8), :], weight[:, 0, bass.ds(t, 1)], xt, ALU.mult, ALU.add
                                         ).then_inc(sem.first_added, 1)
                dve.wait_ge(sem.first_added, t + 1)
                dve.scalar_tensor_tensor(xt, back[:, 2 * (added[0] % 8) + 1, :], weight[:, 1, bass.ds(t, 1)], xt, ALU.mult, ALU.add
                                         ).then_inc(sem.combined, 1)
                added[0] += 1

            with dve.Fori(0, TILES // 8) as i:
                for j in range(8):
                    combine(i * 8 + j, i)
    give_back(nc, sem, stage_stored, row_loaded, row_stored, fetched)


def attention(nc, core, w, tag):
    q_dram = nc.dram_tensor(f"{tag}_q", (BLOCKS, GROUPS, P, BW), FP16, kind="Internal").ap()
    k_dram = nc.dram_tensor(f"{tag}_k", (BLOCKS, GROUPS, P, BW), FP16, kind="Internal").ap()
    v_dram = nc.dram_tensor(f"{tag}_v", (BLOCKS, GROUPS, BT, P, P), FP32, kind="Internal").ap()
    lines(nc, core, w, f"{tag}_lines", q_dram, k_dram, v_dram)
    attend(nc, core, w, f"{tag}_attend", q_dram, k_dram, v_dram)


def lines(nc, core, w, tag, q_dram, k_dram, v_dram):
    ctx = ExitStack()
    with ctx:
        sb = lambda name, shape, dt=FP32: ctx.enter_context(nc.sbuf_tensor(f"{tag}_{name}", shape, dt))
        x, bank = core.x, core.bank
        s = Core()
        s.parts, s.mean, s.gap = sb("parts", [P, TILES, 6]), sb("mean", [P, TILES]), sb("gap", [P, TILES])
        s.var, s.root, s.rstd = sb("var", [P, TILES]), sb("root", [P, TILES]), sb("rstd", [P, TILES])
        w_now = sb("w_now", [P, DC, 2 * D])
        w_prev = sb("w_prev", [P, DC, P])
        b_v, b_o = sb("b_v", [P, D]), sb("b_o", [P, D])
        goes_on = sb("goes_on", [P, BLOCKS])
        stage = sb("stage", [P, BT, D])
        xt = sb("xt", [P, DC, 1 + BW])
        points = sb("points", [P, 2 * BT, 2, H, 4])
        line, other = sb("line", [P, 2 * BT * H, PL]), sb("other", [P, 2 * BT * H, PL])
        size, inverse = sb("size", [P, 2 * BT * H]), sb("inverse", [P, 2 * BT * H])
        feats = sb("feats", [P, 2, BT * H, HR], FP16)
        q_out, k_out = sb("q_out", [P, GROUPS, BW], FP16), sb("k_out", [P, GROUPS, BW], FP16)
        v_out = sb("v_out", [P, BT, H, HR])
        sem = semaphores(nc, tag, "weights_loaded stat_step stats var_ready root_ready filled staged turned xt0_ready xt1_ready "
                    "projected points_ready value_ready other_ready line_step squared size_ready feats_ready "
                    "store_turn q_turned k_turned q_ready k_ready q_stored k_stored v_stored bo_added")
        block = ctx.enter_context(nc.Block())
        WEIGHTS = 16 * 9

        @block.sync
        def _(sp):
            heads = [(w["W1_q"], 0), (w["W2_q"], 64), (w["W1_k"], 128), (w["W2_k"], 192), (w["W_v"], 256)]
            for weight, at in heads:
                n = weight.shape[1]
                sp.dma_start(w_now[:, :, at:at + n], weight[0:D, :].rearrange("(c p) n -> p c n", p=P)).then_inc(sem.weights_loaded, 16)
            for weight, at in heads[0:2]:
                sp.dma_start(w_prev[:, :, at:at + 64], weight[D:2 * D, :].rearrange("(c p) n -> p c n", p=P)).then_inc(sem.weights_loaded, 16)
            sp.dma_start(b_v[:], over_partitions(w["b_v"], P, D)).then_inc(sem.weights_loaded, 16)
            sp.dma_start(b_o[:], over_partitions(w["b_o"], P, D)).then_inc(sem.weights_loaded, 16)
            with sp.Fori(0, BLOCKS) as i:
                sp.wait_ge(sem.value_ready, BT * i + BT)
                for j in range(BT):
                    sp.dma_start(v_dram[bass.ds(i, 1), :, j, :, :].rearrange("o g p n -> p (o g) n"),
                                 v_out[:, j, :, :].rearrange("p (g h) r -> p g (h r)", g=GROUPS)).then_inc(sem.v_stored, 16)
                sp.wait_ge(sem.q_ready, 2 * i + 2)
                sp.sem_inc(sem.store_turn, 1)
                sp.dma_start(q_dram[bass.ds(i, 1), :, :, :].rearrange("o g p n -> p (o g) n"), q_out[:]).then_inc(sem.q_stored, 16)
                sp.wait_ge(sem.k_ready, 2 * i + 2)
                sp.sem_inc(sem.store_turn, 1)
                sp.dma_start(k_dram[bass.ds(i, 1), :, :, :].rearrange("o g p n -> p (o g) n"), k_out[:]).then_inc(sem.k_stored, 16)
            sp.wait_ge(sem.v_stored, 16 * BT * BLOCKS)
            sp.wait_ge(sem.q_stored, 16 * BLOCKS)
            sp.wait_ge(sem.k_stored, 16 * BLOCKS)

        @block.gpsimd
        def _(pool):
            pool.memset(feats[:], 0.0)
            pool.memset(xt[:], 0.0)
            pool.memset(v_out[:], 1.0)
            pool.memset(goes_on[:], 1.0).then_inc(sem.filled, 1)
            pool.wait_ge(sem.filled, 1)
            pool.memset(goes_on[:, 0:BLOCKS:BLOCKS // BATCH], 0.0).then_inc(sem.filled, 1)
            pool.wait_ge(sem.weights_loaded, WEIGHTS)
            with pool.Fori(0, BLOCKS) as i:
                pool.wait_ge(sem.staged, i + 1)
                part = x[:, bass.ds(i * BT, BT), :]
                pool.tensor_tensor(part, part, b_o[:].rearrange("p (o d) -> p o d", o=1).to_broadcast([P, BT, D]), ALU.add
                                   ).then_inc(sem.bo_added, 1)
                pool.wait_ge(sem.points_ready, BT * i + BT)
                p1, p2 = points[:, :, 0, :, :], points[:, :, 1, :, :]
                o = other[:].rearrange("p (a h) c -> p a h c", h=H)
                spread = lambda ap, m: ap.to_broadcast([P, 2 * BT, H, m])
                pool.wait_ge(sem.squared, i + 1)
                pool.tensor_tensor(o[:, :, :, 0:3], p1[:, :, :, 1:4], spread(p2[:, :, :, 0:1], 3), ALU.mult)
                pool.tensor_tensor(o[:, :, :, 3:5], p1[:, :, :, 2:4], spread(p2[:, :, :, 1:2], 2), ALU.mult)
                pool.tensor_tensor(o[:, :, :, 5:6], p1[:, :, :, 3:4], p2[:, :, :, 2:3], ALU.mult).then_inc(sem.other_ready, 1)

        @block.tensor
        def _(pe):
            pe.wait_ge(sem.weights_loaded, WEIGHTS)
            pe.wait_ge(sem.filled, 2)

            def block_step(i):
                pe.wait_ge(sem.staged, i + 1)
                if not isinstance(i, int) or i > 0:
                    pe.wait_ge(sem.k_ready, 2 * i)
                for c in range(DC):
                    for j in range(BT):
                        last = pe.transpose(bank[c][:, j * P:(j + 1) * P], stage[:, j, c * P:(c + 1) * P], core.ident[:])
                last.then_inc(sem.turned, 1)
                pe.wait_ge(sem.xt0_ready, 2 * i + 2)
                pe.wait_ge(sem.xt1_ready, i + 1)
                for j in range(BT):
                    if not isinstance(i, int) or i > 0:
                        pe.wait_ge(sem.points_ready, BT * (i - 1) + j + 1)
                        pe.wait_ge(sem.value_ready, BT * (i - 1) + j + 1)
                    now = lambda c: xt[:, c, 1 + j * P:1 + (j + 1) * P]
                    pe.matmul(bank[2 + j], now(0), w_now[:, 0, :], start=True, stop=False)
                    for c in range(DC):
                        pe.matmul(bank[2 + j][:, 0:P], xt[:, c, j * P:(j + 1) * P], w_prev[:, c, :], start=False, stop=False)
                    pe.matmul(bank[2 + j], now(1), w_now[:, 1, :], start=False, stop=True).then_inc(sem.projected, 1)
                pe.wait_ge(sem.feats_ready, i + 1)
                for side, first, signal in ((0, 6, sem.q_turned), (1, 0, sem.k_turned)):
                    if side == 0 and (not isinstance(i, int) or i > 0):
                        pe.wait_ge(sem.q_ready, 2 * i)
                    for g in range(GROUPS):
                        turned = bank[first + g // 2].bitcast(FP16)
                        for j in range(BT):
                            at = (g % 2) * BW + j * P
                            last = pe.transpose(turned[:, at:at + P],
                                                feats[:, side, j * H + g * HG:j * H + (g + 1) * HG, :].rearrange("p h r -> p (h r)"),
                                                core.ident16[:])
                        if g % 2:
                            last.then_inc(signal, 1)

            block_step(0)
            with pe.Fori(1, BLOCKS) as i:
                block_step(i)

        @block.scalar
        def _(act):
            norm_statistics(nc, None, act, core, s, sem)
            act.wait_ge(sem.filled, 2)

            def block_step(i):
                act.wait_ge(sem.turned, i + 1)
                if not isinstance(i, int) or i > 0:
                    act.wait_ge(sem.projected, BT * i)
                act.activation(xt[:, 0, 0:1], xt[:, 0, BW:BW + 1], ACT.Copy, scale=goes_on[:, bass.ds(i, 1)]).then_inc(sem.xt0_ready, 1)
                act.wait_ge(sem.xt0_ready, 2 * i + 1)
                act.activation(xt[:, 0, 1:], bank[0], ACT.Copy).then_inc(sem.xt0_ready, 1)
                for j in range(BT):
                    act.wait_ge(sem.value_ready, BT * i + j + 1)
                    if j == 0 and (not isinstance(i, int) or i > 0):
                        act.wait_ge(sem.other_ready, i)
                        act.wait_ge(sem.squared, i + 1)
                    act.activation(points[:, j:2 * BT:BT, :, :, :].rearrange("p a b h c -> p a (b h c)"),
                                   bank[2 + j][:, 0:2 * P].rearrange("p (a n) -> p a n", a=2), ACT.Copy).then_inc(sem.points_ready, 1)
                act.wait_ge(sem.squared, i + 2)
                act.activation(size[:], size[:], ACT.Sqrt).then_inc(sem.size_ready, 1)
                for g in range(2):
                    act.wait_ge(sem.q_turned, 2 * i + g + 1)
                    if g == 0 and (not isinstance(i, int) or i > 0):
                        act.wait_ge(sem.q_stored, 16 * i)
                    act.activation(q_out[:, 2 * g:2 * g + 2, :].rearrange("p g n -> p (g n)"), bank[6 + g].bitcast(FP16), ACT.Copy
                                   ).then_inc(sem.q_ready, 1)

            block_step(0)
            with act.Fori(1, BLOCKS) as i:
                block_step(i)

        STEPS = 10

        @block.vector
        def _(dve):
            norm_statistics(nc, dve, None, core, s, sem)
            dve.wait_ge(sem.filled, 2)
            dve.wait_ge(sem.weights_loaded, WEIGHTS)
            dve.sem_inc(sem.squared, 1)

            def block_step(i):
                n = [0]

                def step(ins):
                    n[0] += 1
                    ins.then_inc(sem.line_step, 1)
                    dve.wait_ge(sem.line_step, i * STEPS + n[0])

                for j in range(BT):
                    t = i * BT + j
                    if j == 0 and (not isinstance(i, int) or i > 0):
                        dve.wait_ge(sem.turned, i)
                    last = dve.tensor_scalar(stage[:, j, :], x[:, bass.ds(t, 1), :].rearrange("p o d -> p (o d)"),
                                             s.mean[:, bass.ds(t, 1)], s.rstd[:, bass.ds(t, 1)], ALU.subtract, ALU.mult)
                last.then_inc(sem.staged, 1)
                dve.wait_ge(sem.turned, i + 1)
                if not isinstance(i, int) or i > 0:
                    dve.wait_ge(sem.projected, BT * i)
                step(dve.tensor_scalar(xt[:, 1, 0:1], xt[:, 1, BW:BW + 1], goes_on[:, bass.ds(i, 1)], None, ALU.mult))
                dve.tensor_copy(xt[:, 1, 1:], bank[1]).then_inc(sem.xt1_ready, 1)
                for j in range(BT):
                    dve.wait_ge(sem.projected, BT * i + j + 1)
                    if j == 0 and (not isinstance(i, int) or i > 0):
                        dve.wait_ge(sem.v_stored, 16 * BT * i)
                    dve.tensor_tensor(v_out[:, j, :, 0:DH], bank[2 + j][:, 2 * P:].rearrange("p (h d) -> p h d", h=H),
                                      b_v[:].rearrange("p (h d) -> p h d", h=H), ALU.add).then_inc(sem.value_ready, 1)
                dve.wait_ge(sem.points_ready, BT * i + BT)
                p1, p2 = points[:, :, 0, :, :], points[:, :, 1, :, :]
                o = line[:].rearrange("p (a h) c -> p a h c", h=H)
                spread = lambda ap, m: ap.to_broadcast([P, 2 * BT, H, m])
                dve.tensor_tensor(o[:, :, :, 0:3], spread(p1[:, :, :, 0:1], 3), p2[:, :, :, 1:4], ALU.mult)
                dve.tensor_tensor(o[:, :, :, 3:5], spread(p1[:, :, :, 1:2], 2), p2[:, :, :, 2:4], ALU.mult)
                step(dve.tensor_tensor(o[:, :, :, 5:6], p1[:, :, :, 2:3], p2[:, :, :, 3:4], ALU.mult))
                dve.wait_ge(sem.other_ready, i + 1)
                step(dve.tensor_tensor(line[:], line[:], other[:], ALU.subtract))
                step(dve.tensor_tensor(other[:], line[:], line[:], ALU.mult))
                dve.tensor_reduce(size[:], other[:], AX, ALU.add).then_inc(sem.squared, 1)
                dve.wait_ge(sem.size_ready, i + 1)
                step(dve.tensor_scalar(size[:], size[:], 1e-12, None, ALU.max))
                step(dve.reciprocal(inverse[:], size[:]))
                step(dve.tensor_tensor(line[:], line[:], inverse[:].rearrange("p (n o) -> p n o", o=1)
                                       .to_broadcast([P, 2 * BT * H, PL]), ALU.mult))
                lq, lk = line[:, 0:BT * H, :], line[:, BT * H:, :]
                step(dve.tensor_scalar(lk[:, :, 1:5:3], lk[:, :, 1:5:3], -1.0, None, ALU.mult))
                if not isinstance(i, int) or i > 0:
                    dve.wait_ge(sem.k_turned, 2 * i)
                twice = lambda ap: ap.rearrange("p n (o c) -> p n o c", o=1).to_broadcast([P, BT * H, 2, PL])
                lk = lk[:, :, ::-1]
                q_high = feats[:, 0, :, 0:2 * PL].rearrange("p n (a c) -> p n a c", a=2)
                q_low = feats[:, 0, :, 2 * PL:4 * PL].rearrange("p n (a c) -> p n a c", a=2)
                k_both = feats[:, 1, :, 0:4 * PL].rearrange("p n (a c) -> p n a c", a=2)
                k_high, k_low = k_both[:, :, :, 0:PL], k_both[:, :, :, PL:]
                step(dve.tensor_copy(q_high, twice(lq)))
                step(dve.tensor_copy(k_high, twice(lk)))
                dve.tensor_tensor(q_low, twice(lq), q_high, ALU.subtract)
                dve.tensor_tensor(k_low, twice(lk), k_high, ALU.subtract).then_inc(sem.feats_ready, 1)
                for g in range(2):
                    dve.wait_ge(sem.k_turned, 2 * i + g + 1)
                    if g == 0 and (not isinstance(i, int) or i > 0):
                        dve.wait_ge(sem.k_stored, 16 * i)
                    dve.tensor_copy(k_out[:, 2 * g:2 * g + 2, :].rearrange("p g n -> p (g n)"), bank[g].bitcast(FP16)
                                    ).then_inc(sem.k_ready, 1)
                assert n[0] == STEPS

            block_step(0)
            with dve.Fori(1, BLOCKS) as i:
                block_step(i)
    give_back(nc, sem)


def attend(nc, core, w, tag, q_dram, k_dram, v_dram):
    ctx = ExitStack()
    with ctx:
        sb = lambda name, shape, dt=FP32: ctx.enter_context(nc.sbuf_tensor(f"{tag}_{name}", shape, dt))
        x, banks = core.x, core.banks
        SLOTS, RING, LAG = 3, 4, 2
        ALL = BATCH * GROUPS
        q_now = sb("q_now", [P, HG, T], FP16)
        k_now = sb("k_now", [P, T], FP16)
        v_now = sb("v_now", [P, KT, P])
        probs = sb("probs", [P, RING, HG, QW])
        w_o = sb("w_o", [P, GROUPS, D])
        sums, below = sb("sums", [P, QW]), sb("below", [P, QW])
        heads = sb("heads", [P, 2, QW])
        score = [banks[:, 2 * n:2 * n + 2, :] for n in range(SLOTS)]
        out_bank, proj_bank = banks[:, 6, :], banks[:, 7, :]
        sem = semaphores(nc, tag, "zeroed w_loaded mask_turn shuffle_turn load_turn scores_ready exp_done masked pv_done sums_kept chain_step heads_ready "
                    "proj_done proj_added")
        q_loaded, kv_loaded = ring_semaphores(nc, f"{tag}_q_loaded", QC), ring_semaphores(nc, f"{tag}_kv_loaded", QC)
        block = ctx.enter_context(nc.Block())

        per_chunk = QW // P
        units = [(qc, kt, max(0, kt - per_chunk * qc) * P) for qc in range(QC) for kt in range(per_chunk * (qc + 1))]
        U = len(units)
        last_of = [max(u for u, v in enumerate(units) if v[0] == qc) for qc in range(QC)]
        diagonal = [u for u, (qc, kt, _) in enumerate(units) if kt >= per_chunk * qc]
        project_at = {10: (3, 0), 11: (3, 1), 12: (0, 0), 13: (0, 1), 21: (1, 0), 22: (1, 1), 33: (2, 0), 34: (2, 1)}
        turn = {3: 0, 0: 1, 1: 2, 2: 3}

        def projected_before(g, qc, half):
            return 2 * (QC * g - 1 + turn[qc]) + half

        def batch_of(g):
            return g // GROUPS

        def groups(eng, emit, end=None):
            emit(0)
            with eng.Fori(1, end or ALL) as g:
                emit(g)

        def later(g):
            return not isinstance(g, int) or g > 0

        @block.sync
        def _(sp):
            sp.wait_ge(sem.zeroed, 1)
            for j in range(HG):
                sp.dma_start(w_o[j * HR:j * HR + DH, :, :], w["W_o"].rearrange("(g j d) n -> j d g n", j=HG, d=DH)[j]
                             ).then_inc(sem.w_loaded, 16)

            def load_q(g, m):
                i, gr = batch_of(g) * QC + m, g % GROUPS
                for j in range(HG):
                    rows = slice(j * HR, (j + 1) * HR)
                    sp.dma_start(q_now[rows, j, m * QW:(m + 1) * QW],
                                 q_dram[bass.ds(i, 1), bass.ds(gr, 1), rows, :].rearrange("o g p n -> p (o g n)")).then_inc(q_loaded[m], 16)

            def load_kv(g, m):
                i, gr = batch_of(g) * QC + m, g % GROUPS
                sp.dma_start(k_now[:, m * QW:(m + 1) * QW],
                             k_dram[bass.ds(i, 1), bass.ds(gr, 1), :, :].rearrange("o g p n -> p (o g n)")).then_inc(kv_loaded[m], 16)
                sp.dma_start(v_now[:, m * BT:(m + 1) * BT, :],
                             v_dram[bass.ds(i, 1), bass.ds(gr, 1), :, :, :].rearrange("o g t p n -> p (o g t) n")).then_inc(kv_loaded[m], 16)

            for m in range(QC):
                load_q(0, m)
                load_kv(0, m)
            with sp.Fori(0, ALL - 1) as g:
                for m in range(QC - 1):
                    sp.wait_ge(sem.scores_ready, 2 * (U * g + last_of[m] + 1))
                    sp.sem_inc(sem.load_turn, 1)
                    load_q(g + 1, m)
                for m in range(QC):
                    sp.wait_ge(sem.pv_done, U * g + last_of[QC - 2] + 1 + (m + 1) * BT)
                    sp.sem_inc(sem.load_turn, 1)
                    load_kv(g + 1, m)
                load_q(g + 1, QC - 1)

        @block.tensor
        def _(pe):
            def half_scores(g, u, half):
                qc, kt, c0 = units[u]
                hu = 2 * u + half
                if u == 0 or units[u - 1][0] != qc:
                    if half == 0:
                        pe.wait_ge(q_loaded[qc], 16 * HG * (g + 1))
                        pe.wait_ge(kv_loaded[qc], 32 * (g + 1))
                older = hu - SLOTS if hu >= SLOTS else max(h for h in range(-SLOTS, 0) if (h + 2 * U) % SLOTS == hu % SLOTS)
                if later(g) or older >= 0:
                    pe.wait_ge(sem.exp_done, 2 * U * g + older + 1)
                for j in range(2):
                    h = 2 * half + j
                    last = pe.matmul(score[hu % SLOTS][:, j, c0:QW], k_now[:, kt * P:(kt + 1) * P],
                                     q_now[:, h, qc * QW + c0:(qc + 1) * QW], start=True, stop=True)
                last.then_inc(sem.scores_ready, 1)

            def weigh(g, u):
                qc, kt, c0 = units[u]
                pe.wait_ge(sem.exp_done, 2 * (U * g + u + 1))
                if u in diagonal:
                    pe.wait_ge(sem.masked, len(diagonal) * g + diagonal.index(u) + 1)
                if kt == 0 and (later(g) or qc > 0):
                    pe.wait_ge(sem.sums_kept, QC * g + qc)
                for h in range(HG):
                    rows = slice(h * HR, (h + 1) * HR)
                    last = pe.matmul(out_bank[rows, c0:QW], v_now[:, kt, rows], probs[:, u % RING, h, c0:QW],
                                     start=(kt == 0), stop=(u == last_of[qc]))
                last.then_inc(sem.pv_done, 1)

            def project(g, qc, half):
                mine = g - 1 if qc == QC - 1 else g
                pe.wait_ge(sem.heads_ready, QC * mine + qc + 1)
                before = projected_before(g, qc, half)
                if later(before):
                    pe.wait_ge(sem.proj_added, before)
                for j in range(2):
                    at = (2 * half + j) * P
                    last = pe.matmul(proj_bank[:, j * D:(j + 1) * D], heads[:, qc % 2, at:at + P],
                                     w_o[:, bass.ds(mine % GROUPS, 1), :].rearrange("p o d -> p (o d)"), start=True, stop=True)
                last.then_inc(sem.proj_done, 1)

            def step(g, u):
                half_scores(g, u, 0)
                half_scores(g, u, 1)
                if u >= LAG:
                    weigh(g, u - LAG)
                elif later(g):
                    weigh(g - 1, U + u - LAG)
                if u in project_at:
                    qc, half = project_at[u]
                    if qc < QC - 1 or later(g):
                        project(g, qc, half)

            def group(g):
                for u in range(U):
                    step(g, u)

            pe.wait_ge(sem.w_loaded, 16 * HG)
            groups(pe, group)
            for u in range(U - LAG, U):
                weigh(ALL - 1, u)
            for half in range(2):
                project(ALL, QC - 1, half)

        @block.scalar
        def _(act):
            def group(g):
                for u, (qc, kt, c0) in enumerate(units):
                    for half in range(2):
                        hu = 2 * u + half
                        act.wait_ge(sem.scores_ready, 2 * U * g + hu + 1)
                        if half == 0 and (later(g) or u >= RING):
                            act.wait_ge(sem.pv_done, U * g + u - RING + 1)
                        act.activation(probs[:, u % RING, 2 * half:2 * half + 2, c0:QW], score[hu % SLOTS][:, :, c0:QW], ACT.Exp,
                                       scale=SCALE).then_inc(sem.exp_done, 1)

            groups(act, group)

        @block.gpsimd
        def _(pool):
            pool.memset(q_now[:], 0.0)
            pool.memset(w_o[:], 0.0).then_inc(sem.zeroed, 1)

            def group(g):
                for u in diagonal:
                    c0 = units[u][2]
                    pool.wait_ge(sem.exp_done, 2 * (U * g + u + 1))
                    pool.sem_inc(sem.mask_turn, 1)
                    part = probs[:, u % RING, :, c0:c0 + P]
                    pool.affine_select(out=part, in_=part, compare_op=ALU.is_ge, fill=0.0, base=0,
                                       pattern=[[0, HG], [1, P]], channel_multiplier=-1).then_inc(sem.masked, 1)

            groups(pool, group)

        @block.vector
        def _(dve):
            def chunk(g, qc):
                dve.wait_ge(sem.pv_done, U * g + last_of[qc] + 1)
                if later(g) or qc > 0:
                    dve.wait_ge(sem.heads_ready, QC * g + qc)
                dve.tensor_copy(sums[:], out_bank).then_inc(sem.sums_kept, 1)
                dve.wait_ge(sem.sums_kept, QC * g + qc + 1)
                dve.sem_inc(sem.shuffle_turn, 1)
                dve.stream_shuffle(below[:], sums[:], [DH] * HR).then_inc(sem.chain_step, 1)
                dve.wait_ge(sem.chain_step, 2 * (QC * g + qc) + 1)
                dve.reciprocal(below[:], below[:]).then_inc(sem.chain_step, 1)
                dve.wait_ge(sem.chain_step, 2 * (QC * g + qc) + 2)
                dve.tensor_tensor(heads[:, qc % 2, :], sums[:], below[:], ALU.mult).then_inc(sem.heads_ready, 1)

            def add(g, qc):
                mine = g - 1 if qc == QC - 1 else g
                for half in range(2):
                    dve.wait_ge(sem.proj_done, projected_before(g, qc, half) + 1)
                    t = batch_of(mine) * KT + qc * BT + 2 * half
                    pair = x[:, bass.ds(t, 2), :].rearrange("p n d -> p (n d)")
                    dve.tensor_tensor(pair, proj_bank, pair, ALU.add).then_inc(sem.proj_added, 1)

            def group(g):
                chunk(g, 0)
                if later(g):
                    add(g, QC - 1)
                add(g, 0)
                for qc in range(1, QC - 1):
                    chunk(g, qc)
                    add(g, qc)
                chunk(g, QC - 1)

            groups(dve, group)
            add(ALL, QC - 1)
    give_back(nc, sem, q_loaded, kv_loaded)


FFN_NAMES = "gate_w gate_b We1 be1 We2 be2 We3 be3 ws1 bs1 ws2 bs2 ws3 bs3"
ATTN_NAMES = "W1_q W2_q W1_k W2_k W_v b_v W_o b_o"


def macaron(nc, d, out):
    w = {n: d[f"L0_ffn_{n}"] for n in FFN_NAMES.split()}
    a = {n: d[f"L0_attn_{n}"] for n in ATTN_NAMES.split()}
    xn_rows = nc.dram_tensor("xn_rows", (BATCH * T, D), FP32, kind="Internal").ap()
    y_slots = nc.dram_tensor("y_slots", (SLOT_TILES * P, D), FP32, kind="Internal").ap()
    core = Core()
    with ExitStack() as ctx:
        x_loaded = setup(nc, core, d["L0_attn_x"], ctx)
        ffn(nc, core, w, xn_rows, y_slots, "f1", x_loaded=x_loaded)
        attention(nc, core, a, "attn")
        ffn(nc, core, w, xn_rows, y_slots, "f2", out=out)


def kernel(**inputs):
    import numpy as np
    import concourse.bacc as bacc
    from concourse.bass_utils import run_bass_kernel_spmd

    nc = bacc.Bacc("TRN2", target_bir_lowering=False, num_devices=1)
    arrays, d = {}, {}
    for name, value in inputs.items():
        a = np.ascontiguousarray(value)
        arrays[name] = a
        d[name] = nc.dram_tensor(name, a.shape, mybir.dt.from_np(a.dtype), kind="ExternalInput").ap()
    out = nc.dram_tensor("out", (BATCH, T, D), FP32, kind="ExternalOutput").ap()
    macaron(nc, d, out)
    return run_bass_kernel_spmd(nc, [arrays], core_ids=[0]).results[0]["out"]
```

```python
from collections import namedtuple
from contextlib import ExitStack

import concourse.bass as bass
from concourse import mybir

FP32 = mybir.dt.float32
FP16 = mybir.dt.float16
BF16 = mybir.dt.bfloat16
I32 = mybir.dt.int32
ALU = mybir.AluOpType
ACT = mybir.ActivationFunctionType
AX = mybir.AxisListType.X

P = 128
BATCH, T, D = 2, 2048, 256
DC = D // P
TILES = BATCH * T // P
BT = 4
BLOCKS = TILES // BT
BW = BT * P
EPS = 1e-5

E, G, TOPK, INTER = 16, 4, 2, 128
SHARED = 2 * INTER
ROUND = 4
SLOT_TILES = -(-((TOPK * TILES * P + E * (P - 1)) // P) // (2 * ROUND)) * 2 * ROUND
TO_WHOLE = 1.5 * 2.0 ** 23
LOWEST = -3.0e38

H, PL = 16, 6
DH = D // H
HG = 4
GROUPS = H // HG
HR = P // HG
QW = 512
QC = T // QW
KT = T // P
SCALE = 6.0 ** -0.5


def dma_rows(ap):
    return ap.rearrange("(n p) d -> p n d", p=P)


def over_partitions(ap, n, *shape):
    flat = ap.rearrange("(o n) -> o n", o=1) if len(ap.shape) == 1 else ap.rearrange("(o e) i -> o e i", o=1)
    return flat.to_broadcast([n, *shape])


class Core:
    pass


def setup(nc, core, x_dram, ctx):
    sb = lambda name, shape, dt=FP32: ctx.enter_context(nc.sbuf_tensor(name, shape, dt))
    core.x = sb("x_res", [P, TILES, D])
    core.parts = sb("parts", [P, TILES, 6])
    core.ident = sb("ident", [P, P])
    core.ident16 = sb("ident16", [P, P], FP16)
    core.before = sb("before", [P, P], BF16)
    core.ones = sb("ones", [P, P], BF16)
    core.falling = sb("falling", [P, E])
    core.zero, core.one = sb("zero", [P, 1]), sb("one", [P, 1])
    core.lower4 = sb("lower4", [P, G, G])
    core.full_tiles = sb("full_tiles", [P, TILES])
    core.tile_id = sb("tile_id", [P, SLOT_TILES])
    core.tile_id16 = sb("tile_id16", [P, SLOT_TILES], BF16)
    core.row_id = sb("row_id", [P, P], BF16)
    core.part_id = sb("part_id", [P, 1])
    core.tile_of_pair = sb("tile_of_pair", [P, TILES * TOPK], BF16)
    core.slots = sb("slots", [P, TILES, TOPK], I32)
    core.weight = sb("weight", [P, TOPK, TILES])
    core.banks = ctx.enter_context(nc.psum_tensor("banks", [P, 8, 512], FP32))
    core.bank = [core.banks[:, i, :] for i in range(8)]
    x_loaded = ring_semaphores(nc, "x_loaded", BLOCKS)
    with nc.Block() as block:
        filled = nc.alloc_semaphore(name="filled")

        @block.sync
        def _(sp):
            rows = dma_rows(x_dram.rearrange("b t d -> (b t) d"))
            for b in range(BLOCKS):
                sp.dma_start(core.x[:, b * BT:(b + 1) * BT, :], rows[:, b * BT:(b + 1) * BT, :]).then_inc(x_loaded[b], 16)

        @block.gpsimd
        def _(pool):
            pool.memset(core.ident[:], 0.0)
            pool.memset(core.ident16[:], 0.0)
            pool.memset(core.before[:], 1.0)
            pool.memset(core.ones[:], 1.0)
            pool.memset(core.zero[:], 0.0)
            pool.memset(core.one[:], 1.0)
            pool.memset(core.lower4[:], 1.0).then_inc(filled, 1)
            pool.iota(core.falling[:], [[-1, E]], base=E, channel_multiplier=0, allow_small_or_imprecise_dtypes=True)
            pool.iota(core.full_tiles[:], [[P, TILES]], base=0, channel_multiplier=0, allow_small_or_imprecise_dtypes=True)
            pool.iota(core.row_id[:], [[1, P]], base=0, channel_multiplier=0, allow_small_or_imprecise_dtypes=True)
            pool.iota(core.tile_id16[:], [[1, SLOT_TILES]], base=0, channel_multiplier=0, allow_small_or_imprecise_dtypes=True)
            pool.iota(core.part_id[:], [[0, 1]], base=0, channel_multiplier=1, allow_small_or_imprecise_dtypes=True)
            pool.iota(core.tile_of_pair[:], [[1, TILES], [0, TOPK]], base=0, channel_multiplier=0, allow_small_or_imprecise_dtypes=True)
            pool.iota(core.tile_id[:], [[1, SLOT_TILES]], base=0, channel_multiplier=0, allow_small_or_imprecise_dtypes=True)
            pool.wait_ge(filled, 1)
            for eye in (core.ident, core.ident16):
                pool.affine_select(out=eye[:], in_=eye[:], compare_op=ALU.not_equal, fill=1.0, base=0,
                                   pattern=[[-1, P]], channel_multiplier=1)
            pool.affine_select(out=core.before[:], in_=core.before[:], compare_op=ALU.is_gt, fill=0.0, base=0,
                               pattern=[[1, P]], channel_multiplier=-1)
            pool.affine_select(out=core.lower4[:], in_=core.lower4[:], compare_op=ALU.is_gt, fill=0.0, base=0,
                               pattern=[[1, G], [-1, G]], channel_multiplier=0)
    return x_loaded


def bn_stats(dve, core, i):
    for j in range(BT):
        t = bass.ds(i * BT + j, 1)
        last = dve.bn_stats(core.parts[:, t, :], core.x[:, t, :].rearrange("p o d -> p (o d)"))
    return last


def norm_statistics(nc, dve, act, core, s, sem, x_loaded=None):
    if dve is not None:
        n = [0]

        def step(ins):
            n[0] += 1
            ins.then_inc(sem.stat_step, 1)
            dve.wait_ge(sem.stat_step, n[0])

        if x_loaded is not None:
            for i in range(BLOCKS):
                dve.wait_ge(x_loaded[i], 16)
                bn_stats(dve, core, i).then_inc(sem.stats, 1)
            dve.wait_ge(sem.stats, BLOCKS)
        mean_even, m2_even = core.parts[:, :, 1], core.parts[:, :, 2]
        mean_odd, m2_odd = core.parts[:, :, 4], core.parts[:, :, 5]
        step(dve.tensor_tensor(s.mean[:], mean_even, mean_odd, ALU.add))
        step(dve.tensor_scalar(s.mean[:], s.mean[:], 0.5, None, ALU.mult))
        step(dve.tensor_tensor(s.gap[:], mean_even, mean_odd, ALU.subtract))
        step(dve.tensor_tensor(s.gap[:], s.gap[:], s.gap[:], ALU.mult))
        step(dve.tensor_tensor(s.var[:], m2_even, m2_odd, ALU.add))
        step(dve.tensor_scalar(s.var[:], s.var[:], 1.0 / D, EPS, ALU.mult, ALU.add))
        dve.scalar_tensor_tensor(s.var[:], s.gap[:], 0.25, s.var[:], ALU.mult, ALU.add).then_inc(sem.var_ready, 1)
        dve.wait_ge(sem.root_ready, 1)
        step(dve.reciprocal(s.rstd[:], s.root[:]))
    if act is not None:
        act.wait_ge(sem.var_ready, 1)
        act.activation(s.root[:], s.var[:], ACT.Sqrt).then_inc(sem.root_ready, 1)


class Statistics:

    STEPS = 3

    def __init__(self, x, sb, sem):
        self.x, self.sem = x, sem
        self.parts, self.mean, self.gap = sb("parts", [P, 2, BT, 6]), sb("mean", [P, 2, BT]), sb("gap", [P, 2, BT])
        self.var, self.root, self.rstd = sb("var", [P, 2, BT]), sb("root", [P, 2, BT]), sb("rstd", [P, 2, BT])
        self.shift = sb("shift", [P, 2, BT])

    def tile(self, t):
        return self.x[:, bass.ds(t, 1), :].rearrange("p o d -> p (o d)")

    def sum_up(self, dve, n, q):
        sem, done = self.sem, [0]

        def step(ins):
            done[0] += 1
            ins.then_inc(sem.stat_step, 1)
            dve.wait_ge(sem.stat_step, n * self.STEPS + done[0])

        parts, mean, gap, var = self.parts[:, q], self.mean[:, q], self.gap[:, q], self.var[:, q]
        if after(n, 2):
            dve.wait_ge(sem.staged, n - 1)
            dve.sem_inc(sem.stat_turn, 1)
        for j in range(BT):
            last = dve.bn_stats(parts[:, j, :], self.tile(n * BT + j))
        step(last)
        dve.tensor_tensor(mean, parts[:, :, 1], parts[:, :, 4], ALU.add)
        dve.tensor_tensor(gap, parts[:, :, 1], parts[:, :, 4], ALU.subtract)
        step(dve.tensor_tensor(var, parts[:, :, 2], parts[:, :, 5], ALU.add))
        dve.tensor_scalar(mean, mean, 0.5, None, ALU.mult)
        dve.tensor_tensor(gap, gap, gap, ALU.mult)
        step(dve.tensor_scalar(var, var, 1.0 / D, EPS, ALU.mult, ALU.add))
        dve.scalar_tensor_tensor(var, gap, 0.25, var, ALU.mult, ALU.add).then_inc(sem.var_ready, 1)

    def take_root(self, act, n, q):
        act.wait_ge(self.sem.var_ready, n + 1)
        act.activation(self.root[:, q], self.var[:, q], ACT.Sqrt).then_inc(self.sem.root_ready, 1)

    def invert(self, dve, n, q):
        sem = self.sem
        dve.wait_ge(sem.root_ready, n + 1)
        dve.reciprocal(self.rstd[:, q], self.root[:, q]).then_inc(sem.inverse_ready, 1)
        dve.wait_ge(sem.inverse_ready, n + 1)
        dve.scalar_tensor_tensor(self.shift[:, q], self.mean[:, q], -1.0, self.rstd[:, q], ALU.mult, ALU.mult).then_inc(sem.rstd_ready, 1)

    def normalize(self, act, n, q, stage):
        act.wait_ge(self.sem.rstd_ready, n + 1)
        for j in range(BT):
            last = act.activation(stage[:, j, :], self.tile(n * BT + j), ACT.Identity, scale=self.rstd[:, q, j:j + 1], bias=self.shift[:, q, j:j + 1])
        last.then_inc(self.sem.staged, 1)


def semaphores(nc, tag, names):
    names = names.split()
    return namedtuple("Semaphores", names)(*[nc.alloc_semaphore(name=f"{tag}_{name}") for name in names])


def ring_semaphores(nc, name, n):
    return [nc.alloc_semaphore(name=f"{name}{k}") for k in range(n)]


def give_back(nc, *kinds):
    nc.clear_and_free_semaphores([one for kind in kinds for one in kind])
    nc.all_engine_barrier()


def block_steps(eng, emit, lag):
    for n in range(4):
        emit(n, n % 2, n // 2)
    with eng.Fori(2, BLOCKS // 2) as i:
        for q in range(2):
            emit(i * 2 + q, q, i)
    for n in range(BLOCKS, BLOCKS + lag):
        emit(n, n % 2, n // 2)


def has_block(n, lag):
    return not isinstance(n, int) or 0 <= n - lag < BLOCKS


def after(n, first):
    return not isinstance(n, int) or n >= first


def ffn(nc, core, w, xn_rows, y_slots, tag, x_loaded=None, out=None):
    ctx = ExitStack()
    with ctx:
        sb = lambda name, shape, dt=FP32: ctx.enter_context(nc.sbuf_tensor(f"{tag}_{name}", shape, dt))
        x, bank = core.x, core.bank
        s = Core()
        s.mean, s.gap = sb("mean", [P, TILES]), sb("gap", [P, TILES])
        s.var, s.root, s.rstd = sb("var", [P, TILES]), sb("root", [P, TILES]), sb("rstd", [P, TILES])
        stage = sb("stage", [P, 2, BT, D])
        UP = DC * 2 * INTER + 2
        w_all = sb("w_all", [P, E, UP + 2 * D])
        ws13 = sb("ws13", [P, DC, 2 * SHARED])
        ws2 = sb("ws2", [P, SHARED // P, D])
        bs = sb("bs", [P, 2 * SHARED // P])
        bs2 = sb("bs2", [P, D])
        gate_t = sb("gate_t", [P, DC, E])
        gate_b = sb("gate_b", [P, E])
        PAIRS = TILES * TOPK
        region = sb("region", [P, PAIRS * (P + 2 * SLOT_TILES) // 2])
        table = [region[:, n * TILES * E:(n + 1) * TILES * E] for n in range(16)]
        gate_rows, bs_rows, be_rows = table[15][0:E, 0:D], table[15][0:2 * SHARED // P, D:D + P], table[15][0:2 * E, D + P:D + 2 * P]
        row_hot = region[:, 0:PAIRS * P // 2].bitcast(BF16).rearrange("p (q s) -> p q s", q=PAIRS)
        tile_hot = region[:, PAIRS * P // 2:].bitcast(BF16).rearrange("p (q a s) -> p q a s", q=PAIRS, a=2)
        back = region[:, 0:16 * D].rearrange("p (n d) -> p n d", d=D)
        rows_in = region[:, 16 * D:(16 + ROUND) * D].rearrange("p (n d) -> p n d", d=D)
        xnt = sb("xnt", [P, DC, TILES * P])
        rings = xnt[:, :, :].rearrange("p c n -> p (c n)")
        taken = [0]

        def ring(n, width):
            at = taken[0]
            taken[0] += n * width
            return rings[:, at:at + n * width].rearrange("p (n w) -> p n w", n=n)

        w_up, w_down = ring(ROUND, UP), ring(ROUND, 2 * D)
        rows_t, gated, prod_t, y_rows = ring(2, D), ring(2, P), ring(ROUND, P), ring(ROUND, D)
        s_silu, s_lin = sb("s_silu", [P, 2, BW]), sb("s_lin", [P, 2, BW])
        s_prod = stage[:, 0, :, :].rearrange("p t d -> p (t d)").rearrange("p (c n) -> p c n", c=2)
        logits_t = s_silu[0:E, 0, :]
        z_half = sb("z_half", [P, 2, 2 * D])
        slots_f = sb("slots_f", [P, PAIRS])
        slot_tile = sb("slot_tile", [P, PAIRS])
        row_of, tile_of = sb("row_of", [P, PAIRS], BF16), sb("tile_of", [P, PAIRS], BF16)
        token_of = sb("token_of", [P, SLOT_TILES], I32)
        token_f = sb("token_f", [P, SLOT_TILES])
        slots, weight = core.slots, core.weight
        small = sb("small", [P, 4, E])
        col = sb("col", [P, 2, TILES])
        expert_of = sb("expert_of", [1, SLOT_TILES], I32)
        expert_f = sb("expert_f", [1, SLOT_TILES])
        assigned = sb("assigned", [P, TILES * E], BF16)
        expert_hit = sb("expert_hit", [1, SLOT_TILES, E], BF16)

        sem = semaphores(nc, tag, "half_ready gate_loaded shared_loaded experts_loaded "
                         "stat_step stats var_ready root_ready gate_turned gate_ready staged turned "
                         "xnt0_ready xnt1_ready logits_ready logits_kept logits_turned logits_stored "
                         "route_step shifted exp_ready pairs_ready counted slots_ready hot_ready inverted tokens_ready "
                         "up_ready silu_ready lin_ready prod_ready down_ready z_ready z_added bs2_added "
                         "rows_turned rows_kept up_kept down_kept up_done gated_ready prod_done "
                         "y_done y_ready first_added combined out_stored")
        stage_stored = ring_semaphores(nc, f"{tag}_stage_stored", 2)
        row_loaded = ring_semaphores(nc, f"{tag}_row_loaded", ROUND)
        row_stored = ring_semaphores(nc, f"{tag}_row_stored", ROUND)
        fetched = ring_semaphores(nc, f"{tag}_fetched", 8)

        def tile(buf, t):
            return buf[:, bass.ds(t, 1), :].rearrange("p o d -> p (o d)")

        block = ctx.enter_context(nc.Block())

        def expert_steps(eng, emit, lag):
            for n in range(2 * ROUND):
                emit(n, n % ROUND, n // ROUND)
            with eng.Fori(1, SLOT_TILES // (2 * ROUND)) as i:
                for j in range(2 * ROUND):
                    emit(i * (2 * ROUND) + j, j % ROUND, i * 2 + j // ROUND)
            for n in range(SLOT_TILES, SLOT_TILES + lag):
                emit(n, n % ROUND, n // ROUND)

        def runs(n, lag):
            return not isinstance(n, int) or 0 <= n - lag < SLOT_TILES

        @block.sync
        def _(sp):
            sp.dma_start(gate_rows, w["gate_w"]).then_inc(sem.gate_loaded, 16)
            for n, name in enumerate(("bs1", "bs3")):
                sp.dma_start(bs_rows[2 * n:2 * n + 2, :], w[name].rearrange("(c p) -> c p", p=P)).then_inc(sem.gate_loaded, 16)
            for n, name in enumerate(("be1", "be3")):
                sp.dma_start(be_rows[n * E:(n + 1) * E, :], w[name]).then_inc(sem.gate_loaded, 16)
            sp.dma_start(gate_b[:], over_partitions(w["gate_b"], P, E)).then_inc(sem.gate_loaded, 16)
            sp.dma_start(bs2[:], over_partitions(w["bs2"], P, D)).then_inc(sem.gate_loaded, 16)
            sp.dma_start(ws13[:, :, 0:SHARED], w["ws1"].rearrange("(c p) f -> p c f", p=P)).then_inc(sem.shared_loaded, 16)
            sp.dma_start(ws13[:, :, SHARED:], w["ws3"].rearrange("(c p) f -> p c f", p=P)).then_inc(sem.shared_loaded, 16)
            sp.dma_start(ws2[:], w["ws2"].rearrange("(c p) d -> p c d", p=P)).then_inc(sem.shared_loaded, 16)

            def store_block(n, q, r):
                sp.wait_ge(sem.staged, n + 1)
                sp.dma_start(dma_rows(xn_rows)[:, bass.ds(n * BT, BT), :], stage[:, q, :, :]).then_inc(stage_stored[q], 16)

            block_steps(sp, store_block, 0)
            for c in range(DC):
                sp.dma_start(w_all[:, :, 2 * c * INTER:(2 * c + 1) * INTER], w["We1"][:, c * P:(c + 1) * P, :].rearrange("e p i -> p e i")
                             ).then_inc(sem.experts_loaded, 16)
                sp.dma_start(w_all[:, :, (2 * c + 1) * INTER:(2 * c + 2) * INTER], w["We3"][:, c * P:(c + 1) * P, :].rearrange("e p i -> p e i")
                             ).then_inc(sem.experts_loaded, 16)
            sp.dma_start(w_all[:, :, UP:UP + D], w["We2"].rearrange("e i d -> i e d")).then_inc(sem.experts_loaded, 16)
            sp.dma_start(w_all[:, :, UP + D:], over_partitions(w["be2"], P, E, D)).then_inc(sem.experts_loaded, 16)

            def store_rows(n, j, r):
                sp.wait_ge(sem.y_ready, n + 1)
                sp.dma_start(y_slots[bass.ds(n * P, P), :], y_rows[:, j, :]).then_inc(row_stored[j], 16)

            expert_steps(sp, store_rows, 0)
            for stored in row_stored:
                sp.wait_ge(stored, 16 * (SLOT_TILES // ROUND))
            if out is not None:
                rows = dma_rows(out.rearrange("b t d -> (b t) d"))
                for g in range(TILES // 8):
                    sp.wait_ge(sem.combined, 8 * (g + 1))
                    sp.dma_start(rows[:, g * 8:(g + 1) * 8, :], x[:, g * 8:(g + 1) * 8, :]).then_inc(sem.out_stored, 16)
                sp.wait_ge(sem.out_stored, 16 * (TILES // 8))

        TO_TOKENS = 3

        @block.tensor
        def _(pe):
            def gate_weights():
                pe.wait_ge(sem.gate_loaded, 16 * 7)
                for c in range(DC):
                    pe.transpose(bank[2][:, c * E:(c + 1) * E], gate_rows[:, c * P:(c + 1) * P], core.ident[0:E, 0:E])
                pe.transpose(bank[2][:, 2 * E:2 * E + 4], bs_rows, core.ident[0:4, 0:4])
                pe.transpose(bank[2][:, 2 * E + 4:4 * E + 4], be_rows, core.ident[0:2 * E, 0:2 * E]).then_inc(sem.gate_turned, 1)

            def gate_step(n, q, r):
                if has_block(n, 0):
                    pe.wait_ge(sem.staged, n + 1)
                    if after(n, 1):
                        pe.wait_ge(sem.xnt0_ready, n)
                        pe.wait_ge(sem.xnt1_ready, n)
                    for c in range(DC):
                        for j in range(BT):
                            last = pe.transpose(bank[c][:, j * P:(j + 1) * P], stage[:, q, j, c * P:(c + 1) * P], core.ident[:])
                    last.then_inc(sem.turned, 1)
                if isinstance(n, int) and n == 0:
                    gate_weights()
                if has_block(n, 1):
                    if isinstance(n, int) and n == 1:
                        pe.wait_ge(sem.gate_ready, 1)
                    pe.wait_ge(sem.xnt0_ready, n)
                    pe.wait_ge(sem.xnt1_ready, n)
                    if after(n, 2):
                        pe.wait_ge(sem.logits_kept, n - 1)
                    for c in range(DC):
                        last = pe.matmul(bank[2][0:E, :], gate_t[:, c, :], xnt[:, c, bass.ds((n - 1) * BW, BW)],
                                         start=(c == 0), stop=(c == DC - 1))
                    last.then_inc(sem.logits_ready, 1)
                if has_block(n, 2):
                    pe.wait_ge(sem.logits_kept, n - 1)
                    if after(n, 3):
                        pe.wait_ge(sem.logits_stored, n - 2)
                    for j in range(BT):
                        last = pe.matmul(bank[3][:, j * E:(j + 1) * E], logits_t[:, j * P:(j + 1) * P], core.ident[0:E, 0:E], start=True, stop=True)
                    last.then_inc(sem.logits_turned, 1)

            block_steps(pe, gate_step, 2)

            def shared_down(i):
                pe.wait_ge(sem.prod_ready, i + 1)
                for j in range(BT):
                    if j % 2 == 0 and after(i, 1):
                        pe.wait_ge(sem.z_ready, 2 * (i - 1) + j // 2 + 1)
                    for c in range(SHARED // P):
                        last = pe.matmul(bank[4 + j // 2][:, j % 2 * D:(j % 2 + 1) * D], s_prod[:, c, j * P:(j + 1) * P],
                                         ws2[:, c, :], start=(c == 0), stop=(c == SHARED // P - 1))
                    if j % 2:
                        last.then_inc(sem.down_ready, 1)

            def shared_up(i):
                for f in range(4):
                    if after(i, 1):
                        if f < 2:
                            pe.wait_ge(sem.silu_ready, 2 * (i - 1) + f + 1)
                        else:
                            pe.wait_ge(sem.lin_ready, 2 * (i - 1) + f - 1)
                    for c in range(DC):
                        last = pe.matmul(bank[f][:, :], ws13[:, c, f * P:(f + 1) * P], xnt[:, c, bass.ds(i * BW, BW)],
                                         start=(c == 0), stop=(c == DC - 1))
                    last.then_inc(sem.up_ready, 1)

            def shared_pairs(first, end):
                with pe.Fori(first, end) as k:
                    for q in range(2):
                        shared_up(k * 2 + q)
                        shared_down(k * 2 + q - 1)

            pe.wait_ge(sem.shared_loaded, 48)
            pe.wait_ge(sem.logits_stored, BLOCKS)
            shared_up(0)
            shared_up(1)
            shared_down(0)
            pe.wait_ge(sem.pairs_ready, 1)
            pe.matmul(bank[6][:, :], core.before[:], assigned[:], start=True, stop=True)
            pe.matmul(bank[7][:, :], core.ones[:], assigned[:], start=True, stop=True).then_inc(sem.counted, 1)
            shared_pairs(1, TO_TOKENS)
            pe.wait_ge(sem.hot_ready, 1)
            for q in range(PAIRS):
                last = pe.matmul(bank[7][:, 0:2 * SLOT_TILES], row_hot[:, q, :], tile_hot[:, q, :, :].rearrange("p a s -> p (a s)"),
                                 start=(q == 0), stop=(q == PAIRS - 1))
            last.then_inc(sem.inverted, 1)
            shared_pairs(TO_TOKENS, BLOCKS // 2)
            shared_down(BLOCKS - 1)

            pe.wait_ge(sem.lin_ready, 2 * BLOCKS)
            pe.wait_ge(sem.z_ready, 2 * BLOCKS)

            def emit(n, j, r):
                if runs(n, 0):
                    pe.wait_ge(row_loaded[j], 16 * r + 16)
                    if after(n, 2):
                        pe.wait_ge(sem.rows_kept, n - 1)
                    for c in range(DC):
                        last = pe.transpose(bank[j % 2][:, c * P:(c + 1) * P], rows_in[:, j, c * P:(c + 1) * P], core.ident[:])
                    last.then_inc(sem.rows_turned, 1)
                if runs(n, 1):
                    at, m = (j - 1) % ROUND, (j - 1) % 2
                    pe.wait_ge(sem.up_kept, n)
                    pe.wait_ge(sem.rows_kept, n)
                    if after(n, 3):
                        pe.wait_ge(sem.prod_done, n - 2)
                    for f in range(2):
                        for c in range(DC):
                            col_at = (2 * c + f) * INTER
                            last = pe.matmul(bank[2 + m][:, f * P:(f + 1) * P], w_up[:, at, col_at:col_at + INTER],
                                             rows_t[:, m, c * P:(c + 1) * P], start=(c == 0), stop=(c == DC - 1))
                    last.then_inc(sem.up_done, 1)
                if runs(n, 3):
                    at, m = (j - 3) % ROUND, (j - 3) % 2
                    pe.wait_ge(sem.down_kept, n - 2)
                    pe.wait_ge(sem.prod_done, n - 2)
                    if after(n, 5):
                        pe.wait_ge(sem.y_ready, n - 4)
                    pe.matmul(bank[4 + m][:, 0:D], prod_t[:, at, :], w_down[:, at, 0:D], start=True, stop=True).then_inc(sem.y_done, 1)

            expert_steps(pe, emit, 3)

        @block.scalar
        def _(act):
            norm_statistics(nc, None, act, core, s, sem)
            act.wait_ge(sem.gate_turned, 1)
            act.activation(gate_t[:].rearrange("p c e -> p (c e)"), bank[2][:, 0:DC * E], ACT.Copy)
            act.activation(w_all[:, :, UP - 2:UP], bank[2][:, 2 * E + 4:4 * E + 4].rearrange("p (a e) -> p e a", a=2), ACT.Copy)
            act.activation(bs[:], bank[2][:, 2 * E:2 * E + 4], ACT.Copy).then_inc(sem.gate_ready, 1)

            def gate_step(n, q, r):
                if has_block(n, 0):
                    act.wait_ge(sem.turned, n + 1)
                    act.activation(xnt[:, 0, bass.ds(n * BW, BW)], bank[0][:, :], ACT.Copy).then_inc(sem.xnt0_ready, 1)
                if has_block(n, 1):
                    act.wait_ge(sem.logits_ready, n)
                    if after(n, 2):
                        act.wait_ge(sem.logits_turned, n - 1)
                    act.activation(logits_t, bank[2][0:E, :], ACT.Copy).then_inc(sem.logits_kept, 1)

            block_steps(act, gate_step, 1)
            act.wait_ge(sem.shifted, 1)
            act.activation(table[1], table[1], ACT.Exp).then_inc(sem.exp_ready, 1)

            def shared_block(i):
                for f in range(2):
                    act.wait_ge(sem.up_ready, 4 * i + f + 1)
                    if f == 0 and after(i, 1):
                        act.wait_ge(sem.prod_ready, i)
                    act.activation(s_silu[:, f, :], bank[f][:, :], ACT.Silu, bias=bs[:, f:f + 1]).then_inc(sem.silu_ready, 1)
                for f in range(2):
                    act.wait_ge(sem.up_ready, 4 * i + f + 3)
                    act.activation(s_lin[:, f, :], bank[2 + f][:, :], ACT.Identity, bias=bs[:, 2 + f:3 + f]).then_inc(sem.lin_ready, 1)

            def shared_out(i):
                for j in range(2):
                    act.wait_ge(sem.down_ready, 2 * i + j + 1)
                    if after(i, 1):
                        act.wait_ge(sem.z_added, 2 * (i - 1) + j + 1)
                    act.activation(z_half[:, j, :], bank[4 + j][:, :], ACT.Copy, scale=0.5).then_inc(sem.z_ready, 1)

            shared_block(0)
            shared_block(1)
            shared_out(0)
            with act.Fori(2, BLOCKS) as i:
                shared_block(i)
                shared_out(i - 1)
            shared_out(BLOCKS - 1)

            act.wait_ge(sem.experts_loaded, 16 * 6)
            act.wait_ge(sem.slots_ready, 1)
            act.wait_ge(sem.up_ready, 4 * BLOCKS)

            def emit(n, j, r):
                if runs(n, 0):
                    expert = act.value_load(expert_of[0:1, bass.ds(n, 1)], min_val=0, max_val=E - 1)
                    if after(n, ROUND):
                        act.wait_ge(sem.prod_done, n - ROUND + 1)
                    act.activation(w_up[:, j, :], w_all[:, bass.ds(expert, 1), 0:UP].rearrange("p o f -> p (o f)"), ACT.Copy
                                   ).then_inc(sem.up_kept, 1)
                    act.wait_ge(sem.rows_turned, n + 1)
                    if after(n, 2):
                        act.wait_ge(sem.up_done, n - 1)
                    act.activation(rows_t[:, j % 2, :], bank[j % 2][:, 0:D], ACT.Copy).then_inc(sem.rows_kept, 1)
                if runs(n, 1):
                    at, m = (j - 1) % ROUND, (j - 1) % 2
                    act.wait_ge(sem.up_done, n)
                    act.wait_ge(sem.up_kept, n)
                    if after(n, 3):
                        act.wait_ge(sem.prod_done, n - 2)
                    act.activation(gated[:, m, :], bank[2 + m][:, 0:P], ACT.Silu, bias=w_up[:, at, UP - 2:UP - 1]).then_inc(sem.gated_ready, 1)

            expert_steps(act, emit, 1)

        @block.gpsimd
        def _(pool):
            pool.wait_ge(sem.gate_loaded, 16 * 7)
            pool.tensor_scalar(bs2[:], bs2[:], 0.5, 0.0, ALU.mult, ALU.add).then_inc(sem.half_ready, 1)
            pool.wait_ge(sem.half_ready, 1)
            with pool.Fori(0, BLOCKS) as i:
                pool.wait_ge(sem.staged, i + 1)
                part = x[:, bass.ds(i * BT, BT), :]
                pool.tensor_tensor(part, part, bs2[:].rearrange("p (o d) -> p o d", o=1).to_broadcast([P, BT, D]), ALU.add
                                   ).then_inc(sem.bs2_added, 1)

            def shared_block(i):
                pool.wait_ge(sem.silu_ready, 2 * i + 2)
                pool.wait_ge(sem.lin_ready, 2 * i + 2)
                if after(i, 1):
                    pool.wait_ge(sem.down_ready, 2 * i)
                pool.tensor_tensor(s_prod.rearrange("p c n -> p (c n)"), s_silu[:].rearrange("p c n -> p (c n)"),
                                   s_lin[:].rearrange("p c n -> p (c n)"), ALU.mult).then_inc(sem.prod_ready, 1)

            def shared_out(i):
                for j in range(2):
                    pool.wait_ge(sem.z_ready, 2 * i + j + 1)
                    pair = x[:, bass.ds(i * BT + 2 * j, 2), :].rearrange("p n d -> p (n d)")
                    pool.tensor_tensor(pair, pair, z_half[:, j, :], ALU.add).then_inc(sem.z_added, 1)

            pool.wait_ge(sem.bs2_added, BLOCKS)
            for stored in stage_stored:
                pool.wait_ge(stored, 16 * (BLOCKS // 2))
            shared_block(0)
            shared_block(1)
            shared_out(0)
            with pool.Fori(2, BLOCKS - 1) as i:
                shared_block(i)
                shared_out(i - 1)

            def bring(n):
                if n >= ROUND:
                    pool.wait_ge(sem.rows_turned, n - ROUND + 1)
                pool.indirect_dma_start(out=rows_in[:, n % ROUND, :], out_offset=None, in_=xn_rows,
                                        in_offset=bass.IndirectOffsetOnAxis(ap=token_of[:, n:n + 1], axis=0)
                                        ).then_inc(row_loaded[n % ROUND], 16)

            pool.wait_ge(sem.tokens_ready, 1)
            for n in range(ROUND):
                bring(n)
            shared_block(BLOCKS - 1)
            shared_out(BLOCKS - 2)
            shared_out(BLOCKS - 1)
            for n in range(ROUND, SLOT_TILES):
                bring(n)
            if out is None:
                return
            for stored in row_stored:
                pool.wait_ge(stored, 16 * (SLOT_TILES // ROUND))
            for t in range(TILES):
                if t >= 8:
                    pool.wait_ge(sem.combined, t - 7)
                for k in range(TOPK):
                    pool.indirect_dma_start(out=back[:, 2 * (t % 8) + k, :], out_offset=None, in_=y_slots,
                                            in_offset=bass.IndirectOffsetOnAxis(ap=slots[:, t, k:k + 1], axis=0)
                                            ).then_inc(fetched[t % 8], 16)

        @block.vector
        def _(dve):
            norm_statistics(nc, dve, None, core, s, sem, x_loaded)
            logits = table[0].rearrange("p (t e) -> p t e", e=E)

            def gate_step(n, q, r):
                if has_block(n, 0):
                    if after(n, 2):
                        dve.wait_ge(sem.turned, n - 1)
                        dve.wait_ge(stage_stored[q], 16 * r)
                    for j in range(BT):
                        t = n * BT + j
                        last = dve.tensor_scalar(stage[:, q, j, :], tile(x, t), s.mean[:, bass.ds(t, 1)], s.rstd[:, bass.ds(t, 1)],
                                                 ALU.subtract, ALU.mult)
                    last.then_inc(sem.staged, 1)
                if has_block(n, 1):
                    dve.wait_ge(sem.turned, n)
                    dve.tensor_copy(xnt[:, 1, bass.ds((n - 1) * BW, BW)], bank[1][:, :]).then_inc(sem.xnt1_ready, 1)
                if has_block(n, 3):
                    dve.wait_ge(sem.logits_turned, n - 2)
                    if isinstance(n, int) and n == 3:
                        dve.wait_ge(sem.gate_ready, 1)
                    dve.tensor_copy(logits[:, bass.ds((n - 3) * BT, BT), :].rearrange("p t e -> p (t e)"), bank[3][:, 0:BT * E]
                                    ).then_inc(sem.logits_stored, 1)

            block_steps(dve, gate_step, 3)

            n = [0]

            def step(ins):
                n[0] += 1
                ins.then_inc(sem.route_step, 1)
                dve.wait_ge(sem.route_step, n[0])

            def by_expert(tab):
                return tab.rearrange("p (t e) -> p t e", e=E)

            def by_group(tab):
                return tab.rearrange("p (q m) -> p q m", m=E // G)

            def spread(ap, m):
                return ap.rearrange("p (n o) -> p n o", o=1).to_broadcast([P, ap.shape[1], m])

            def rows(ap, r):
                return ap.rearrange("p (o m) -> p o m", o=1).to_broadcast([P, r, ap.shape[1]])

            top, total = col[:, 0, :], col[:, 1, :]
            probs, score, work, first, second = table[1], table[2], table[3], table[4], table[5]
            equal, above = table[6], table[7]
            gsum, keep = table[8][:, 0:TILES * G], table[8][:, 256:256 + TILES * G]
            pairs = region[:, 9 * TILES * E:9 * TILES * E + TILES * G * 6].rearrange("p (q m) -> p q m", m=6)
            dve.wait_ge(sem.logits_stored, BLOCKS)
            step(dve.tensor_reduce(top, logits, AX, ALU.max))
            dve.tensor_tensor(by_expert(probs), logits, spread(top, E), ALU.subtract).then_inc(sem.shifted, 1)
            dve.wait_ge(sem.exp_ready, 1)
            step(dve.tensor_reduce(total, by_expert(probs), AX, ALU.add))
            step(dve.reciprocal(total, total))
            step(dve.tensor_tensor(by_expert(probs), by_expert(probs), spread(total, E), ALU.mult))
            step(dve.tensor_tensor(by_expert(score), by_expert(probs), rows(gate_b[:], TILES), ALU.add))
            quad = by_group(score)
            dve.tensor_tensor(pairs[:, :, 0:3], quad[:, :, 0:3], quad[:, :, 1:4], ALU.add)
            dve.tensor_tensor(pairs[:, :, 3:5], quad[:, :, 0:2], quad[:, :, 2:4], ALU.add)
            step(dve.tensor_tensor(pairs[:, :, 5:6], quad[:, :, 0:1], quad[:, :, 3:4], ALU.add))
            step(dve.tensor_reduce(gsum, pairs, AX, ALU.max))
            others = gsum.rearrange("p (t o g) -> p t o g", o=1, g=G).to_broadcast([P, TILES, G, G])
            own = gsum.rearrange("p (t g o) -> p t g o", o=1, g=G).to_broadcast([P, TILES, G, G])
            square = lambda tab: tab.rearrange("p (t g h) -> p t g h", g=G, h=G)
            dve.tensor_tensor(square(above), others, own, ALU.is_gt)
            step(dve.tensor_tensor(square(equal), others, own, ALU.is_equal))
            step(dve.tensor_tensor(by_expert(equal), by_expert(equal), rows(core.lower4[:].rearrange("p g h -> p (g h)"), TILES), ALU.mult))
            step(dve.tensor_tensor(above, above, equal, ALU.add))
            step(dve.tensor_reduce(keep, above.rearrange("p (q m) -> p q m", m=G), AX, ALU.add))
            step(dve.tensor_scalar(keep, keep, float(2), None, ALU.is_lt))
            step(dve.tensor_tensor(quad, quad, spread(keep, E // G), ALU.mult))
            step(dve.tensor_scalar(keep, keep, 1.0, -LOWEST, ALU.subtract, ALU.mult))
            step(dve.tensor_tensor(quad, quad, spread(keep, E // G), ALU.add))
            for k, pick in ((0, first), (1, second)):
                step(dve.tensor_reduce(top, by_expert(score), AX, ALU.max))
                step(dve.tensor_tensor(by_expert(work), by_expert(score), spread(top, E), ALU.is_equal))
                step(dve.tensor_tensor(by_expert(work), by_expert(work), rows(core.falling[:], TILES), ALU.mult))
                step(dve.tensor_reduce(top, by_expert(work), AX, ALU.max))
                step(dve.tensor_tensor(by_expert(pick), by_expert(work), spread(top, E), ALU.is_equal))
                if k == 0:
                    step(dve.scalar_tensor_tensor(score, first, LOWEST, score, ALU.mult, ALU.add))
            dve.tensor_tensor(assigned[:], first, second, ALU.add).then_inc(sem.pairs_ready, 1)
            for k, pick in ((0, first), (1, second)):
                step(dve.tensor_tensor(work, pick, probs, ALU.mult))
                step(dve.tensor_reduce(weight[:, k, :], by_expert(work), AX, ALU.add))
            step(dve.tensor_scalar(weight[:].rearrange("p k t -> p (k t)"), weight[:].rearrange("p k t -> p (k t)"), 0.5, None, ALU.mult))
            per_tile, ahead, offset = table[11], table[12], table[13]
            expert_major = lambda tab: tab.rearrange("p (e t) -> p e t", t=TILES)
            count, tiles_of, tiles_end, shift = small[:, 0, :], small[:, 1, :], small[:, 2, :], small[:, 3, :]
            dve.wait_ge(sem.counted, 1)
            step(dve.tensor_copy(expert_major(per_tile), bank[7][:, :].rearrange("p (t e) -> p e t", e=E)))
            step(dve.tensor_reduce(count, expert_major(per_tile), AX, ALU.add))
            step(dve.tensor_tensor_scan(ahead, core.ones[:, 0:1].to_broadcast([P, TILES * E]), per_tile, 0.0, ALU.mult, ALU.add))
            step(dve.tensor_tensor(ahead, ahead, per_tile, ALU.subtract))
            step(dve.tensor_tensor(expert_major(work), spread(count, TILES), rows(core.full_tiles[:], E), ALU.is_gt))
            step(dve.tensor_reduce(tiles_of, expert_major(work), AX, ALU.add))
            step(dve.tensor_tensor_scan(tiles_end, core.ones[:, 0:1].to_broadcast([P, E]), tiles_of, 0.0, ALU.mult, ALU.add))
            step(dve.tensor_tensor(shift, tiles_end, tiles_of, ALU.subtract))
            step(dve.scalar_tensor_tensor(shift, shift, float(P), expert_major(ahead)[:, :, 0], ALU.mult, ALU.subtract))
            step(dve.tensor_tensor(offset.rearrange("p (t e) -> p e t", e=E), expert_major(ahead), spread(shift, TILES), ALU.add))
            step(dve.tensor_tensor(offset, bank[6][:, :], offset, ALU.add))
            for k, pick in ((0, first), (1, second)):
                step(dve.tensor_tensor(work, pick, offset, ALU.mult))
                step(dve.tensor_reduce(slots_f[:, k::TOPK], by_expert(work), AX, ALU.add))
            step(dve.tensor_scalar(slot_tile[:], slots_f[:], (P - 1) / 2, 1.0 / P, ALU.subtract, ALU.mult))
            step(dve.tensor_scalar(slot_tile[:], slot_tile[:], TO_WHOLE, None, ALU.add))
            step(dve.tensor_scalar(slot_tile[:], slot_tile[:], TO_WHOLE, None, ALU.subtract))
            dve.tensor_copy(tile_of[:], slot_tile[:])
            step(dve.scalar_tensor_tensor(row_of[:], slot_tile[:], -float(P), slots_f[:], ALU.mult, ALU.add))
            by_pair = lambda ap, m: ap.rearrange("p (q o) -> p q o", o=1).to_broadcast([P, PAIRS, m])
            per_pair = lambda ap: ap.rearrange("p (o m) -> p o m", o=1).to_broadcast([P, PAIRS, ap.shape[1]])
            dve.tensor_tensor(row_hot, per_pair(core.row_id[:]), by_pair(row_of[:], P), ALU.is_equal)
            step(dve.tensor_tensor(tile_hot[:, :, 0, :], per_pair(core.tile_id16[:]), by_pair(tile_of[:], SLOT_TILES), ALU.is_equal))
            step(dve.tensor_tensor(tile_hot[:, :, 1, :], tile_hot[:, :, 0, :], by_pair(core.tile_of_pair[:], SLOT_TILES), ALU.mult))
            dve.tensor_scalar(tile_hot[:, :, 0, :], tile_hot[:, :, 0, :], core.part_id[:], None, ALU.mult).then_inc(sem.hot_ready, 1)
            step(dve.tensor_tensor(expert_hit[:], tiles_end[0:1, :].rearrange("p (o e) -> p o e", o=1).to_broadcast([1, SLOT_TILES, E]),
                                   core.tile_id[0:1, :].rearrange("p (n o) -> p n o", o=1).to_broadcast([1, SLOT_TILES, E]), ALU.is_le))
            step(dve.tensor_reduce(expert_f[:], expert_hit[:], AX, ALU.add))
            step(dve.tensor_scalar(expert_of[:], expert_f[:], float(E - 1), None, ALU.min))
            dve.tensor_copy(slots[:].rearrange("p t k -> p (t k)"), slots_f[:]).then_inc(sem.slots_ready, 1)
            dve.wait_ge(sem.inverted, 1)
            step(dve.tensor_scalar(token_f[:], bank[7][:, SLOT_TILES:2 * SLOT_TILES], float(P), None, ALU.mult))
            step(dve.tensor_tensor(token_f[:], token_f[:], bank[7][:, 0:SLOT_TILES], ALU.add))
            dve.tensor_copy(token_of[:], token_f[:]).then_inc(sem.tokens_ready, 1)

            dve.wait_ge(sem.experts_loaded, 16 * 6)
            dve.wait_ge(sem.slots_ready, 1)
            dve.wait_ge(sem.up_ready, 4 * BLOCKS)

            def emit(n, j, r):
                if runs(n, 0):
                    expert = dve.value_load(expert_of[0:1, bass.ds(n, 1)], min_val=0, max_val=E - 1)
                    if after(n, ROUND):
                        dve.wait_ge(sem.y_ready, n - ROUND + 1)
                    dve.tensor_copy(w_down[:, j, :], w_all[:, bass.ds(expert, 1), UP:].rearrange("p o f -> p (o f)")).then_inc(sem.down_kept, 1)
                if runs(n, 3):
                    at, m = (j - 3) % ROUND, (j - 3) % 2
                    dve.wait_ge(sem.y_done, n - 2)
                    dve.wait_ge(sem.down_kept, n - 2)
                    if after(n, ROUND + 3):
                        dve.wait_ge(row_stored[at], 16 * (r if j >= 3 else r - 1))
                    dve.tensor_tensor(y_rows[:, at, :], bank[4 + m][:, 0:D], w_down[:, at, D:], ALU.add).then_inc(sem.y_ready, 1)
                if runs(n, 1):
                    at, m = (j - 1) % ROUND, (j - 1) % 2
                    dve.wait_ge(sem.gated_ready, n)
                    if after(n, ROUND + 1):
                        dve.wait_ge(sem.y_done, n - ROUND)
                    dve.scalar_tensor_tensor(prod_t[:, at, :], bank[2 + m][:, P:2 * P], w_up[:, at, UP - 1:UP], gated[:, m, :], ALU.add, ALU.mult
                                             ).then_inc(sem.prod_done, 1)

            expert_steps(dve, emit, 3)

            if out is None:
                return
            dve.wait_ge(sem.z_added, 2 * BLOCKS)
            added = [0]

            def combine(t, i):
                xt = tile(x, t)
                dve.wait_ge(fetched[added[0] % 8], 32 * (i + 1))
                dve.scalar_tensor_tensor(xt, back[:, 2 * (added[0] % 8), :], weight[:, 0, bass.ds(t, 1)], xt, ALU.mult, ALU.add
                                         ).then_inc(sem.first_added, 1)
                dve.wait_ge(sem.first_added, t + 1)
                dve.scalar_tensor_tensor(xt, back[:, 2 * (added[0] % 8) + 1, :], weight[:, 1, bass.ds(t, 1)], xt, ALU.mult, ALU.add
                                         ).then_inc(sem.combined, 1)
                added[0] += 1

            with dve.Fori(0, TILES // 8) as i:
                for j in range(8):
                    combine(i * 8 + j, i)
    give_back(nc, sem, stage_stored, row_loaded, row_stored, fetched)


def attention(nc, core, w, tag, y_slots):
    q_dram = nc.dram_tensor(f"{tag}_q", (BLOCKS, GROUPS, P, BW), FP16, kind="Internal").ap()
    k_dram = nc.dram_tensor(f"{tag}_k", (BLOCKS, GROUPS, P, BW), FP16, kind="Internal").ap()
    v_dram = nc.dram_tensor(f"{tag}_v", (BLOCKS, GROUPS, BT, P, P), FP32, kind="Internal").ap()
    with ExitStack() as ctx:
        made = lines(nc, core, w, f"{tag}_lines", ctx, y_slots, q_dram, k_dram, v_dram)
        lines_sem, v_stored, _ = made.semaphores
        weighed, clear, load_first = attend(nc, core, w, f"{tag}_attend", ctx, lines_sem, v_stored, q_dram, k_dram, v_dram)
        with nc.Block() as block:
            @block.sync
            def _(sp):
                made.sync(sp, load_first)
                weighed.sync(sp)

            @block.tensor
            def _(pe):
                made.tensor(pe)
                weighed.tensor(pe)

            @block.scalar
            def _(act):
                clear(act)
                made.scalar(act)
                weighed.scalar(act)

            @block.gpsimd
            def _(pool):
                made.gpsimd(pool)
                weighed.gpsimd(pool)

            @block.vector
            def _(dve):
                made.vector(dve)
                weighed.vector(dve)
    give_back(nc, *made.semaphores, *weighed.semaphores)


Programs = namedtuple("Programs", "sync tensor scalar gpsimd vector semaphores")


def lines(nc, core, w, tag, ctx, y_slots, q_dram, k_dram, v_dram):
    sb = lambda name, shape, dt=FP32: ctx.enter_context(nc.sbuf_tensor(f"{tag}_{name}", shape, dt))
    x, bank = core.x, core.bank
    w_now = sb("w_now", [P, DC, 2 * D])
    w_prev = sb("w_prev", [P, DC, P])
    w_o, b_o = sb("w_o", [P, DC, D]), sb("b_o", [P, D])
    b_v, b_v_wide = sb("b_v", [P, DC]), sb("b_v_wide", [P, DC, P])
    goes_on = sb("goes_on", [P, BLOCKS])
    stage = sb("stage", [P, 2, BT, D])
    back = sb("back", [P, 2, BT, TOPK, D])
    rows_of = sb("rows_of", [P, 2, BT, TOPK], I32)
    xt = sb("xt", [P, DC, 1 + BW])
    points = sb("points", [P, 2, 2 * BT, 2, H, 4])
    line, other = sb("line", [P, 2 * BT * H, PL]), sb("other", [P, 2 * BT * H, PL])
    size, inverse = sb("size", [P, 2 * BT * H]), sb("inverse", [P, 2 * BT * H])
    feats = sb("feats", [P, 2, 2, BT * H, HR], FP16)
    q_out, k_out = sb("q_out", [P, GROUPS, BW], FP16), sb("k_out", [P, GROUPS, BW], FP16)
    v_out = sb("v_out", [P, 2, BT, H * HR + 2 * DH])
    values = lambda q, j: v_out[:, q, j, :].rearrange("p (a n) -> p a n", a=2)[:, :, 0:H // 2 * HR].rearrange(
        "p a (h r) -> p a h r", r=HR)[:, :, :, 0:DH]
    sem = semaphores(nc, tag, "weights_loaded stat_turn pick_turn stat_step var_ready root_ready inverse_ready rstd_ready picked first_added combined marked filled b_wide b_projected b_ready "
                     "staged turned edge_ready xt_ready projected points_ready value_ready other_ready line_step squared "
                     "size_ready parts_ready feats_ready store_turn q_turned k_turned q_ready k_ready q_stored k_stored bo_added")
    v_stored, fetched = ring_semaphores(nc, f"{tag}_v_stored", 2), ring_semaphores(nc, f"{tag}_fetched", 2 * BT)
    stats = Statistics(x, sb, sem)
    WEIGHTS = 16 * 10

    def sync(sp, load_first):
        heads = [(w["W1_q"], 0), (w["W2_q"], 64), (w["W1_k"], 128), (w["W2_k"], 192), (w["W_v"], 256)]
        for weight, at in heads:
            n = weight.shape[1]
            sp.dma_start(w_now[:, :, at:at + n], weight[0:D, :].rearrange("(c p) n -> p c n", p=P)).then_inc(sem.weights_loaded, 16)
        for weight, at in heads[0:2]:
            sp.dma_start(w_prev[:, :, at:at + 64], weight[D:2 * D, :].rearrange("(c p) n -> p c n", p=P)).then_inc(sem.weights_loaded, 16)
        sp.dma_start(w_o[:], w["W_o"].rearrange("(c p) n -> p c n", p=P)).then_inc(sem.weights_loaded, 16)
        sp.dma_start(b_v[:], w["b_v"].rearrange("(c p) -> p c", p=P), allow_slow_non_contiguous=True).then_inc(sem.weights_loaded, 16)
        sp.dma_start(b_o[:], over_partitions(w["b_o"], P, D)).then_inc(sem.weights_loaded, 16)

        def step(n, q, r):
            if has_block(n, 2):
                sp.wait_ge(sem.q_ready, 2 * (n - 1))
                sp.sem_inc(sem.store_turn, 1)
                sp.dma_start(q_dram[bass.ds(n - 2, 1), :, :, :].rearrange("o g p n -> p (o g) n"), q_out[:]).then_inc(sem.q_stored, 16)
                sp.wait_ge(sem.k_ready, 2 * (n - 1))
                sp.sem_inc(sem.store_turn, 1)
                sp.dma_start(k_dram[bass.ds(n - 2, 1), :, :, :].rearrange("o g p n -> p (o g) n"), k_out[:]).then_inc(sem.k_stored, 16)
            if has_block(n, 0):
                sp.wait_ge(sem.value_ready, BT * n + BT)
                for j in range(BT):
                    sp.dma_start(v_dram[bass.ds(n, 1), :, j, :, :].rearrange("o g p n -> p (o g) n"),
                                 v_out[:, q, j, 0:H * HR].rearrange("p (g n) -> p g n", g=GROUPS)).then_inc(v_stored[q], 16)

        block_steps(sp, step, 1)
        load_first(sp)
        step(BLOCKS + 1, (BLOCKS + 1) % 2, (BLOCKS + 1) // 2)

    def gpsimd(pool):
        def halves(n, q):
            if has_block(n, 1):
                pool.wait_ge(sem.points_ready, BT * n)
                if after(n, 2):
                    pool.wait_ge(sem.squared, n - 1)
                p1, p2 = points[:, 1 - q, :, 0, :, :], points[:, 1 - q, :, 1, :, :]
                o = other[:].rearrange("p (a h) c -> p a h c", h=H)
                spread = lambda ap, m: ap.to_broadcast([P, 2 * BT, H, m])
                pool.tensor_tensor(o[:, :, :, 0:3], p1[:, :, :, 1:4], spread(p2[:, :, :, 0:1], 3), ALU.mult)
                pool.tensor_tensor(o[:, :, :, 3:5], p1[:, :, :, 2:4], spread(p2[:, :, :, 1:2], 2), ALU.mult)
                pool.tensor_tensor(o[:, :, :, 5:6], p1[:, :, :, 3:4], p2[:, :, :, 2:3], ALU.mult).then_inc(sem.other_ready, 1)

        def step(n, q, r):
            if has_block(n, 0):
                if after(n, 2):
                    pool.wait_ge(sem.combined, n - 1)
                pool.tensor_copy(rows_of[:, q, :, :], core.slots[:, bass.ds(n * BT, BT), :]).then_inc(sem.picked, 1)
                pool.wait_ge(sem.picked, n + 1)
                pool.sem_inc(sem.pick_turn, 1)
                for j in range(BT):
                    for k in range(TOPK):
                        pool.indirect_dma_start(out=back[:, q, j, k, :], out_offset=None, in_=y_slots,
                                                in_offset=bass.IndirectOffsetOnAxis(ap=rows_of[:, q, j, k:k + 1], axis=0)
                                                ).then_inc(fetched[q * BT + j], 16)
            halves(n - 1, 1 - q)
            if isinstance(n, int) and n >= BLOCKS:
                pool.wait_ge(sem.b_ready, 1)
                for b in bias_at[n]:
                    pool.wait_ge(sem.staged, b + 1)
                    part = x[:, b * BT:(b + 1) * BT, :]
                    pool.tensor_tensor(part, part, b_o[:].rearrange("p (o d) -> p o d", o=1).to_broadcast([P, BT, D]), ALU.add
                                       ).then_inc(sem.bo_added, 1)

        bias_at = {BLOCKS: range(BLOCKS // 2), BLOCKS + 1: range(BLOCKS // 2, BLOCKS)}
        block_steps(pool, step, 2)

    def tensor(pe):
        pe.wait_ge(sem.weights_loaded, WEIGHTS)
        pe.wait_ge(sem.b_wide, 1)
        for c in range(DC):
            last = pe.matmul(bank[2][:, 0:D], b_v_wide[:, c, :], w_o[:, c, :], start=(c == 0), stop=(c == DC - 1))
        last.then_inc(sem.b_projected, 1)
        pe.wait_ge(sem.filled, 2)
        pe.wait_ge(sem.b_ready, 1)

        def step(n, q, r):
            if has_block(n, 0):
                pe.wait_ge(sem.staged, n + 1)
                if after(n, 1):
                    pe.wait_ge(sem.xt_ready, 2 * n)
                for c in range(DC):
                    for j in range(BT):
                        last = pe.transpose(bank[c][:, j * P:(j + 1) * P], stage[:, q, j, c * P:(c + 1) * P], core.ident[:])
                last.then_inc(sem.turned, 1)
            if has_block(n, 2):
                pe.wait_ge(sem.feats_ready, n - 1)
                for side, first, signal in ((0, 6, sem.q_turned), (1, 4, sem.k_turned)):
                    if side == 0 and after(n, 3):
                        pe.wait_ge(sem.q_ready, 2 * (n - 2))
                    if side == 1:
                        pe.wait_ge(sem.value_ready, BT * (min(n, BLOCKS) if isinstance(n, int) else n))
                        if after(n, 3):
                            pe.wait_ge(sem.k_ready, 2 * (n - 2))
                    for g in range(GROUPS):
                        turned = bank[first + g // 2].bitcast(FP16)
                        for j in range(BT):
                            at = (g % 2) * BW + j * P
                            last = pe.transpose(turned[:, at:at + P],
                                                feats[:, q, side, j * H + g * HG:j * H + (g + 1) * HG, :].rearrange("p h r -> p (h r)"),
                                                core.ident16[:])
                        if g % 2:
                            last.then_inc(signal, 1)
            if has_block(n, 0):
                pe.wait_ge(sem.xt_ready, 2 * n + 2)
                for j in range(BT):
                    if after(n, 1):
                        pe.wait_ge(sem.value_ready, BT * (n - 1) + j + 1)
                    if j >= 2 and after(n, 2):
                        pe.wait_ge(sem.k_ready, 2 * (n - 2) + j - 1)
                    now = lambda c: xt[:, c, 1 + j * P:1 + (j + 1) * P]
                    pe.matmul(bank[2 + j], now(0), w_now[:, 0, :], start=True, stop=False)
                    for c in range(DC):
                        pe.matmul(bank[2 + j][:, 0:P], xt[:, c, j * P:(j + 1) * P], w_prev[:, c, :], start=False, stop=False)
                    pe.matmul(bank[2 + j], now(1), w_now[:, 1, :], start=False, stop=True).then_inc(sem.projected, 1)

        block_steps(pe, step, 2)

    def scalar(act):
        act.activation(v_out[:].rearrange("p q t n -> p (q t n)"), core.one[:].to_broadcast([P, 2 * BT * (H * HR + 2 * DH)]), ACT.Copy
                       ).then_inc(sem.filled, 1)
        act.wait_ge(sem.filled, 2)

        def transposed(n):
            act.wait_ge(sem.turned, n + 1)
            act.activation(xt[:, :, 0:1], xt[:, :, BW:BW + 1], ACT.Copy, scale=goes_on[:, bass.ds(n, 1)]).then_inc(sem.edge_ready, 1)
            act.wait_ge(sem.edge_ready, n + 1)
            for c in range(DC):
                act.activation(xt[:, c, 1:], bank[c], ACT.Copy).then_inc(sem.xt_ready, 1)

        def second_copies(n, q):
            act.wait_ge(sem.parts_ready, n + 1)
            both = feats[:, q, 0, :, 0:4 * PL].rearrange("p n (a c) -> p n a c", a=2)
            act.activation(both[:, :, :, PL:], both[:, :, :, 0:PL], ACT.Copy)
            act.activation(feats[:, q, 1, :, 2 * PL:4 * PL], feats[:, q, 1, :, 0:2 * PL], ACT.Copy).then_inc(sem.feats_ready, 1)

        def features(n):
            for buf, first, turned, stored, signal in ((q_out, 6, sem.q_turned, sem.q_stored, sem.q_ready),
                                                       (k_out, 4, sem.k_turned, sem.k_stored, sem.k_ready)):
                if after(n, 1):
                    act.wait_ge(stored, 16 * n)
                for g in range(2):
                    act.wait_ge(turned, 2 * n + g + 1)
                    act.activation(buf[:, 2 * g:2 * g + 2, :].rearrange("p g n -> p (g n)"), bank[first + g].bitcast(FP16), ACT.Copy
                                   ).then_inc(signal, 1)

        def points_and_values(n, q, r):
            if after(n, 2):
                act.wait_ge(sem.other_ready, n - 1)
                act.wait_ge(sem.squared, n - 1)
                act.wait_ge(v_stored[q], 16 * BT * r)
            for j in range(BT):
                act.wait_ge(sem.projected, BT * n + j + 1)
                act.activation(points[:, q, j:2 * BT:BT, :, :, :].rearrange("p a b h c -> p a (b h c)"),
                               bank[2 + j][:, 0:2 * P].rearrange("p (a n) -> p a n", a=2), ACT.Copy).then_inc(sem.points_ready, 1)
                act.activation(values(q, j), bank[2 + j][:, 2 * P:].rearrange("p (a h d) -> p a h d", a=2, d=DH), ACT.Copy
                               ).then_inc(sem.value_ready, 1)

        def step(n, q, r):
            if has_block(n, 3):
                second_copies(n - 3, 1 - q)
            if has_block(n, 1):
                transposed(n - 1)
            if has_block(n, 3):
                features(n - 3)
            if has_block(n, 0):
                stats.take_root(act, n, q)
            if has_block(n, 2):
                act.wait_ge(sem.squared, n - 1)
                act.activation(size[:], size[:], ACT.Sqrt).then_inc(sem.size_ready, 1)
            if has_block(n, 0):
                if after(n, 2):
                    act.wait_ge(sem.turned, n - 1)
                stats.normalize(act, n, q, stage[:, q])
            if has_block(n, 1):
                points_and_values(n - 1, 1 - q, r if q else r - 1)

        block_steps(act, step, 3)

    STEPS = 9

    def vector(dve):
        dve.memset(feats[:], 0.0)
        dve.memset(xt[:], 0.0)
        dve.memset(goes_on[:], 1.0).then_inc(sem.marked, 1)
        dve.wait_ge(sem.marked, 1)
        dve.memset(goes_on[:, 0:BLOCKS:BLOCKS // BATCH], 0.0).then_inc(sem.filled, 1)
        dve.wait_ge(sem.weights_loaded, WEIGHTS)
        dve.tensor_copy(b_v_wide[:], b_v[:].rearrange("p (c o) -> p c o", o=1).to_broadcast([P, DC, P])).then_inc(sem.b_wide, 1)
        dve.wait_ge(sem.b_projected, 1)
        dve.tensor_tensor(b_o[:], bank[2][:, 0:D], b_o[:], ALU.add).then_inc(sem.b_ready, 1)
        dve.wait_ge(sem.filled, 2)

        def step_block(n, q, r):
            if has_block(n, 0):
                combine(n, q, r)
                dve.wait_ge(sem.combined, n + 1)
                stats.sum_up(dve, n, q)
            if has_block(n, 2):
                measure_lines(n - 1, q)
            if has_block(n, 0):
                stats.invert(dve, n, q)
            if has_block(n, 2):
                split_lines(n - 1, q)

        def combine(n, q, r):
            for k in range(TOPK):
                for j in range(BT):
                    t = n * BT + j
                    if k == 0:
                        dve.wait_ge(fetched[q * BT + j], 16 * TOPK * (r + 1))
                    last = dve.scalar_tensor_tensor(stats.tile(t), back[:, q, j, k, :], core.weight[:, k, bass.ds(t, 1)], stats.tile(t),
                                                    ALU.mult, ALU.add)
                if k == 0:
                    last.then_inc(sem.first_added, 1)
                    dve.wait_ge(sem.first_added, n + 1)
            last.then_inc(sem.combined, 1)

        def stepper(n, ahead):
            done = [ahead]

            def step(ins):
                done[0] += 1
                ins.then_inc(sem.line_step, 1)
                dve.wait_ge(sem.line_step, (n - 1) * STEPS + done[0])

            return step

        def measure_lines(n, ring):
            step = stepper(n, 0)
            dve.wait_ge(sem.points_ready, BT * n)
            if after(n, 2):
                dve.wait_ge(sem.parts_ready, n - 1)
            p1, p2 = points[:, ring, :, 0, :, :], points[:, ring, :, 1, :, :]
            o = line[:].rearrange("p (a h) c -> p a h c", h=H)
            spread = lambda ap, m: ap.to_broadcast([P, 2 * BT, H, m])
            dve.tensor_tensor(o[:, :, :, 0:3], spread(p1[:, :, :, 0:1], 3), p2[:, :, :, 1:4], ALU.mult)
            dve.tensor_tensor(o[:, :, :, 3:5], spread(p1[:, :, :, 1:2], 2), p2[:, :, :, 2:4], ALU.mult)
            step(dve.tensor_tensor(o[:, :, :, 5:6], p1[:, :, :, 2:3], p2[:, :, :, 3:4], ALU.mult))
            dve.wait_ge(sem.other_ready, n)
            step(dve.tensor_tensor(line[:], line[:], other[:], ALU.subtract))
            step(dve.tensor_tensor(other[:], line[:], line[:], ALU.mult))
            dve.tensor_reduce(size[:], other[:], AX, ALU.add).then_inc(sem.squared, 1)

        def split_lines(n, ring):
            step = stepper(n, 3)
            dve.wait_ge(sem.size_ready, n)
            step(dve.tensor_scalar(size[:], size[:], 1e-12, None, ALU.max))
            step(dve.reciprocal(inverse[:], size[:]))
            step(dve.tensor_tensor(line[:], line[:], inverse[:].rearrange("p (n o) -> p n o", o=1)
                                   .to_broadcast([P, 2 * BT * H, PL]), ALU.mult))
            lq, lk = line[:, 0:BT * H, :], line[:, BT * H:, :]
            step(dve.tensor_scalar(lk[:, :, 1:5:3], lk[:, :, 1:5:3], -1.0, None, ALU.mult))
            if after(n, 3):
                dve.wait_ge(sem.k_turned, 2 * (n - 2))
            lk = lk[:, :, ::-1]
            q_high, q_low = feats[:, ring, 0, :, 0:PL], feats[:, ring, 0, :, 2 * PL:3 * PL]
            k_high, k_low = feats[:, ring, 1, :, 0:PL], feats[:, ring, 1, :, PL:2 * PL]
            step(dve.tensor_copy(q_high, lq))
            step(dve.tensor_copy(k_high, lk))
            dve.tensor_tensor(q_low, lq, q_high, ALU.subtract)
            dve.tensor_tensor(k_low, lk, k_high, ALU.subtract).then_inc(sem.parts_ready, 1)

        block_steps(dve, step_block, 2)

    return Programs(sync, tensor, scalar, gpsimd, vector, (sem, v_stored, fetched))




def attend(nc, core, w, tag, ctx, lines_sem, v_stored, q_dram, k_dram, v_dram):
    sb = lambda name, shape, dt=FP32: ctx.enter_context(nc.sbuf_tensor(f"{tag}_{name}", shape, dt))
    x, banks = core.x, core.banks
    SLOTS, RING, LAG = 3, 4, 2
    ALL = BATCH * GROUPS
    q_now = sb("q_now", [P, HG, T], FP16)
    k_now = sb("k_now", [P, T], FP16)
    v_now = sb("v_now", [P, KT, P])
    probs = sb("probs", [P, RING, HG, QW])
    w_o = sb("w_o", [P, GROUPS // 2, D])
    holds = sb("holds", [P, 2])
    sums, below = sb("sums", [P, QW]), sb("below", [P, QW])
    upper, heads = sb("upper", [P, QW]), sb("heads", [P, QC, QW])
    score = [banks[:, 2 * n:2 * n + 2, :] for n in range(SLOTS)]
    out_bank, proj_bank = banks[:, 6, :], banks[:, 7, :]
    sem = semaphores(nc, tag, "zeroed w_loaded mask_turn stat_turn shuffle_turn load_turn scores_ready exp_done masked pv_done sums_kept chain_step holds_ready divided heads_ready "
                "proj_done proj_added")
    q_loaded, kv_loaded = ring_semaphores(nc, f"{tag}_q_loaded", QC), ring_semaphores(nc, f"{tag}_kv_loaded", QC)

    per_chunk = QW // P
    units = [(qc, kt, max(0, kt - per_chunk * qc) * P) for qc in range(QC) for kt in range(per_chunk * (qc + 1))]
    U = len(units)
    last_of = [max(u for u, v in enumerate(units) if v[0] == qc) for qc in range(QC)]
    diagonal = [u for u, (qc, kt, _) in enumerate(units) if kt >= per_chunk * qc]
    project_at = {7: (QC - 1, 0), 8: (QC - 1, 1), 9: (0, 0), 10: (0, 1), 20: (1, 0), 22: (1, 1), 36: (2, 0), 38: (2, 1)}
    def projected_before(two, qc, half):
        return 2 * (QC * two + qc) + half

    def place(g):
        return g % 2 * 2 + g // 2 % 2

    def groups(eng, emit):
        for side in range(2):
            emit(side, side, 0)
        with eng.Fori(1, ALL // 2) as two:
            for side in range(2):
                emit(two * 2 + side, side, two)

    def later(g):
        return not isinstance(g, int) or g > 0

    def load_q(sp, g, m):
        i, gr = g // GROUPS * QC + m, place(g)
        for j in range(HG):
            rows = slice(j * HR, (j + 1) * HR)
            sp.dma_start(q_now[rows, j, m * QW:(m + 1) * QW],
                         q_dram[bass.ds(i, 1), bass.ds(gr, 1), rows, :].rearrange("o g p n -> p (o g n)")).then_inc(q_loaded[m], 16)

    def load_kv(sp, g, m):
        i, gr = g // GROUPS * QC + m, place(g)
        sp.dma_start(k_now[:, m * QW:(m + 1) * QW],
                     k_dram[bass.ds(i, 1), bass.ds(gr, 1), :, :].rearrange("o g p n -> p (o g n)")).then_inc(kv_loaded[m], 16)
        sp.dma_start(v_now[:, m * BT:(m + 1) * BT, :],
                     v_dram[bass.ds(i, 1), bass.ds(gr, 1), :, :, :].rearrange("o g t p n -> p (o g t) n")).then_inc(kv_loaded[m], 16)

    def load_weights(sp):
        for j in range(HG):
            for side in range(2):
                at = j * HR + side * DH
                sp.dma_start(w_o[at:at + DH, :, :], w["W_o"].rearrange("(s g j d) n -> s j d g n", s=2, j=HG, d=DH)[side, j]
                             ).then_inc(sem.w_loaded, 16)

    def load_first(sp):
        load_weights(sp)
        sp.wait_ge(sem.zeroed, 1)
        sp.wait_ge(lines_sem.q_stored, 16 * QC)
        sp.wait_ge(lines_sem.k_stored, 16 * QC)
        for stored in v_stored:
            sp.wait_ge(stored, 16 * BT * QC // 2)
        for m in range(QC):
            load_q(sp, 0, m)
            load_kv(sp, 0, m)

    def sync(sp):
        sp.wait_ge(lines_sem.q_stored, 16 * BLOCKS)
        sp.wait_ge(lines_sem.k_stored, 16 * BLOCKS)
        for stored in v_stored:
            sp.wait_ge(stored, 16 * BT * BLOCKS // 2)
        with sp.Fori(0, ALL - 1) as g:
            for m in range(QC - 1):
                sp.wait_ge(sem.scores_ready, 2 * (U * g + last_of[m] + 1))
                sp.sem_inc(sem.load_turn, 1)
                load_q(sp, g + 1, m)
            for m in range(QC):
                sp.wait_ge(sem.pv_done, U * g + last_of[QC - 2] + 1 + (m + 1) * BT)
                sp.sem_inc(sem.load_turn, 1)
                load_kv(sp, g + 1, m)
            load_q(sp, g + 1, QC - 1)

    def tensor(pe):
        def half_scores(g, u, half):
            qc, kt, c0 = units[u]
            hu = 2 * u + half
            if u == 0 or units[u - 1][0] != qc:
                if half == 0:
                    pe.wait_ge(q_loaded[qc], 16 * HG * (g + 1))
                    pe.wait_ge(kv_loaded[qc], 32 * (g + 1))
            older = hu - SLOTS if hu >= SLOTS else max(h for h in range(-SLOTS, 0) if (h + 2 * U) % SLOTS == hu % SLOTS)
            if later(g) or older >= 0:
                pe.wait_ge(sem.exp_done, 2 * U * g + older + 1)
            for j in range(2):
                h = 2 * half + j
                last = pe.matmul(score[hu % SLOTS][:, j, c0:QW], k_now[:, kt * P:(kt + 1) * P],
                                 q_now[:, h, qc * QW + c0:(qc + 1) * QW], start=True, stop=True)
            last.then_inc(sem.scores_ready, 1)

        def weigh(g, u):
            qc, kt, c0 = units[u]
            pe.wait_ge(sem.exp_done, 2 * (U * g + u + 1))
            if u in diagonal:
                pe.wait_ge(sem.masked, len(diagonal) * g + diagonal.index(u) + 1)
            if kt == 0 and (later(g) or qc > 0):
                pe.wait_ge(sem.sums_kept, QC * g + qc)
            for h in range(HG):
                rows = slice(h * HR, (h + 1) * HR)
                last = pe.matmul(out_bank[rows, c0:QW], v_now[:, kt, rows], probs[:, u % RING, h, c0:QW],
                                 start=(kt == 0), stop=(u == last_of[qc]))
            last.then_inc(sem.pv_done, 1)

        def project(two, qc, half):
            pe.wait_ge(sem.heads_ready, QC * two + qc + 1)
            before = projected_before(two, qc, half)
            if not isinstance(before, int) or before > 0:
                pe.wait_ge(sem.proj_added, before)
            for j in range(2):
                at = (2 * half + j) * P
                last = pe.matmul(proj_bank[:, j * D:(j + 1) * D], heads[:, qc, at:at + P],
                                 w_o[:, bass.ds(two % (GROUPS // 2), 1), :].rearrange("p o d -> p (o d)"), start=True, stop=True)
            last.then_inc(sem.proj_done, 1)

        def step(g, side, two, u):
            half_scores(g, u, 0)
            if u >= LAG:
                weigh(g, u - LAG)
            elif later(g):
                weigh(g - 1, U + u - LAG)
            half_scores(g, u, 1)
            if u in project_at:
                qc, part = project_at[u]
                if qc < QC - 1 and side == 1:
                    project(two, qc, part)
                elif qc == QC - 1 and side == 0 and later(g):
                    project(two - 1, qc, part)

        def group(g, side, two):
            for u in range(U):
                step(g, side, two, u)

        pe.wait_ge(sem.w_loaded, 16 * 2 * HG)
        pe.wait_ge(lines_sem.xt_ready, DC * BLOCKS)
        pe.wait_ge(lines_sem.value_ready, BT * BLOCKS)
        pe.wait_ge(lines_sem.q_ready, 2 * BLOCKS)
        pe.wait_ge(lines_sem.k_ready, 2 * BLOCKS)
        groups(pe, group)
        for u in range(U - LAG, U):
            weigh(ALL - 1, u)
        for half in range(2):
            project(ALL // 2 - 1, QC - 1, half)

    def scalar(act):
        def group(g, side, two):
            for u, (qc, kt, c0) in enumerate(units):
                for half in range(2):
                    hu = 2 * u + half
                    act.wait_ge(sem.scores_ready, 2 * U * g + hu + 1)
                    if half == 0 and (later(g) or u >= RING):
                        act.wait_ge(sem.pv_done, U * g + u - RING + 1)
                    act.activation(probs[:, u % RING, 2 * half:2 * half + 2, c0:QW], score[hu % SLOTS][:, :, c0:QW], ACT.Exp,
                                   scale=SCALE).then_inc(sem.exp_done, 1)

        groups(act, group)

    def clear(act):
        act.activation(q_now[:].rearrange("p h n -> p (h n)"), core.zero[:].to_broadcast([P, HG * T]), ACT.Copy).then_inc(sem.zeroed, 1)

    def gpsimd(pool):
        def group(g, side, two):
            for u in diagonal:
                c0 = units[u][2]
                pool.wait_ge(sem.exp_done, 2 * (U * g + u + 1))
                pool.sem_inc(sem.mask_turn, 1)
                part = probs[:, u % RING, :, c0:c0 + P]
                pool.affine_select(out=part, in_=part, compare_op=ALU.is_ge, fill=0.0, base=0,
                                   pattern=[[0, HG], [1, P]], channel_multiplier=-1).then_inc(sem.masked, 1)

        groups(pool, group)

    def vector(dve):
        def chunk(g, side, two, qc):
            dve.wait_ge(sem.pv_done, U * g + last_of[qc] + 1)
            if later(g) or qc > 0:
                dve.wait_ge(sem.divided, QC * g + qc)
            dve.tensor_copy(sums[:], out_bank).then_inc(sem.sums_kept, 1)
            dve.wait_ge(sem.sums_kept, QC * g + qc + 1)
            dve.sem_inc(sem.shuffle_turn, 1)
            dve.stream_shuffle(below[:], sums[:], [(1 - side) * DH] * HR).then_inc(sem.chain_step, 1)
            dve.wait_ge(sem.chain_step, 2 * (QC * g + qc) + 1)
            dve.reciprocal(below[:], below[:]).then_inc(sem.chain_step, 1)
            dve.wait_ge(sem.chain_step, 2 * (QC * g + qc) + 2)
            into = upper[:] if side else heads[:, qc, :]
            dve.scalar_tensor_tensor(into, sums[:], holds[:, side:side + 1], below[:], ALU.mult, ALU.mult).then_inc(sem.divided, 1)
            if side:
                dve.wait_ge(sem.divided, QC * g + qc + 1)
                dve.tensor_tensor(heads[:, qc, :], heads[:, qc, :], upper[:], ALU.add).then_inc(sem.heads_ready, 1)

        def add(two, qc):
            batch = two // (GROUPS // 2)
            for half in range(2):
                dve.wait_ge(sem.proj_done, projected_before(two, qc, half) + 1)
                pair = x[:, bass.ds(batch * KT + qc * BT + 2 * half, 2), :].rearrange("p n d -> p (n d)")
                dve.tensor_tensor(pair, proj_bank, pair, ALU.add).then_inc(sem.proj_added, 1)
            if later(two):
                dve.wait_ge(sem.proj_added, projected_before(two, qc, 1) + 1)
                dve.sem_inc(sem.stat_turn, 1)
                bn_stats(dve, core, batch * QC + qc)

        def group(g, side, two):
            for qc in range(QC):
                chunk(g, side, two, qc)
                if side == 1 and qc < QC - 1:
                    add(two, qc)
                if side == 0 and qc == 0 and later(g):
                    add(two - 1, QC - 1)

        dve.tensor_reduce(holds[:, 0:1], core.ident[:].rearrange("p (j r) -> p j r", r=HR)[:, :, 0:DH], mybir.AxisListType.XY, ALU.add)
        dve.tensor_reduce(holds[:, 1:2], core.ident[:].rearrange("p (j r) -> p j r", r=HR)[:, :, DH:], mybir.AxisListType.XY, ALU.add
                          ).then_inc(sem.holds_ready, 1)
        dve.wait_ge(sem.holds_ready, 1)
        dve.wait_ge(lines_sem.bo_added, BLOCKS)
        groups(dve, group)
        add(ALL // 2 - 1, QC - 1)

    return Programs(sync, tensor, scalar, gpsimd, vector, (sem, q_loaded, kv_loaded)), clear, load_first




FFN_NAMES = "gate_w gate_b We1 be1 We2 be2 We3 be3 ws1 bs1 ws2 bs2 ws3 bs3"
ATTN_NAMES = "W1_q W2_q W1_k W2_k W_v b_v W_o b_o"


def macaron(nc, d, out):
    w = {n: d[f"L0_ffn_{n}"] for n in FFN_NAMES.split()}
    a = {n: d[f"L0_attn_{n}"] for n in ATTN_NAMES.split()}
    xn_rows = nc.dram_tensor("xn_rows", (BATCH * T, D), FP32, kind="Internal").ap()
    y_slots = nc.dram_tensor("y_slots", (SLOT_TILES * P, D), FP32, kind="Internal").ap()
    core = Core()
    with ExitStack() as ctx:
        x_loaded = setup(nc, core, d["L0_attn_x"], ctx)
        ffn(nc, core, w, xn_rows, y_slots, "f1", x_loaded=x_loaded)
        attention(nc, core, a, "attn", y_slots)
        ffn(nc, core, w, xn_rows, y_slots, "f2", out=out)


def kernel(**inputs):
    import numpy as np
    import concourse.bacc as bacc
    from concourse.bass_utils import run_bass_kernel_spmd

    nc = bacc.Bacc("TRN2", target_bir_lowering=False, num_devices=1)
    arrays, d = {}, {}
    for name, value in inputs.items():
        a = np.ascontiguousarray(value)
        arrays[name] = a
        d[name] = nc.dram_tensor(name, a.shape, mybir.dt.from_np(a.dtype), kind="ExternalInput").ap()
    out = nc.dram_tensor("out", (BATCH, T, D), FP32, kind="ExternalOutput").ap()
    macaron(nc, d, out)
    return run_bass_kernel_spmd(nc, [arrays], core_ids=[0]).results[0]["out"]
```
